# Optimizing a Trainium2 kernel written in Bass

```python
import numpy as np
import jax
import jax.numpy as jnp

def _softmax(x, axis=-1):
    return jax.nn.softmax(x, axis=axis)

def _gelu(x):
    return jax.nn.gelu(x, approximate=True)

def _silu(x):
    return jax.nn.silu(x)

def _sigmoid(x):
    return jax.nn.sigmoid(x)

def _layernorm(x, axis=-1, eps=1e-05):
    m = jnp.mean(x, axis=axis, keepdims=True)
    v = jnp.var(x, axis=axis, keepdims=True)
    return (x - m) / jnp.sqrt(v + eps)

def _scatter_add(tgt, idx, src, axis=0):
    return tgt.at[idx].add(src)

def _segment_sum(src, seg, n):
    return jax.ops.segment_sum(src, seg, n)
kernel_name = 'mk_decoder_preln_d1_seqx_r4_f0c4bc'

def setup_inputs(seed: int=0):
    np.random.seed(seed)
    _w = jnp.asarray

    def _rec_inputs():
        import jax
        import jax.numpy as jnp
        _rk = jax.random.key(seed)
        x = -0.000125 + 0.9999 * jax.random.normal(jax.random.fold_in(_rk, 1), (16, 256, 512), jnp.float32)
        _lenS = 256 - jax.random.randint(jax.random.fold_in(_rk, 7), (16,), 0, max(1, 256 // 4) + 1, jnp.int32)
        _lenS2 = 256 - jax.random.randint(jax.random.fold_in(_rk, 8), (16,), 0, max(1, 256 // 4) + 1, jnp.int32)
        _ctx_2048P = jax.random.normal(jax.random.fold_in(_rk, 11), (16, 16, 512), jnp.float32)
        _ctx_2048c = jax.random.dirichlet(jax.random.fold_in(_rk, 511), 0.3 * jnp.ones((16,), jnp.float32), (16, 256))
        _ctx_2048t = jnp.einsum('bsk,bkd->bsd', _ctx_2048c, _ctx_2048P)
        _ctx_2048t = _ctx_2048t * jax.lax.rsqrt(jnp.mean(jnp.square(_ctx_2048t)) + 1e-12) * 0.953939
        ctx_2048 = -1.52775e-05 + 0.999936 * (_ctx_2048t + 0.3 * jax.random.normal(jax.random.fold_in(_rk, 611), (16, 256, 512), jnp.float32))
        return (x, ctx_2048)
    x, ctx_2048 = _rec_inputs()

    def _L0_attn_setup():
        import jax, jax.numpy as jnp
        import numpy as np
        DIM = 512
        N_HEADS = 32
        N_KV_HEADS = 8
        HEAD_DIM = DIM // N_HEADS
        ROPE_BASE = 10000.0
        BATCH = 2
        SEQ = 512

        def _rope_cos_sin(seq_len, dtype=jnp.float32):
            inv_freq = 1.0 / ROPE_BASE ** (jnp.arange(0, HEAD_DIM, 2, dtype=jnp.float32) / HEAD_DIM)
            pos = jnp.arange(seq_len, dtype=jnp.float32)
            freqs = pos[:, None] * inv_freq[None, :]
            return (jnp.cos(freqs).astype(dtype), jnp.sin(freqs).astype(dtype))

        def _apply_rope(x, cos, sin):
            cos = cos[None, None, :, :]
            sin = sin[None, None, :, :]
            x_even = x[..., ::2]
            x_odd = x[..., 1::2]
            rot_even = x_even * cos - x_odd * sin
            rot_odd = x_even * sin + x_odd * cos
            out = jnp.stack((rot_even, rot_odd), axis=-1)
            return out.reshape(x.shape)
        key = jax.random.key(seed)
        ks = jax.random.split(key, 5)
        s = 0.02
        return {'x': jax.random.normal(ks[0], (BATCH, SEQ, DIM), dtype=jnp.float32), 'wq': jax.random.normal(ks[1], (DIM, N_HEADS * HEAD_DIM), dtype=jnp.float32) * s, 'wk': jax.random.normal(ks[2], (DIM, N_KV_HEADS * HEAD_DIM), dtype=jnp.float32) * s, 'wv': jax.random.normal(ks[3], (DIM, N_KV_HEADS * HEAD_DIM), dtype=jnp.float32) * s, 'wo': jax.random.normal(ks[4], (DIM, DIM), dtype=jnp.float32) * s}
    _L0_attn_all = _L0_attn_setup()
    _L0_attn_in = {k: v for k, v in _L0_attn_all.items() if k in ('wq', 'wk', 'wv', 'wo')}
    del _L0_attn_all

    def _L0_xattn_setup():
        import jax, jax.numpy as jnp
        import numpy as np
        B, DIM1, DIM2, LATENT, T = (16, 256, 256, 128, 512)
        LN_EPS = 1e-05
        key = jax.random.key(seed)
        ks = jax.random.split(key, 8)

        def xavier(k, shape):
            fan_out, fan_in = shape
            std = float(np.sqrt(2.0 / (fan_in + fan_out)))
            return jax.random.normal(k, shape, dtype=jnp.float32) * std
        return {'input1': jax.random.normal(ks[0], (B, DIM1, T), dtype=jnp.float32), 'input2': jax.random.normal(ks[1], (B, DIM2, T), dtype=jnp.float32), 'theta_w': xavier(ks[2], (LATENT, DIM2)), 'theta_b': jnp.zeros((LATENT,), jnp.float32), 'phi_w': xavier(ks[3], (LATENT, DIM1)), 'phi_b': jnp.zeros((LATENT,), jnp.float32), 'g_w': xavier(ks[4], (LATENT, DIM1)), 'g_b': jnp.zeros((LATENT,), jnp.float32), 'ln_gamma': jnp.ones((LATENT, T), jnp.float32), 'ln_beta': jnp.zeros((LATENT, T), jnp.float32), 'out_w': xavier(ks[5], (DIM2, LATENT)), 'out_b': jnp.zeros((DIM2,), jnp.float32)}
    _L0_xattn_all = _L0_xattn_setup()
    _L0_xattn_in = {k: v for k, v in _L0_xattn_all.items() if k in ('theta_w', 'theta_b', 'phi_w', 'phi_b', 'g_w', 'g_b', 'ln_gamma', 'ln_beta', 'out_w', 'out_b')}
    del _L0_xattn_all

    def _L0_ffn_setup():
        import jax, jax.numpy as jnp
        import numpy as np
        import math
        D_MODEL = 512
        D_FF = 2048
        NUM_EXPERTS = 8
        TOP_K = 2
        CAPACITY_FACTOR = 1.25
        BATCH, SEQ = (4, 512)

        def _moe_forward(x, Wg, w1, w2):
            B, T, d = x.shape
            S = B * T
            E, K = (NUM_EXPERTS, TOP_K)
            C = math.ceil(CAPACITY_FACTOR * S * K / E)
            xr = x.reshape(S, d)
            probs = jax.nn.softmax(xr @ Wg, axis=-1)
            gate_vals, expert_idx = jax.lax.top_k(probs, K)
            flat_e = expert_idx.reshape(-1)
            oh = jax.nn.one_hot(flat_e, E, dtype=jnp.int32)
            pos = jnp.sum((jnp.cumsum(oh, axis=0) - 1) * oh, axis=1)
            kept = pos < C
            i = jnp.arange(S * K)
            slot = i % K * S + i // K
            sentinel = S * K
            pos_w = jnp.where(kept, pos, C)
            dispatch_mask = jnp.full((E, C), sentinel, dtype=jnp.int32)
            dispatch_mask = dispatch_mask.at[flat_e, pos_w].set(slot.astype(jnp.int32), mode='drop')
            combine_weights = (gate_vals * kept.reshape(S, K)).T
            dispatched = xr[dispatch_mask.reshape(-1) % S].reshape(E, C, d)
            h = jax.nn.relu(jnp.einsum('ecd,edf->ecf', dispatched, w1))
            expert_out = jnp.einsum('ecf,efd->ecd', h, w2)
            rerouted = jnp.zeros((S * K + 1, d), dtype=expert_out.dtype)
            rerouted = rerouted.at[dispatch_mask.reshape(-1)].set(expert_out.reshape(-1, d))
            rerouted = rerouted[:-1].reshape(K, S, d)
            out = jnp.einsum('ks,ksm->sm', combine_weights, rerouted)
            return out.reshape(B, T, d)
        key = jax.random.key(seed)
        k1, k2, k3, k4 = jax.random.split(key, 4)
        x = jax.random.normal(k1, (BATCH, SEQ, D_MODEL), dtype=jnp.float32)
        Wg = jax.random.normal(k2, (D_MODEL, NUM_EXPERTS), dtype=jnp.float32) * 0.02
        w1 = jax.random.normal(k3, (NUM_EXPERTS, D_MODEL, D_FF), dtype=jnp.float32) * 0.02
        w2 = jax.random.normal(k4, (NUM_EXPERTS, D_FF, D_MODEL), dtype=jnp.float32) * 0.02
        return {'x': x, 'Wg': Wg, 'w1': w1, 'w2': w2}
    _L0_ffn_all = _L0_ffn_setup()
    _L0_ffn_in = {k: v for k, v in _L0_ffn_all.items() if k in ('Wg', 'w1', 'w2')}
    del _L0_ffn_all
    return {'x': x, 'ctx_2048': ctx_2048, 'L0_attn_wq': _L0_attn_in['wq'], 'L0_attn_wk': _L0_attn_in['wk'], 'L0_attn_wv': _L0_attn_in['wv'], 'L0_attn_wo': _L0_attn_in['wo'], 'L0_xattn_theta_w': _L0_xattn_in['theta_w'], 'L0_xattn_theta_b': _L0_xattn_in['theta_b'], 'L0_xattn_phi_w': _L0_xattn_in['phi_w'], 'L0_xattn_phi_b': _L0_xattn_in['phi_b'], 'L0_xattn_g_w': _L0_xattn_in['g_w'], 'L0_xattn_g_b': _L0_xattn_in['g_b'], 'L0_xattn_ln_gamma': _L0_xattn_in['ln_gamma'], 'L0_xattn_ln_beta': _L0_xattn_in['ln_beta'], 'L0_xattn_out_w': _L0_xattn_in['out_w'], 'L0_xattn_out_b': _L0_xattn_in['out_b'], 'L0_ffn_Wg': _L0_ffn_in['Wg'], 'L0_ffn_w1': _L0_ffn_in['w1'], 'L0_ffn_w2': _L0_ffn_in['w2']}

def reference(x, ctx_2048, L0_attn_wq, L0_attn_wk, L0_attn_wv, L0_attn_wo, L0_xattn_theta_w, L0_xattn_theta_b, L0_xattn_phi_w, L0_xattn_phi_b, L0_xattn_g_w, L0_xattn_g_b, L0_xattn_ln_gamma, L0_xattn_ln_beta, L0_xattn_out_w, L0_xattn_out_b, L0_ffn_Wg, L0_ffn_w1, L0_ffn_w2):
    import jax
    import jax.numpy as jnp

    def _L0_attn_ref(x, wq, wk, wv, wo):
        import jax, jax.numpy as jnp
        import numpy as np
        DIM = 512
        N_HEADS = 32
        N_KV_HEADS = 8
        HEAD_DIM = DIM // N_HEADS
        ROPE_BASE = 10000.0
        BATCH = 2
        SEQ = 512

        def _rope_cos_sin(seq_len, dtype=jnp.float32):
            inv_freq = 1.0 / ROPE_BASE ** (jnp.arange(0, HEAD_DIM, 2, dtype=jnp.float32) / HEAD_DIM)
            pos = jnp.arange(seq_len, dtype=jnp.float32)
            freqs = pos[:, None] * inv_freq[None, :]
            return (jnp.cos(freqs).astype(dtype), jnp.sin(freqs).astype(dtype))

        def _apply_rope(x, cos, sin):
            cos = cos[None, None, :, :]
            sin = sin[None, None, :, :]
            x_even = x[..., ::2]
            x_odd = x[..., 1::2]
            rot_even = x_even * cos - x_odd * sin
            rot_odd = x_even * sin + x_odd * cos
            out = jnp.stack((rot_even, rot_odd), axis=-1)
            return out.reshape(x.shape)
        b, s, _ = x.shape
        q = (x @ wq).reshape(b, s, N_HEADS, HEAD_DIM).transpose(0, 2, 1, 3)
        k = (x @ wk).reshape(b, s, N_KV_HEADS, HEAD_DIM).transpose(0, 2, 1, 3)
        v = (x @ wv).reshape(b, s, N_KV_HEADS, HEAD_DIM).transpose(0, 2, 1, 3)
        cos, sin = _rope_cos_sin(s, x.dtype)
        q = _apply_rope(q, cos, sin)
        k = _apply_rope(k, cos, sin)
        rep = N_HEADS // N_KV_HEADS
        if rep > 1:
            k = jnp.repeat(k, rep, axis=1)
            v = jnp.repeat(v, rep, axis=1)
        scores = jnp.einsum('bhqd,bhkd->bhqk', q, k) / HEAD_DIM ** 0.5
        causal = jnp.tril(jnp.ones((s, s), dtype=bool))
        scores = jnp.where(causal[None, None], scores, -jnp.inf)
        probs = jax.nn.softmax(scores, axis=-1)
        out = jnp.einsum('bhqk,bhkd->bhqd', probs, v)
        out = out.transpose(0, 2, 1, 3).reshape(b, s, DIM)
        return out @ wo

    def _L0_xattn_ref(input1, input2, theta_w, theta_b, phi_w, phi_b, g_w, g_b, ln_gamma, ln_beta, out_w, out_b):
        import jax, jax.numpy as jnp
        import numpy as np
        B, DIM1, DIM2, LATENT, T = (16, 256, 256, 128, 512)
        LN_EPS = 1e-05
        theta_x = jnp.einsum('ld,bdt->btl', theta_w, input2) + theta_b
        phi_x = jnp.einsum('ld,bdt->blt', phi_w, input1) + phi_b[:, None]
        scores = jnp.einsum('btl,bls->bts', theta_x, phi_x)
        p = jax.nn.softmax(scores, axis=-1)
        g_x = jnp.einsum('ld,bdt->btl', g_w, input1) + g_b
        t_x = jnp.einsum('bts,bsl->blt', p, g_x)
        mu = jnp.mean(t_x, axis=(1, 2), keepdims=True)
        var = jnp.var(t_x, axis=(1, 2), keepdims=True)
        h = (t_x - mu) * jax.lax.rsqrt(var + LN_EPS) * ln_gamma + ln_beta
        h = jax.nn.relu(h)
        w_t = jnp.einsum('ol,blt->bot', out_w, h) + out_b[None, :, None]
        return w_t + input2

    def _L0_ffn_ref(x, Wg, w1, w2):
        import jax, jax.numpy as jnp
        import numpy as np
        import math
        D_MODEL = 512
        D_FF = 2048
        NUM_EXPERTS = 8
        TOP_K = 2
        CAPACITY_FACTOR = 1.25
        BATCH, SEQ = (4, 512)

        def _moe_forward(x, Wg, w1, w2):
            B, T, d = x.shape
            S = B * T
            E, K = (NUM_EXPERTS, TOP_K)
            C = math.ceil(CAPACITY_FACTOR * S * K / E)
            xr = x.reshape(S, d)
            probs = jax.nn.softmax(xr @ Wg, axis=-1)
            gate_vals, expert_idx = jax.lax.top_k(probs, K)
            flat_e = expert_idx.reshape(-1)
            oh = jax.nn.one_hot(flat_e, E, dtype=jnp.int32)
            pos = jnp.sum((jnp.cumsum(oh, axis=0) - 1) * oh, axis=1)
            kept = pos < C
            i = jnp.arange(S * K)
            slot = i % K * S + i // K
            sentinel = S * K
            pos_w = jnp.where(kept, pos, C)
            dispatch_mask = jnp.full((E, C), sentinel, dtype=jnp.int32)
            dispatch_mask = dispatch_mask.at[flat_e, pos_w].set(slot.astype(jnp.int32), mode='drop')
            combine_weights = (gate_vals * kept.reshape(S, K)).T
            dispatched = xr[dispatch_mask.reshape(-1) % S].reshape(E, C, d)
            h = jax.nn.relu(jnp.einsum('ecd,edf->ecf', dispatched, w1))
            expert_out = jnp.einsum('ecf,efd->ecd', h, w2)
            rerouted = jnp.zeros((S * K + 1, d), dtype=expert_out.dtype)
            rerouted = rerouted.at[dispatch_mask.reshape(-1)].set(expert_out.reshape(-1, d))
            rerouted = rerouted[:-1].reshape(K, S, d)
            out = jnp.einsum('ks,ksm->sm', combine_weights, rerouted)
            return out.reshape(B, T, d)
        return _moe_forward(x, Wg, w1, w2)
    x = x + _L0_attn_ref(_layernorm(x, axis=-1), L0_attn_wq, L0_attn_wk, L0_attn_wv, L0_attn_wo)
    x = x + _L0_xattn_ref(_layernorm(x, axis=-1), ctx_2048, L0_xattn_theta_w, L0_xattn_theta_b, L0_xattn_phi_w, L0_xattn_phi_b, L0_xattn_g_w, L0_xattn_g_b, L0_xattn_ln_gamma, L0_xattn_ln_beta, L0_xattn_out_w, L0_xattn_out_b)
    x = x + _L0_ffn_ref(_layernorm(x, axis=-1), L0_ffn_Wg, L0_ffn_w1, L0_ffn_w2)
    return x

_drawn_inputs = setup_inputs


def setup_inputs(seed=0):
    import zlib

    import numpy as np

    out = dict(_drawn_inputs(seed))
    spreads = {'L0_xattn_theta_b': (0.0, 0.1),
     'L0_xattn_phi_b': (0.0, 0.8),
     'L0_xattn_g_b': (0.0, 0.1),
     'L0_xattn_ln_gamma': (1.0, 0.2),
     'L0_xattn_ln_beta': (0.0, 0.1),
     'L0_xattn_out_b': (0.0, 0.1)}
    factors = {'L0_attn_wq': 5.563, 'L0_attn_wk': 5.5}
    for name, (base, spread) in spreads.items():
        noise = np.random.default_rng([zlib.crc32(name.encode()), seed]).standard_normal(out[name].shape)
        drawn = base * np.exp(spread * noise) if base else spread * noise
        out[name] = jnp.asarray(drawn.astype(out[name].dtype))
    for name, factor in factors.items():
        out[name] = (out[name] * factor).astype(out[name].dtype)
    return out
```

```python
from contextlib import ExitStack

import concourse.bass as bass
from concourse import mybir

F32 = mybir.dt.float32
F32R = mybir.dt.float32r
BF16 = mybir.dt.bfloat16
I32 = mybir.dt.int32
ALU = mybir.AluOpType
ACT = mybir.ActivationFunctionType
AX = mybir.AxisListType

P = 128
B, S, D = 16, 256, 512
NT = B * S // P
TPB = S // P
KD = D // P
H, G, HD = 32, 8, 16
REP = H // G
KVW = G * HD
QKV = D + 2 * KVW
VW = HD + 2
LAT = 128
E, FF, TOPK = 8, 2048, 2
CAP = (5 * B * S * TOPK) // (4 * E)
NF = FF // P
SLOTS = E * CAP
BLK = CAP // 2
BT = BLK // P
ST = SLOTS // P
EPS = 1e-5
MASKED = -1e30
CH = 4


def wait(eng, sem, value):
    if not (isinstance(value, int) and value <= 0):
        eng.wait_ge(sem, value)


def wait_apart(eng, sem, value, passed):
    eng.wait_ge(sem, value).then_inc(passed, 1)


def f32(ap):
    return ap.bitcast(F32)


class Scope:

    def __init__(self, nc):
        self.nc = nc
        self.ctx = ExitStack()
        self.sems = []

    def __enter__(self):
        self.ctx.__enter__()
        return self

    def __exit__(self, *a):
        self.ctx.__exit__(*a)
        if self.sems:
            self.nc.clear_and_free_semaphores(self.sems)
            self.nc.all_engine_barrier()

    def sb(self, name, shape, dt=F32):
        return self.ctx.enter_context(self.nc.sbuf_tensor(name, shape, dt))

    def ps(self, name, shape, dt=F32):
        return self.ctx.enter_context(self.nc.psum_tensor(name, shape, dt))

    def sem(self, name):
        self.sems.append(self.nc.alloc_semaphore(name))
        return self.sems[-1]


def split_passes(eng, out, lhs, rhs, first=True, last=True, **kw):
    eng.matmul(out, lhs[0], rhs[0], start=first, stop=False, **kw)
    eng.matmul(out, lhs[0], rhs[1], start=False, stop=False, **kw)
    return eng.matmul(out, lhs[1], rhs[0], start=False, stop=last, **kw)


def stage_constants(nc, io, t):
    with Scope(nc) as s:
        raw = {n: s.sb(f"raw_{n}", list(t[n][0].shape)) for n in t["split"]}
        ident_set, mask_set = s.sem("ident_zeroed"), s.sem("mask_zeroed")
        raw_loaded = s.sem("raw_weights_loaded")
        tables_loaded = s.sem("tables_loaded")
        hi_done, lo_done = s.sem("weights_hi_done"), s.sem("weights_lo_done")
        block = s.ctx.enter_context(nc.Block())
        names = list(t["split"])

        @block.sync
        def _(sp):
            for n in names:
                sp.dma_start(raw[n][:], io[n]).then_inc(raw_loaded, 16)
            sp.dma_start(t["cos"][:], io["cos"]).then_inc(tables_loaded, 16)
            sp.dma_start(t["sin"][:], io["sin"]).then_inc(tables_loaded, 16)
            for n in ("theta_b", "phi_b", "g_b"):
                sp.dma_start(t[n][:], io[n].rearrange("(p o) -> p o", o=1)).then_inc(tables_loaded, 16)
            sp.dma_start(t["out_b"][:], io["out_b"]).then_inc(tables_loaded, 16)
            sp.dma_start(t["gamma"][:], io["gamma"]).then_inc(tables_loaded, 16)
            sp.dma_start(t["beta"][:], io["beta"]).then_inc(tables_loaded, 16)
            sp.wait_ge(tables_loaded, 16 * 8)

        @block.gpsimd
        def _(pool):
            pool.memset(t["ident"][:], 0.0).then_inc(ident_set, 1)
            pool.memset(t["identb"][:], 0.0).then_inc(ident_set, 1)
            pool.memset(t["mask"][:], 0.0).then_inc(mask_set, 1)
            pool.memset(t["ones"][:], 1.0)
            pool.memset(t["upper"][:], 1.0).then_inc(mask_set, 1)
            pool.memset(t["avg"][:], 1.0 / P)
            pool.memset(t["half"][:], -0.5)
            pool.memset(t["eps"][:], EPS)
            pool.wait_ge(ident_set, 2)
            for m in (t["ident"], t["identb"]):
                pool.affine_select(out=m[:], in_=m[:], compare_op=ALU.not_equal, fill=1.0, base=0,
                                   pattern=[[-1, P]], channel_multiplier=1)
            pool.wait_ge(mask_set, 2)
            pool.affine_select(out=t["mask"][:], in_=t["mask"][:], compare_op=ALU.is_ge, fill=MASKED, base=0,
                               pattern=[[-1, P]], channel_multiplier=1)
            pool.affine_select(out=t["upper"][:], in_=t["upper"][:], compare_op=ALU.is_gt, fill=0.0, base=0,
                               pattern=[[1, P]], channel_multiplier=-1)

        @block.scalar
        def _(act):
            act.wait_ge(raw_loaded, 16 * len(names))
            for n in names:
                act.activation(t[n][0][:], raw[n][:], ACT.Copy).then_inc(hi_done, 1)

        @block.vector
        def _(dve):
            dve.wait_ge(raw_loaded, 16 * len(names))
            for i, n in enumerate(names):
                dve.wait_ge(hi_done, i + 1)
                dve.tensor_tensor(t[n][1][:], raw[n][:], f32(t[n][0][:]), ALU.subtract).then_inc(lo_done, 1)


def stage_qkv(nc, io, t):
    with Scope(nc) as s:
        x = s.sb("qkv_x", [P, CH, D])
        xn = s.sb("qkv_xn", [P, CH, D])
        xh = [s.sb(f"qkv_xh{c}", [P, KD, P], F32R) for c in range(CH)]
        xl = [s.sb(f"qkv_xl{c}", [P, KD, P], F32R) for c in range(CH)]
        st6 = s.sb("qkv_st6", [P, CH, 6])
        mv = s.sb("qkv_mv", [P, CH, 2])
        ve = s.sb("qkv_ve", [P, CH])
        rstd = s.sb("qkv_rstd", [P, CH])
        rc = s.sb("qkv_rc", [P, 2, D + KVW])
        rs = s.sb("qkv_rs", [P, 2, D + KVW])
        xT = [s.ps(f"qkv_xT{c}", [P, D]) for c in range(2)]
        proj = [s.ps(f"qkv_proj{c}", [P, 1024]) for c in range(2)]
        x_loaded = [s.sem(f"x_loaded{c}") for c in range(CH)]
        stats, moments, eps_added, rstd_ready = (s.sem(n) for n in ("stats", "moments", "eps_added", "rstd_ready"))
        xn_ready, xT_ready, xh_ready, xl_ready = (s.sem(n) for n in ("xn_ready", "xT_ready", "xh_ready", "xl_ready"))
        proj_ready, rot_cos, rot_sin, rot_done, v_done = (
            s.sem(n) for n in ("proj_ready", "rot_cos", "rot_sin", "rot_done", "v_done"))
        block = s.ctx.enter_context(nc.Block())
        steps = NT // CH
        passed_pool, passed_dve = s.sem("qkv_passed_pool"), s.sem("qkv_passed_dve")

        @block.sync
        def _(sp):
            with sp.Fori(0, steps) as j:
                for c in range(CH):
                    sp.wait_ge(xn_ready, CH * j)
                    sp.dma_start(x[:, c, :], io["x_tiles"][CH * j + c]).then_inc(x_loaded[c], 16)

        @block.gpsimd
        def _(pool):
            with pool.Fori(0, steps) as j:
                for c in range(CH):
                    n = CH * j + c
                    pool.wait_ge(moments, n + 1)
                    pool.tensor_tensor(ve[:, c:c + 1], mv[:, c, 1:2], t["eps"][:], ALU.add).then_inc(eps_added, 1)
                    pool.wait_ge(eps_added, n + 1)
                    pool.tensor_tensor(rstd[:, c:c + 1], ve[:, c:c + 1], t["half"][:, 0:1],
                                       ALU.pow).then_inc(rstd_ready, 1)
                for c in range(CH):
                    n = CH * j + c
                    pool.wait_ge(rot_sin, 2 * n + 2)
                    wait_apart(pool, rot_cos, n + 1, passed_pool)
                    pool.tensor_tensor(t["act"][:, n, :], rc[:, c % 2, 0:D], rs[:, c % 2, 0:D],
                                       ALU.add).then_inc(rot_done, 1)
                    pool.tensor_tensor(t["k"][:, n, :], rc[:, c % 2, D:], rs[:, c % 2, D:],
                                       ALU.add).then_inc(rot_done, 1)

        @block.scalar
        def _(act):
            with act.Fori(0, steps) as j:
                for c in range(CH):
                    n = CH * j + c
                    act.wait_ge(xT_ready, n + 1)
                    act.wait_ge(proj_ready, CH * j)
                    act.activation(xh[c][:].rearrange("p k n -> p (k n)"), xT[c % 2][:], ACT.Copy).then_inc(xh_ready, 1)
                for c in range(CH):
                    n = CH * j + c
                    act.wait_ge(rot_sin, 2 * n + 2)
                    act.activation(t["v"][:, n, :, 0:HD],
                                   proj[c % 2][:, D + KVW:QKV].rearrange("p (g d) -> p g d", g=G),
                                   ACT.Copy).then_inc(v_done, 1)

        @block.vector
        def _(dve):
            dve.memset(t["v"][:], 1.0).then_inc(v_done, 1)
            with dve.Fori(0, steps) as j:
                for c in range(CH):
                    dve.wait_ge(x_loaded[c], 16 * j + 16)
                    dve.bn_stats(st6[:, c, :], x[:, c, :]).then_inc(stats, 1)
                for c in range(CH):
                    n = CH * j + c
                    wait_apart(dve, stats, n + 1, passed_dve)
                    dve.bn_aggr(mv[:, c, :], st6[:, c, :]).then_inc(moments, 1)
                for c in range(CH):
                    n = CH * j + c
                    dve.wait_ge(rstd_ready, n + 1)
                    dve.wait_ge(xT_ready, CH * j)
                    dve.tensor_scalar(xn[:, c, :], x[:, c, :], mv[:, c, 0:1], rstd[:, c:c + 1],
                                      ALU.subtract, ALU.mult).then_inc(xn_ready, 1)
                for c in range(CH):
                    n = CH * j + c
                    dve.wait_ge(xh_ready, n + 1)
                    dve.tensor_tensor(xl[c][:].rearrange("p k n -> p (k n)"), xT[c % 2][:],
                                      f32(xh[c][:]).rearrange("p k n -> p (k n)"), ALU.subtract).then_inc(xl_ready, 1)
                for c in range(CH):
                    n = CH * j + c
                    qk = proj[c % 2][:, 0:D + KVW].rearrange("p (h d) -> p h d", d=HD)
                    cs = rc[:, c % 2, :].rearrange("p (h d) -> p h d", d=HD)
                    sn = rs[:, c % 2, :].rearrange("p (h d) -> p h d", d=HD)
                    cos = t["cos"][:, c % TPB, :].unsqueeze(1).to_broadcast([P, H + G, HD])
                    dve.wait_ge(proj_ready, n + 1)
                    if c >= 2:
                        dve.wait_ge(rot_done, 2 * (n - 1))
                    dve.tensor_tensor(cs, qk, cos, ALU.mult).then_inc(rot_cos, 1)
                    for half in range(2):
                        a, b = half * HD // 2, (1 - half) * HD // 2
                        sin = t["sin"][:, c % TPB, a:a + HD // 2].unsqueeze(1).to_broadcast([P, H + G, HD // 2])
                        dve.tensor_tensor(sn[:, :, a:a + HD // 2], qk[:, :, b:b + HD // 2], sin,
                                          ALU.mult).then_inc(rot_sin, 1)

        @block.tensor
        def _(pe):
            with pe.Fori(0, steps) as j:
                for c in range(CH):
                    n = CH * j + c
                    pe.wait_ge(xn_ready, n + 1)
                    if c >= 2:
                        pe.wait_ge(xl_ready, n - 1)
                    for k in range(KD):
                        m = pe.transpose(xT[c % 2][:, k * P:(k + 1) * P], xn[:, c, k * P:(k + 1) * P], t["ident"][:])
                    m.then_inc(xT_ready, 1)
                for c in range(CH):
                    n = CH * j + c
                    pe.wait_ge(xl_ready, n + 1)
                    if c >= 2:
                        pe.wait_ge(v_done, n)
                    else:
                        pe.wait_ge(v_done, CH * j + 1)
                    for half in range(2):
                        a, b = half * 512, min(QKV, half * 512 + 512)
                        for k in range(KD):
                            m = split_passes(pe, proj[c % 2][:, a:b], (xh[c][:, k, :], xl[c][:, k, :]),
                                             [w[:, k, a:b] for w in t["wqkv"]], k == 0, k == KD - 1)
                    m.then_inc(proj_ready, 1)


def stage_attention(nc, t):
    with Scope(nc) as s:
        R = 2
        stk = [s.sb(f"at_stk{r}", [P, TPB, 3 * P], F32R) for r in range(R)]
        qT = [s.sb(f"at_qT{r}", [P, 2, S], F32R) for r in range(R)]
        kz = [s.sb(f"at_kz{r}", [P, 2, S], F32R) for r in range(R)]
        prob = [s.sb(f"at_prob{r}", [P, 3, 512]) for r in range(R)]
        pT = [s.sb(f"at_pT{r}", [P, 3, 512]) for r in range(R)]
        mx = s.sb("at_mx", [P, R, 8])
        nb = s.sb("at_nb", [P, R, 8])
        rinv = s.sb("at_rinv", [P, R, 8])
        sc = [s.ps(f"at_scores{a}", [P, 512]) for a in range(3)]
        tp = [s.ps(f"at_tp{r}", [P, 512]) for r in range(2)]
        ob = s.ps("at_out", [P, 512])
        sk = s.ps("at_stkT", [P, 2, 512])
        names = ("q_hi", "stack_ready", "stackT_ready", "kz_zeroed", "qT_ready", "kz_ready", "scores_ready",
                 "max_ready", "bias_ready", "probs_ready", "probsT_ready", "pT_a", "pT_b", "out_ready", "rinv_ready",
                 "attn_done")
        sm = {n: s.sem("at_" + n) for n in names}
        passed_pool = s.sem("at_passed_pool")
        block = s.ctx.enter_context(nc.Block())
        o4 = ob[:, 0:TPB * REP * VW].rearrange("p (q h d) -> p q h d", q=TPB, h=REP)

        @block.gpsimd
        def _(pool):
            with pool.Fori(0, B) as b:
                for g in range(G):
                    n = G * b + g
                    r = g % R
                    if g >= R:
                        wait_apart(pool, sm["stackT_ready"], n - 1, passed_pool)
                    else:
                        wait_apart(pool, sm["stackT_ready"], G * b, passed_pool)
                    for u in range(TPB):
                        q = t["act"][:, TPB * b + u, g * REP * HD:(g + 1) * REP * HD].rearrange("p (h d) -> p h d", d=HD)
                        k = t["k"][:, TPB * b + u, g * HD:(g + 1) * HD]
                        qs = stk[r][:, u, 0:2 * P].rearrange("p (h c l d) -> p h c l d", h=REP, c=2, l=2)
                        ks = stk[r][:, u, 2 * P:3 * P].rearrange("p (m l c d) -> p m l c d", m=2, l=2, c=2)
                        q4 = q.unsqueeze(2).to_broadcast([P, REP, 2, HD])
                        k4 = k.unsqueeze(1).unsqueeze(1).to_broadcast([P, 2, 2, HD])
                        pool.tensor_copy(qs[:, :, :, 0, :], q4).then_inc(sm["q_hi"], 1)
                        pool.tensor_copy(ks[:, :, 0, :, :], k4).then_inc(sm["q_hi"], 1)
                        wait_apart(pool, sm["q_hi"], 4 * n + 2 * u + 1, passed_pool)
                        pool.tensor_tensor(qs[:, :, :, 1, :], q4, f32(qs[:, :, :, 0, :]),
                                           ALU.subtract).then_inc(sm["stack_ready"], 1)
                        wait_apart(pool, sm["q_hi"], 4 * n + 2 * u + 2, passed_pool)
                        pool.tensor_tensor(ks[:, :, 1, :, :], k4, f32(ks[:, :, 0, :, :]),
                                           ALU.subtract).then_inc(sm["stack_ready"], 1)

        def slots(eng, slot, first):
            first()
            slot(0, 0, True, True, False)
            with eng.Fori(0, B - 1) as b:
                for k in range(1, G + 1):
                    slot(b + k // G, k % G, True, True, True)
            for k in range(1, G + 1):
                slot(B - 1, k, k < G - 1, k < G, True)

        @block.scalar
        def _(act):
            def operand(n, r):
                act.wait_ge(sm["stackT_ready"], n + 1)
                act.activation(qT[r][:].rearrange("p m (u n) -> p u m n", u=TPB),
                               sk[:, :, 0:2 * P].rearrange("p u (m n) -> p u m n", m=2), ACT.Copy)\
                    .then_inc(sm["qT_ready"], 1)

            def exps(n, r, a):
                act.wait_ge(sm["bias_ready"], 3 * n + a + 1)
                w = P if a == 0 else S
                for h in range(512 // w):
                    hb = h if a == 0 else REP + 2 * (a - 1) + h
                    m = act.activation(prob[r][:, a, h * w:(h + 1) * w], sc[a][:, h * w:(h + 1) * w], ACT.Exp,
                                       bias=nb[:, r, hb:hb + 1], scale=HD ** -0.5)
                m.then_inc(sm["probs_ready"], 1)

            def turn(n, r):
                act.wait_ge(sm["probsT_ready"], 3 * n + 2)
                act.activation(pT[r][:, 1, :], tp[1][:], ACT.Copy).then_inc(sm["pT_b"], 1)

            def slot(b, g, has_next, has_this, has_prev):
                n = G * b + g
                if has_this:
                    exps(n, g % R, 0)
                if has_prev:
                    turn(n - 1, (g - 1) % R)
                if has_this:
                    exps(n, g % R, 1)
                    exps(n, g % R, 2)
                if has_next:
                    operand(n + 1, (g + 1) % R)

            slots(act, slot, lambda: operand(0, 0))

        @block.vector
        def _(dve):
            def operand(n, r):
                dve.wait_ge(sm["qT_ready"], n + 1)
                for m in range(2):
                    i = dve.tensor_copy(kz[r][64 * m:64 * m + 64, m, :].rearrange("p (u n) -> p u n", u=TPB),
                                        sk[64 * m:64 * m + 64, :, 2 * P:3 * P])
                i.then_inc(sm["kz_ready"], 1)

            def maxima(n, r, a):
                dve.wait_ge(sm["scores_ready"], 3 * n + a + 1)
                lo, hi = (0, REP) if a == 0 else (REP + 2 * (a - 1), REP + 2 * a)
                dve.tensor_reduce(mx[:, r, lo:hi], sc[a][:].rearrange("p (h k) -> p h k", h=hi - lo), AX.X, ALU.max)\
                    .then_inc(sm["max_ready"], 1)
                dve.wait_ge(sm["max_ready"], 3 * n + a + 1)
                dve.tensor_scalar(nb[:, r, lo:hi], mx[:, r, lo:hi], -HD ** -0.5, None, ALU.mult)\
                    .then_inc(sm["bias_ready"], 1)

            def turn(n, r, c):
                dve.wait_ge(sm["probsT_ready"], 3 * n + c + 1)
                dve.tensor_copy(pT[r][:, c, :], tp[0][:]).then_inc(sm["pT_a"], 1)

            def finish(n, r, b, g):
                dve.wait_ge(sm["out_ready"], n + 1)
                dve.reciprocal(rinv[:, r, :].rearrange("p (q h) -> p q h", q=TPB), o4[:, :, :, HD])\
                    .then_inc(sm["rinv_ready"], 1)
                dve.wait_ge(sm["rinv_ready"], n + 1)
                w = rinv[:, r, :].rearrange("p (q h) -> p q h", q=TPB).unsqueeze(3).to_broadcast([P, TPB, REP, HD])
                i = dve.tensor_tensor(
                    t["act"][:, bass.ds(TPB * b, TPB), g * REP * HD:(g + 1) * REP * HD].rearrange("p u (h d) -> p u h d", d=HD),
                    o4[:, :, :, 0:HD], w, ALU.mult)
                i.then_inc(sm["attn_done"], 1)

            def slot(b, g, has_next, has_this, has_prev):
                n = G * b + g
                r, q = g % R, (g - 1) % R
                if has_this:
                    maxima(n, r, 0)
                if has_prev:
                    turn(n - 1, q, 0)
                if has_this:
                    maxima(n, r, 1)
                    maxima(n, r, 2)
                if has_prev:
                    turn(n - 1, q, 2)
                if has_next:
                    operand(n + 1, (g + 1) % R)
                if has_prev:
                    pb, pg = (b, g - 1) if g else (b - 1, G - 1)
                    finish(n - 1, q, pb, pg)

            def first():
                for r in range(R):
                    i = dve.memset(f32(kz[r][:]), 0.0)
                i.then_inc(sm["kz_zeroed"], 1)
                dve.wait_ge(sm["kz_zeroed"], 1)
                operand(0, 0)

            slots(dve, slot, first)

        @block.tensor
        def _(pe):
            def operand(n, r):
                pe.wait_ge(sm["stack_ready"], 4 * n + 4)
                wait(pe, sm["kz_ready"], n)
                for u in range(TPB):
                    for a in range(3):
                        m = pe.transpose(sk[:, u, a * P:(a + 1) * P], f32(stk[r][:, u, a * P:(a + 1) * P]), t["ident"][:])
                m.then_inc(sm["stackT_ready"], 1)

            def scores(n, r, a):
                if a == 0:
                    pe.wait_ge(sm["kz_ready"], n + 1)
                    heads, width = REP, P
                else:
                    heads, width = 2, S
                wait(pe, sm["probs_ready"], 3 * n - 2 + a)
                bank = sc[a][:].rearrange("p (h k) -> p h k", h=heads)
                pe.matmul(bank[:, :, width - P:width], t["identb"][:],
                          t["mask"][:].unsqueeze(1).to_broadcast([P, heads, P]), start=True, stop=False,
                          skip_group_check=True)
                for pair in ((0, 1) if a == 0 else (a - 1,)):
                    out = sc[a][:, pair * S:(pair + 1) * S] if a == 0 else sc[a][:]
                    lhs = qT[r][:, pair, 0:P] if a == 0 else qT[r][:, pair, P:S]
                    m = pe.matmul(out.rearrange("p (z k) -> p z k", z=2), lhs, kz[r][:, :, 0:width],
                                  start=False, stop=True, skip_group_check=True)
                m.then_inc(sm["scores_ready"], 1)

            def turn(n, r, c):
                pe.wait_ge(sm["probs_ready"], 3 * n + c + 1)
                if c == 1:
                    wait(pe, sm["pT_b"], n)
                else:
                    wait(pe, sm["pT_a"], 2 * n + c // 2)
                for k in range(4):
                    m = pe.transpose(tp[c % 2][:, k * P:(k + 1) * P], prob[r][:, c, k * P:(k + 1) * P], t["ident"][:])
                m.then_inc(sm["probsT_ready"], 1)

            def values(n, r, b, g):
                pe.wait_ge(sm["pT_a"], 2 * n + 2)
                pe.wait_ge(sm["pT_b"], n + 1)
                wait(pe, sm["attn_done"], n)
                v = [t["v"][:, TPB * b + u, g, :] for u in range(TPB)]
                for h in range(REP):
                    pe.matmul(o4[:, 0, h, :], pT[r][:, 0, h * P:(h + 1) * P], v[0], start=True, stop=True)
                    for u in range(TPB):
                        k = (2 * (h % 2) + u) * P
                        m = pe.matmul(o4[:, 1, h, :], pT[r][:, 1 + h // 2, k:k + P], v[u], start=u == 0,
                                      stop=u == TPB - 1)
                m.then_inc(sm["out_ready"], 1)

            def slot(b, g, has_next, has_this, has_prev):
                n = G * b + g
                for a in range(3):
                    if has_this:
                        scores(n, g % R, a)
                    if has_prev:
                        turn(n - 1, (g - 1) % R, a)
                if has_next:
                    operand(n + 1, (g + 1) % R)
                if has_prev:
                    pb, pg = (b, g - 1) if g else (b - 1, G - 1)
                    values(n - 1, (g - 1) % R, pb, pg)

            slots(pe, slot, lambda: operand(0, 0))


def stage_out_proj(nc, io, t):
    with Scope(nc) as s:
        x = s.sb("op_x", [P, CH, D])
        at = [s.sb(f"op_at{c}", [P, D]) for c in range(CH)]
        ah = [s.sb(f"op_ah{c}", [P, KD, P], F32R) for c in range(CH)]
        al = [s.sb(f"op_al{c}", [P, KD, P], F32R) for c in range(CH)]
        st6 = s.sb("op_st6", [P, CH, 6])
        mv = s.sb("op_mv", [P, CH, 2])
        ve = s.sb("op_ve", [P, CH])
        aT = [s.ps(f"op_aT{c}", [P, D]) for c in range(CH)]
        y = [s.ps(f"op_y{c}", [P, D]) for c in range(CH)]
        x_loaded = [s.sem(f"op_x_loaded{c}") for c in range(CH)]
        names = ("copied", "turned", "hi", "lo", "y_ready", "x1_done", "stats", "moments", "eps", "rstd_ready",
                 "mean_kept", "passed_pool", "passed_dve")
        sm = {n: s.sem("op_" + n) for n in names}
        block = s.ctx.enter_context(nc.Block())
        steps = NT // CH

        @block.sync
        def _(sp):
            with sp.Fori(0, steps) as j:
                for c in range(CH):
                    sp.wait_ge(sm["x1_done"], CH * j)
                    sp.dma_start(x[:, c, :], io["x_tiles"][CH * j + c]).then_inc(x_loaded[c], 16)

        @block.gpsimd
        def _(pool):
            with pool.Fori(0, steps) as j:
                for c in range(CH):
                    n = CH * j + c
                    wait_apart(pool, sm["turned"], CH * j, sm["passed_pool"])
                    pool.tensor_copy(at[c][:], t["act"][:, n, :]).then_inc(sm["copied"], 1)
                for c in range(CH):
                    n = CH * j + c
                    pool.wait_ge(sm["moments"], n + 1)
                    pool.tensor_tensor(ve[:, c:c + 1], mv[:, c, 1:2], t["eps"][:], ALU.add).then_inc(sm["eps"], 1)
                    wait_apart(pool, sm["eps"], n + 1, sm["passed_pool"])
                    pool.tensor_tensor(t["rstd1"][:, n, :], ve[:, c:c + 1], t["half"][:],
                                       ALU.pow).then_inc(sm["rstd_ready"], 1)
                    pool.tensor_copy(t["mean1"][:, n, :], mv[:, c, 0:1]).then_inc(sm["mean_kept"], 1)

        @block.scalar
        def _(act):
            with act.Fori(0, steps) as j:
                for c in range(CH):
                    n = CH * j + c
                    act.wait_ge(sm["turned"], n + 1)
                    act.wait_ge(sm["y_ready"], CH * j)
                    act.activation(ah[c][:].rearrange("p k n -> p (k n)"), aT[c][:], ACT.Copy).then_inc(sm["hi"], 1)

        @block.vector
        def _(dve):
            with dve.Fori(0, steps) as j:
                for c in range(CH):
                    n = CH * j + c
                    dve.wait_ge(sm["hi"], n + 1)
                    dve.tensor_tensor(al[c][:].rearrange("p k n -> p (k n)"), aT[c][:],
                                      f32(ah[c][:]).rearrange("p k n -> p (k n)"), ALU.subtract).then_inc(sm["lo"], 1)
                for c in range(CH):
                    n = CH * j + c
                    dve.wait_ge(x_loaded[c], 16 * j + 16)
                    wait_apart(dve, sm["y_ready"], n + 1, sm["passed_dve"])
                    dve.tensor_tensor(t["act"][:, n, :], y[c][:], x[:, c, :], ALU.add).then_inc(sm["x1_done"], 1)
                for c in range(CH):
                    n = CH * j + c
                    wait_apart(dve, sm["x1_done"], n + 1, sm["passed_dve"])
                    dve.bn_stats(st6[:, c, :], t["act"][:, n, :]).then_inc(sm["stats"], 1)
                for c in range(CH):
                    n = CH * j + c
                    dve.wait_ge(sm["mean_kept"], CH * j)
                    wait_apart(dve, sm["stats"], n + 1, sm["passed_dve"])
                    dve.bn_aggr(mv[:, c, :], st6[:, c, :]).then_inc(sm["moments"], 1)

        @block.tensor
        def _(pe):
            with pe.Fori(0, steps) as j:
                for c in range(CH):
                    n = CH * j + c
                    pe.wait_ge(sm["copied"], n + 1)
                    pe.wait_ge(sm["lo"], CH * j)
                    for k in range(KD):
                        m = pe.transpose(aT[c][:, k * P:(k + 1) * P], at[c][:, k * P:(k + 1) * P], t["ident"][:])
                    m.then_inc(sm["turned"], 1)
                for c in range(CH):
                    n = CH * j + c
                    pe.wait_ge(sm["lo"], n + 1)
                    pe.wait_ge(sm["x1_done"], CH * j)
                    for k in range(KD):
                        m = split_passes(pe, y[c][:], (ah[c][:, k, :], al[c][:, k, :]),
                                         [w[:, k, :] for w in t["wo"]], k == 0, k == KD - 1)
                    m.then_inc(sm["y_ready"], 1)


def stage_cross(nc, io, t):
    CB = 2
    NTT = D // P
    with Scope(nc) as s:
        ctx_in = [s.sb(f"cx_ctx{c}", [P, TPB, D]) for c in range(CB)]
        xin = [s.sb(f"cx_xin{c}", [P, TPB, D]) for c in range(CB)]
        R1 = [s.sb(f"cx_r1_{c}", [P, 8, D], F32R) for c in range(CB)]
        R2 = [s.sb(f"cx_r2_{c}", [P, 6, D], F32R) for c in range(CB)]
        prob = [s.sb(f"cx_prob{c}", [P, NTT, D]) for c in range(CB)]
        bank = [[s.ps(f"cx_bank{c}_{i}", [P, 512]) for i in range(4)] for c in range(CB)]
        st6 = s.sb("cx_st6", [P, CB, TPB, 6])
        mv = s.sb("cx_mv", [P, CB, TPB, 2])
        ve = s.sb("cx_ve", [P, CB, TPB])
        rstd = s.sb("cx_rstd", [P, CB, TPB])
        mx = s.sb("cx_mx", [P, CB, NTT])
        nmx = s.sb("cx_nmx", [P, CB, NTT])
        rsum = s.sb("cx_rsum", [P, CB, NTT])
        rinv = s.sb("cx_rinv", [P, CB, NTT])
        pst = s.sb("cx_pst", [P, CB, 6])
        pmv = s.sb("cx_pmv", [P, CB, 2])
        psq = s.sb("cx_psq", [P, CB])
        gmv = s.sb("cx_gmv", [P, CB, 2])
        gsq = s.sb("cx_gsq", [P, CB])
        gve = s.sb("cx_gve", [P, CB])
        gvar = s.sb("cx_gvar", [P, CB])
        grstd = s.sb("cx_grstd", [P, CB])
        ctx_loaded = [s.sem(f"ctx_loaded{c}") for c in range(CB)]
        stored = [s.sem(f"cx_stored{c}") for c in range(CB)]
        names = ("xin", "ctx_hi", "ctx_lo", "ctx_res", "xin_hi", "xin_lo", "theta", "phi", "g", "theta_hi", "theta_lo",
                 "phi_hi", "phi_lo", "g_hi", "g_lo", "scores", "max", "neg_max", "exp", "rinv", "norm", "turned",
                 "pT_hi", "pT_lo", "tx", "tx_kept", "row_stats", "row_moments", "row_sq", "row_m2", "all_moments",
                 "gmv", "gsq", "gvar", "gve", "grstd", "centred", "scaled", "h_hi", "h_lo", "out", "x2", "stats",
                 "moments", "eps", "rstd", "xn3", "x3T", "x3_hi", "x3_lo", "logits", "logits_kept",
                 "passed_act", "passed_dve", "passed_pool")
        sm = {n: s.sem("cx_" + n) for n in names}
        block = s.ctx.enter_context(nc.Block())
        steps = B // CB

        def flat(ap):
            return ap.rearrange("p a n -> p (a n)")

        @block.sync
        def _(sp):
            with sp.Fori(0, steps) as j:
                for c in range(CB):
                    n = CB * j + c
                    sp.wait_ge(sm["x2"], TPB * CB * j)
                    sp.dma_start(ctx_in[c][:], io["ctx_tiles"][n]).then_inc(ctx_loaded[c], 16)
                for c in range(CB):
                    n = CB * j + c
                    sp.wait_ge(sm["x2"], TPB * (n + 1))
                    sp.dma_start(io["x2_tiles"][n], xin[c][:]).then_inc(stored[c], 16)
                for c in range(CB):
                    n = CB * j + c
                    sp.wait_ge(sm["xn3"], TPB * (n + 1))
                    sp.dma_start(io["xn3_tiles"][n], prob[c][:, 0:TPB, :]).then_inc(stored[c], 16)
            for c in range(CB):
                sp.wait_ge(stored[c], 32 * steps)

        @block.gpsimd
        def _(pool):
            with pool.Fori(0, steps) as j:
                for c in range(CB):
                    n = CB * j + c
                    pool.wait_ge(ctx_loaded[c], 16 * j + 16)
                    wait_apart(pool, sm["tx"], CB * j, sm["passed_pool"])
                    pool.tensor_copy(R1[c][:, 0:2, :], ctx_in[c][:]).then_inc(sm["ctx_hi"], 1)
                for c in range(CB):
                    n = CB * j + c
                    wait_apart(pool, sm["ctx_hi"], n + 1, sm["passed_pool"])
                    pool.tensor_tensor(R1[c][:, 2:4, :], ctx_in[c][:], f32(R1[c][:, 0:2, :]),
                                       ALU.subtract).then_inc(sm["ctx_lo"], 1)
                for c in range(CB):
                    n = CB * j + c
                    wait_apart(pool, sm["ctx_lo"], n + 1, sm["passed_pool"])
                    pool.tensor_tensor(ctx_in[c][:], ctx_in[c][:], t["act"][:, bass.ds(TPB * n, TPB), :],
                                       ALU.add).then_inc(sm["ctx_res"], 1)
                for c in range(CB):
                    n = CB * j + c
                    pool.wait_ge(sm["gvar"], n + 1)
                    pool.tensor_tensor(gve[:, c:c + 1], gvar[:, c:c + 1], t["eps"][:], ALU.add).then_inc(sm["gve"], 1)
                    pool.wait_ge(sm["gve"], n + 1)
                    pool.tensor_tensor(grstd[:, c:c + 1], gve[:, c:c + 1], t["half"][:], ALU.pow)\
                        .then_inc(sm["grstd"], 1)
                for c in range(CB):
                    n = CB * j + c
                    pool.wait_ge(sm["moments"], TPB * (n + 1))
                    pool.tensor_tensor(ve[:, c, :], mv[:, c, :, 1], t["eps"][:].to_broadcast([P, TPB]),
                                       ALU.add).then_inc(sm["eps"], 1)
                    pool.wait_ge(sm["eps"], n + 1)
                    pool.tensor_tensor(rstd[:, c, :], ve[:, c, :], t["half"][:].to_broadcast([P, TPB]),
                                       ALU.pow).then_inc(sm["rstd"], 1)

        @block.scalar
        def _(act):
            with act.Fori(0, steps) as j:
                for c in range(CB):
                    n = CB * j + c
                    act.wait_ge(sm["xin"], TPB * (n + 1))
                    act.wait_ge(sm["tx"], CB * j)
                    act.activation(R1[c][:, 4:6, :], xin[c][:], ACT.Copy).then_inc(sm["xin_hi"], 1)
                for bank_at, r2, name, bias in ((0, 0, "theta", "theta_b"), (1, 2, "phi", "phi_b"), (2, 4, "g", None)):
                    for c in range(CB):
                        n = CB * j + c
                        act.wait_ge(sm[name], n + 1)
                        if bias:
                            act.activation(R2[c][:, r2, :], bank[c][bank_at][:], ACT.Identity, bias=t[bias][:])\
                                .then_inc(sm[name + "_hi"], 1)
                        else:
                            act.activation(R2[c][:, r2, :], bank[c][bank_at][:], ACT.Copy)\
                                .then_inc(sm[name + "_hi"], 1)
                for c in range(CB):
                    n = CB * j + c
                    act.wait_ge(sm["neg_max"], n + 1)
                    act.wait_ge(stored[c], 32 * j)
                    for i in range(NTT):
                        act.activation(prob[c][:, i, :], bank[c][(3 + i) % 4][:], ACT.Exp, bias=nmx[:, c, i:i + 1],
                                       accum_out=rsum[:, c, i:i + 1]).then_inc(sm["exp"], 1)
                for c in range(CB):
                    n = CB * j + c
                    for i in range(NTT):
                        act.wait_ge(sm["turned"], NTT * n + i + 1)
                        act.activation(R1[c][:, i, :], bank[c][i][:], ACT.Copy).then_inc(sm["pT_hi"], 1)
                for c in range(CB):
                    n = CB * j + c
                    act.wait_ge(sm["tx"], n + 1)
                    act.activation(prob[c][:, 0, :], bank[c][0][:], ACT.Identity, bias=t["g_b"][:])\
                        .then_inc(sm["tx_kept"], 1)
                for c in range(CB):
                    n = CB * j + c
                    act.wait_ge(sm["scaled"], n + 1)
                    act.activation(R2[c][:, 0, :], prob[c][:, 2, :], ACT.Relu).then_inc(sm["h_hi"], 1)
                for c in range(CB):
                    n = CB * j + c
                    for u in range(TPB):
                        act.wait_ge(sm["x3T"], TPB * n + u + 1)
                        act.activation(R2[c][:, 2 + u, :], bank[c][u][:], ACT.Copy).then_inc(sm["x3_hi"], 1)

        @block.vector
        def _(dve):
            with dve.Fori(0, steps) as j:
                for c in range(CB):
                    n = CB * j + c
                    wait_apart(dve, stored[c], 32 * j, sm["passed_dve"])
                    for u in range(TPB):
                        dve.tensor_scalar(xin[c][:, u, :], t["act"][:, TPB * n + u, :], t["mean1"][:, TPB * n + u, :],
                                          t["rstd1"][:, TPB * n + u, :], ALU.subtract, ALU.mult)\
                            .then_inc(sm["xin"], 1)
                for c in range(CB):
                    n = CB * j + c
                    dve.wait_ge(sm["xin_hi"], n + 1)
                    dve.tensor_tensor(R1[c][:, 6:8, :], xin[c][:], f32(R1[c][:, 4:6, :]), ALU.subtract)\
                        .then_inc(sm["xin_lo"], 1)
                for bank_at, r2, name, bias in ((0, 0, "theta", "theta_b"), (1, 2, "phi", "phi_b"), (2, 4, "g", None)):
                    for c in range(CB):
                        n = CB * j + c
                        dve.wait_ge(sm[name + "_hi"], n + 1)
                        if bias:
                            dve.scalar_tensor_tensor(R2[c][:, r2 + 1, :], bank[c][bank_at][:], t[bias][:],
                                                     f32(R2[c][:, r2, :]), ALU.add, ALU.subtract)\
                                .then_inc(sm[name + "_lo"], 1)
                        else:
                            dve.tensor_tensor(R2[c][:, r2 + 1, :], bank[c][bank_at][:], f32(R2[c][:, r2, :]),
                                              ALU.subtract).then_inc(sm[name + "_lo"], 1)
                for c in range(CB):
                    n = CB * j + c
                    for i in range(NTT):
                        dve.wait_ge(sm["scores"], NTT * n + i + 1)
                        dve.tensor_reduce(mx[:, c, i:i + 1], bank[c][(3 + i) % 4][:], AX.X, ALU.max)\
                            .then_inc(sm["max"], 1)
                    dve.wait_ge(sm["max"], NTT * (n + 1))
                    dve.tensor_scalar(nmx[:, c, :], mx[:, c, :], -1.0, None, ALU.mult).then_inc(sm["neg_max"], 1)
                for c in range(CB):
                    n = CB * j + c
                    dve.wait_ge(sm["exp"], NTT * (n + 1))
                    dve.reciprocal(rinv[:, c, :], rsum[:, c, :]).then_inc(sm["rinv"], 1)
                    dve.wait_ge(sm["rinv"], n + 1)
                    for i in range(NTT):
                        dve.tensor_scalar(prob[c][:, i, :], prob[c][:, i, :], rinv[:, c, i:i + 1], None, ALU.mult)\
                            .then_inc(sm["norm"], 1)
                for c in range(CB):
                    n = CB * j + c
                    for i in range(NTT):
                        dve.wait_ge(sm["pT_hi"], NTT * n + i + 1)
                        dve.tensor_tensor(R1[c][:, NTT + i, :], bank[c][i][:], f32(R1[c][:, i, :]), ALU.subtract)\
                            .then_inc(sm["pT_lo"], 1)
                for c in range(CB):
                    n = CB * j + c
                    dve.wait_ge(sm["tx_kept"], n + 1)
                    dve.bn_stats(pst[:, c, :], prob[c][:, 0, :]).then_inc(sm["row_stats"], 1)
                for c in range(CB):
                    n = CB * j + c
                    wait_apart(dve, sm["row_stats"], n + 1, sm["passed_dve"])
                    dve.bn_aggr(pmv[:, c, :], pst[:, c, :]).then_inc(sm["row_moments"], 1)
                for c in range(CB):
                    n = CB * j + c
                    dve.wait_ge(sm["row_moments"], n + 1)
                    dve.tensor_tensor(psq[:, c:c + 1], pmv[:, c, 0:1], pmv[:, c, 0:1], ALU.mult)\
                        .then_inc(sm["row_sq"], 1)
                    dve.wait_ge(sm["row_sq"], n + 1)
                    dve.tensor_tensor(pmv[:, c, 1:2], pmv[:, c, 1:2], psq[:, c:c + 1], ALU.add)\
                        .then_inc(sm["row_m2"], 1)
                for c in range(CB):
                    n = CB * j + c
                    dve.wait_ge(sm["all_moments"], n + 1)
                    dve.tensor_copy(gmv[:, c, :], bank[c][1][:, 0:2]).then_inc(sm["gmv"], 1)
                    dve.wait_ge(sm["gmv"], n + 1)
                    dve.tensor_tensor(gsq[:, c:c + 1], gmv[:, c, 0:1], gmv[:, c, 0:1], ALU.mult)\
                        .then_inc(sm["gsq"], 1)
                    dve.wait_ge(sm["gsq"], n + 1)
                    dve.tensor_tensor(gvar[:, c:c + 1], gmv[:, c, 1:2], gsq[:, c:c + 1], ALU.subtract)\
                        .then_inc(sm["gvar"], 1)
                for c in range(CB):
                    n = CB * j + c
                    dve.scalar_tensor_tensor(prob[c][:, 1, :], prob[c][:, 0, :], gmv[:, c, 0:1], t["gamma"][:],
                                             ALU.subtract, ALU.mult).then_inc(sm["centred"], 1)
                for c in range(CB):
                    n = CB * j + c
                    dve.wait_ge(sm["grstd"], n + 1)
                    dve.wait_ge(sm["centred"], n + 1)
                    dve.scalar_tensor_tensor(prob[c][:, 2, :], prob[c][:, 1, :], grstd[:, c:c + 1], t["beta"][:],
                                             ALU.mult, ALU.add).then_inc(sm["scaled"], 1)
                for c in range(CB):
                    n = CB * j + c
                    dve.wait_ge(sm["h_hi"], n + 1)
                    dve.scalar_tensor_tensor(R2[c][:, 1, :], prob[c][:, 2, :], 0.0, f32(R2[c][:, 0, :]),
                                             ALU.max, ALU.subtract).then_inc(sm["h_lo"], 1)
                for c in range(CB):
                    n = CB * j + c
                    dve.wait_ge(sm["ctx_res"], n + 1)
                    for u in range(TPB):
                        dve.wait_ge(sm["out"], TPB * n + u + 1)
                        dve.scalar_tensor_tensor(xin[c][:, u, :], bank[c][2 + u][:], t["out_b"][:, u:u + 1],
                                                 ctx_in[c][:, u, :], ALU.add, ALU.add).then_inc(sm["x2"], 1)
                for c in range(CB):
                    n = CB * j + c
                    for u in range(TPB):
                        dve.wait_ge(sm["x2"], TPB * n + u + 1)
                        dve.bn_stats(st6[:, c, u, :], xin[c][:, u, :]).then_inc(sm["stats"], 1)
                for c in range(CB):
                    n = CB * j + c
                    wait_apart(dve, sm["stats"], TPB * (n + 1), sm["passed_dve"])
                    for u in range(TPB):
                        dve.bn_aggr(mv[:, c, u, :], st6[:, c, u, :]).then_inc(sm["moments"], 1)
                for c in range(CB):
                    n = CB * j + c
                    dve.wait_ge(sm["rstd"], n + 1)
                    for u in range(TPB):
                        dve.tensor_scalar(prob[c][:, u, :], xin[c][:, u, :], mv[:, c, u, 0:1], rstd[:, c, u:u + 1],
                                          ALU.subtract, ALU.mult).then_inc(sm["xn3"], 1)
                for c in range(CB):
                    n = CB * j + c
                    for u in range(TPB):
                        dve.wait_ge(sm["x3_hi"], TPB * n + u + 1)
                        dve.tensor_tensor(R2[c][:, 4 + u, :], bank[c][u][:], f32(R2[c][:, 2 + u, :]),
                                          ALU.subtract).then_inc(sm["x3_lo"], 1)
                for c in range(CB):
                    n = CB * j + c
                    wait_apart(dve, sm["logits"], n + 1, sm["passed_dve"])
                    dve.tensor_copy(t["logits"][:, bass.ds(TPB * n, TPB), :],
                                    bank[c][2][:, 0:TPB * E].rearrange("p (u e) -> p u e", u=TPB))\
                        .then_inc(sm["logits_kept"], 1)

        @block.tensor
        def _(pe):
            with pe.Fori(0, steps) as j:
                for c in range(CB):
                    n = CB * j + c
                    pe.wait_ge(sm["ctx_lo"], n + 1)
                    for k in range(TPB):
                        m = split_passes(pe, bank[c][0][:], [w[:, k, :] for w in t["theta_w"]],
                                         (R1[c][:, k, :], R1[c][:, 2 + k, :]), k == 0, k == TPB - 1)
                    m.then_inc(sm["theta"], 1)
                for c in range(CB):
                    n = CB * j + c
                    pe.wait_ge(sm["xin_lo"], n + 1)
                    for k in range(TPB):
                        m = split_passes(pe, bank[c][1][:], [w[:, k, :] for w in t["phi_w"]],
                                         (R1[c][:, 4 + k, :], R1[c][:, 6 + k, :]), k == 0, k == TPB - 1)
                    m.then_inc(sm["phi"], 1)
                for c in range(CB):
                    n = CB * j + c
                    pe.wait_ge(sm["logits_kept"], CB * j)
                    for i in range(NTT):
                        for k in range(TPB):
                            m = split_passes(pe, bank[c][2][:, i * P:(i + 1) * P],
                                             (R1[c][:, 4 + k, i * P:(i + 1) * P], R1[c][:, 6 + k, i * P:(i + 1) * P]),
                                             [w[:, k, :] for w in t["g_w"]], k == 0, k == TPB - 1)
                    m.then_inc(sm["g"], 1)
                for c in range(CB):
                    n = CB * j + c
                    pe.wait_ge(sm["theta_lo"], n + 1)
                    pe.wait_ge(sm["phi_lo"], n + 1)
                    for i in range(NTT):
                        if i == 3:
                            pe.wait_ge(sm["g_lo"], n + 1)
                        m = split_passes(pe, bank[c][(3 + i) % 4][:],
                                         (R2[c][:, 0, i * P:(i + 1) * P], R2[c][:, 1, i * P:(i + 1) * P]),
                                         (R2[c][:, 2, :], R2[c][:, 3, :]))
                        m.then_inc(sm["scores"], 1)
                for c in range(CB):
                    n = CB * j + c
                    for i in range(NTT):
                        pe.wait_ge(sm["norm"], NTT * (n + 1))
                        for k in range(NTT):
                            m = pe.transpose(bank[c][i][:, k * P:(k + 1) * P], prob[c][:, k, i * P:(i + 1) * P],
                                             t["ident"][:])
                        m.then_inc(sm["turned"], 1)
                for c in range(CB):
                    n = CB * j + c
                    for i in range(NTT):
                        pe.wait_ge(sm["pT_lo"], NTT * (n + 1))
                        m = split_passes(pe, bank[c][0][:],
                                         (R2[c][:, 4, i * P:(i + 1) * P], R2[c][:, 5, i * P:(i + 1) * P]),
                                         (R1[c][:, i, :], R1[c][:, NTT + i, :]), i == 0, i == NTT - 1)
                    m.then_inc(sm["tx"], 1)
                for c in range(CB):
                    n = CB * j + c
                    pe.wait_ge(sm["row_m2"], n + 1)
                    pe.matmul(bank[c][1][:, 0:2], t["avg"][:], pmv[:, c, :], start=True, stop=True)\
                        .then_inc(sm["all_moments"], 1)
                for c in range(CB):
                    n = CB * j + c
                    pe.wait_ge(sm["h_lo"], n + 1)
                    for u in range(TPB):
                        split_passes(pe, bank[c][2 + u][:], [w[:, u * P:(u + 1) * P] for w in t["out_w"]],
                                     (R2[c][:, 0, :], R2[c][:, 1, :])).then_inc(sm["out"], 1)
                for c in range(CB):
                    n = CB * j + c
                    for u in range(TPB):
                        pe.wait_ge(sm["xn3"], TPB * n + u + 1)
                        for k in range(KD):
                            m = pe.transpose(bank[c][u][:, k * P:(k + 1) * P], prob[c][:, u, k * P:(k + 1) * P],
                                             t["ident"][:])
                        m.then_inc(sm["x3T"], 1)
                for c in range(CB):
                    n = CB * j + c
                    for u in range(TPB):
                        pe.wait_ge(sm["x3_lo"], TPB * n + u + 1)
                        for k in range(KD):
                            m = split_passes(pe, bank[c][2][:, u * E:(u + 1) * E],
                                             (R2[c][:, 2 + u, k * P:(k + 1) * P], R2[c][:, 4 + u, k * P:(k + 1) * P]),
                                             [w[:, k, :] for w in t["router_w"]], k == 0, k == KD - 1)
                    m.then_inc(sm["logits"], 1)


def stage_route(nc, io, t):
    with Scope(nc) as s:
        W = [P, NT, E]
        lg = t["logits"]
        red = s.sb("rt_red", [P, 4, NT])
        ex = s.sb("rt_ex", W)
        prob = s.sb("rt_prob", W)
        eq = s.sb("rt_eq", W)
        hot = [s.sb(f"rt_hot{k}", W) for k in range(TOPK)]
        chosen = s.sb("rt_chosen", W)
        scan = [s.sb(f"rt_scan{k}", W) for k in range(2)]
        total = s.sb("rt_total", W)
        place = s.sb("rt_place", W)
        kept = s.sb("rt_kept", W)
        tmp = s.sb("rt_tmp", W)
        ei = s.sb("rt_ei", [P, E], I32)
        ef = s.sb("rt_ef", [P, E])
        em = s.sb("rt_em", [P, E])
        ec = s.sb("rt_ec", [P, E])
        token = s.sb("rt_token", [P, NT], I32)
        tokenf = s.sb("rt_tokenf", [P, NT])
        dump = s.sb("rt_dump", [P, NT])
        has = s.sb("rt_has", [P, NT])
        slot = s.sb("rt_slot", [P, NT])
        scat = s.sb("rt_scat", [P, TOPK, NT], I32)
        zero = s.sb("rt_zero", [ST, P], I32)
        tab = s.sb("rt_tab", [ST, P], I32)
        tabf = s.sb("rt_tabf", [ST, P])
        pp = s.ps("rt_pp", [P, 512])
        pt = s.ps("rt_pt", [P, 512])
        names = ("iota", "zeroed", "cleared", "exp_in", "exp", "dve", "counts", "scatter_idx", "scattered",
                 "table_loaded", "table_f", "table_T", "idx")
        sm = {n: s.sem("rt_" + n) for n in names}
        block = s.ctx.enter_context(nc.Block())

        @block.sync
        def _(sp):
            sp.wait_ge(sm["zeroed"], 1)
            sp.dma_start(io["table"][0:SLOTS, :].rearrange("(a b) o -> a (b o)", b=P), zero[:])\
                .then_inc(sm["cleared"], 16)
            sp.wait_ge(sm["scattered"], 16 * TOPK * NT)
            sp.dma_start(tab[:], io["table"][0:SLOTS, :].rearrange("(a b) o -> a (b o)", b=P))\
                .then_inc(sm["table_loaded"], 16)
            sp.wait_ge(sm["table_loaded"], 16)

        @block.gpsimd
        def _(pool):
            pool.iota(ei[:], pattern=[[1, E]], base=0, channel_multiplier=0).then_inc(sm["iota"], 1)
            pool.iota(token[:], pattern=[[P, NT]], base=0, channel_multiplier=1).then_inc(sm["iota"], 1)
            pool.memset(zero[:], 0).then_inc(sm["zeroed"], 1)
            pool.wait_ge(sm["cleared"], 16)
            for k in range(TOPK):
                pool.wait_ge(sm["scatter_idx"], k + 1)
                for n in range(NT):
                    pool.indirect_dma_start(io["table"][:, :], bass.IndirectOffsetOnAxis(scat[:, k, n:n + 1], 0),
                                            token[:, n:n + 1], None).then_inc(sm["scattered"], 16)

        @block.scalar
        def _(act):
            act.wait_ge(sm["exp_in"], 1)
            act.activation(ex[:], ex[:], ACT.Exp).then_inc(sm["exp"], 1)

        @block.vector
        def _(dve):
            count = [0]

            def link(i):
                count[0] += 1
                i.then_inc(sm["dve"], 1)
                dve.wait_ge(sm["dve"], count[0])

            def tiles(ap):
                return ap.unsqueeze(2).to_broadcast(W)

            def experts(ap):
                return ap.unsqueeze(1).to_broadcast(W)

            TT, TS, RED = dve.tensor_tensor, dve.tensor_scalar, dve.tensor_reduce
            link(RED(red[:, 0, :], lg[:], AX.X, ALU.max))
            TT(ex[:], lg[:], tiles(red[:, 0, :]), ALU.subtract).then_inc(sm["exp_in"], 1)
            dve.wait_ge(sm["iota"], 2)
            dve.tensor_copy(ef[:], ei[:])
            link(dve.tensor_copy(tokenf[:], token[:]))
            TS(em[:], ef[:], float(-E), None, ALU.add)
            TS(ec[:], ef[:], float(CAP), None, ALU.mult)
            dve.wait_ge(sm["exp"], 1)
            link(RED(red[:, 1, :], ex[:], AX.X, ALU.add))
            link(dve.reciprocal(red[:, 2, :], red[:, 1, :]))
            link(TT(prob[:], ex[:], tiles(red[:, 2, :]), ALU.mult))
            for k in range(TOPK):
                link(RED(t["gate"][:, k, :], prob[:], AX.X, ALU.max))
                link(TT(eq[:], prob[:], tiles(t["gate"][:, k, :]), ALU.is_equal))
                link(TT(eq[:], eq[:], experts(em[:]), ALU.mult))
                link(RED(red[:, 3, :], eq[:], AX.X, ALU.min))
                link(TT(hot[k][:], tiles(red[:, 3, :]), experts(em[:]), ALU.is_equal))
                if k == 0:
                    link(dve.scalar_tensor_tensor(prob[:], hot[k][:], -2.0, prob[:], ALU.mult, ALU.add))
            TT(chosen[:], hot[0][:], hot[1][:], ALU.add).then_inc(sm["counts"], 1)
            dve.wait_ge(sm["counts"], 2)
            flat = [x[:].rearrange("p a e -> p (a e)") for x in (total, scan[0])]
            dve.tensor_copy(flat[0], pp[:, NT * E:2 * NT * E])
            link(dve.tensor_copy(flat[1], pp[:, NT * E:2 * NT * E]))
            step, a = 1, 0
            while step < NT:
                TT(scan[1 - a][:, step:, :], scan[a][:, step:, :], scan[a][:, :NT - step, :], ALU.add)
                link(dve.tensor_copy(scan[1 - a][:, :step, :], scan[a][:, :step, :]))
                step, a = 2 * step, 1 - a
            link(TT(place[:], scan[a][:], total[:], ALU.subtract))
            link(TT(place[:], place[:], pp[:, 0:NT * E].rearrange("p (a e) -> p a e", e=E), ALU.add))
            TS(kept[:], place[:], float(CAP), None, ALU.is_lt)
            link(TT(place[:], place[:], experts(ec[:]), ALU.add))
            link(TT(place[:], place[:], kept[:], ALU.mult))
            for k in range(TOPK):
                link(TT(tmp[:], hot[k][:], kept[:], ALU.mult))
                link(RED(has[:], tmp[:], AX.X, ALU.add))
                link(TT(tmp[:], hot[k][:], place[:], ALU.mult))
                link(RED(slot[:], tmp[:], AX.X, ALU.add))
                link(TS(dump[:], tokenf[:], float(SLOTS + k * B * S), None, ALU.add))
                TT(t["gate"][:, k, :], t["gate"][:, k, :], has[:], ALU.mult)
                dve.tensor_copy(t["where"][:, k, :], slot[:])
                link(TS(has[:], has[:], -1.0, 1.0, ALU.mult, ALU.add))
                link(TT(dump[:], dump[:], has[:], ALU.mult))
                link(TT(slot[:], slot[:], dump[:], ALU.add))
                dve.tensor_copy(scat[:, k, :], slot[:]).then_inc(sm["scatter_idx"], 1)
                dve.wait_ge(sm["scatter_idx"], k + 1)
            dve.memset(t["slot_token"][:], 0).then_inc(sm["table_f"], 1)
            dve.wait_ge(sm["table_loaded"], 16)
            dve.tensor_copy(tabf[:], tab[:]).then_inc(sm["table_f"], 1)
            dve.wait_ge(sm["table_T"], 1)
            dve.tensor_copy(t["slot_token"][:, 0:ST], pt[:, 0:ST]).then_inc(sm["idx"], 1)

        @block.tensor
        def _(pe):
            pe.wait_ge(sm["counts"], 1)
            c = chosen[:].rearrange("p a e -> p (a e)")
            pe.matmul(pp[:, 0:NT * E], t["upper"][:], c, start=True, stop=True)
            pe.matmul(pp[:, NT * E:2 * NT * E], t["ones"][:], c, start=True, stop=True).then_inc(sm["counts"], 1)
            pe.wait_ge(sm["table_f"], 2)
            pe.transpose(pt[:, 0:ST], tabf[:], t["ident"][0:ST, 0:ST]).then_inc(sm["table_T"], 1)


def stage_experts(nc, io, t):
    with Scope(nc) as s:
        RW = 2
        HB = BLK // 2
        w1 = [s.sb(f"ex_w1_{p}", [P, NF, KD, P], F32R) for p in "hl"]
        w2 = [s.sb(f"ex_w2_{p}", [P, NF, D], F32R) for p in "hl"]
        raw = s.sb("ex_raw", [P, RW, 2, D])
        xT = [[s.sb(f"ex_xT{b}{p}", [P, KD, BLK], F32R) for p in "hl"] for b in range(2)]
        h = [[s.sb(f"ex_h{r}{p}", [P, 2, HB], F32R) for p in "hl"] for r in range(2)]
        xg = [s.sb(f"ex_xg{r}", [P, D]) for r in range(2)]
        gi = [s.sb(f"ex_gi{r}", [P, 1], I32) for r in range(2)]
        ys = s.sb("ex_ys", [P, BT, D])
        hid = s.ps("ex_hid", [P, 2, 512])
        acc = [s.ps(f"ex_acc{i}", [P, D]) for i in range(BT)]
        xb = s.ps("ex_xb", [P, D])
        raw_loaded = [s.sem(f"raw_loaded{r}") for r in range(RW)]
        gathered = [s.sem(f"gathered{r}") for r in range(2)]
        names = ("w_hi", "w_lo", "idx_col", "x_turned", "x_hi", "x_lo", "hidden", "h_hi", "h_lo", "used",
                 "y_act", "y_dve", "y_stored", "passed_pool")
        sm = {n: s.sem("ex_" + n) for n in names}
        block = s.ctx.enter_context(nc.Block())

        TURN = {3 * i: i for i in range(BT)}

        @block.sync
        def _(sp):
            with sp.Fori(0, E) as e:
                for f in range(NF):
                    sp.wait_ge(sm["w_lo"], 2 * (NF * e + f - RW) + 2 if f >= RW else 2 * NF * e)
                    sp.dma_start(raw[:, f % RW, 0, :], io["w1_tiles"][NF * e + f]).then_inc(raw_loaded[f % RW], 16)
                    sp.dma_start(raw[:, f % RW, 1, :], io["w2_tiles"][NF * e + f]).then_inc(raw_loaded[f % RW], 16)

        @block.gpsimd
        def _(pool):
            def gather(n, r, first):
                if not first:
                    wait_apart(pool, sm["x_turned"], n - 1, sm["passed_pool"])
                pool.tensor_copy(gi[r][:], t["slot_token"][:, bass.ds(n, 1)]).then_inc(sm["idx_col"], 1)
                wait_apart(pool, sm["idx_col"], n + 1, sm["passed_pool"])
                pool.indirect_dma_start(xg[r][:], None, io["xn3"][:, :], bass.IndirectOffsetOnAxis(gi[r][:], 0))\
                    .then_inc(gathered[r], 16)

            gather(0, 0, True)
            gather(1, 1, True)
            with pool.Fori(0, (ST + BT - 3) // 2 + 1) as j:
                for r in range(2):
                    gather(2 * j + 2 + r, r, False)
            for r in range(2):
                pool.wait_ge(gathered[r], 16 * (ST + BT + 1) // 2)

        @block.scalar
        def _(act):
            def turn_hi(m, b, i):
                act.wait_ge(sm["x_turned"], BT * m + i + 1)
                act.activation(xT[b][0][:, :, i * P:(i + 1) * P], xb[:].rearrange("p (k n) -> p k n", k=KD), ACT.Copy)\
                    .then_inc(sm["x_hi"], 1)

            def split_hi(e, f):
                act.wait_ge(raw_loaded[f % RW], 32 * ((NF * e + f - f % RW) // RW + 1) if isinstance(e, int) else
                            e * (32 * NF // RW) + 32 * (f // RW + 1))
                wait(act, sm["used"], 2 * NF * e - NF + f + 1 if not isinstance(e, int) or e else 0)
                act.activation(w1[0][:, f, :, :].rearrange("p k n -> p (k n)"), raw[:, f % RW, 0, :], ACT.Copy)\
                    .then_inc(sm["w_hi"], 1)
                act.activation(w2[0][:, f, :], raw[:, f % RW, 1, :], ACT.Copy).then_inc(sm["w_hi"], 1)

            def block_steps(e, b, refill):
                m = 2 * e + b
                for f in range(NF):
                    act.wait_ge(sm["hidden"], NF * m + f + 1)
                    act.activation(h[f % 2][0][:], hid[:, :, 0:HB], ACT.Relu).then_inc(sm["h_hi"], 1)
                    if f in TURN:
                        turn_hi(m + 1, 1 - b, TURN[f])
                    if refill and f >= 2:
                        split_hi(e + 1, f - 2)
                act.wait_ge(sm["used"], NF * (m + 1))
                act.wait_ge(sm["y_stored"], 16 * m)
                for i in range(0, 2):
                    act.activation(ys[:, i, :], acc[i][:], ACT.Copy).then_inc(sm["y_act"], 1)
                if refill:
                    split_hi(e + 1, NF - 2)
                    split_hi(e + 1, NF - 1)
                act.wait_ge(sm["y_dve"], 3 * (m + 1))
                act.wait_ge(sm["y_act"], 2 * (m + 1))
                act.dma_start(io["y_blocks"][m], ys[:]).then_inc(sm["y_stored"], 16)

            for i in range(BT):
                turn_hi(0, 0, i)
            for f in range(NF):
                split_hi(0, f)
            with act.Fori(0, E - 1) as e:
                block_steps(e, 0, False)
                block_steps(e, 1, True)
            block_steps(E - 1, 0, False)
            block_steps(E - 1, 1, False)
            act.wait_ge(sm["y_stored"], 16 * 2 * E)

        @block.vector
        def _(dve):
            def turn_lo(m, b, i):
                dve.wait_ge(sm["x_hi"], BT * m + i + 1)
                dve.tensor_tensor(xT[b][1][:, :, i * P:(i + 1) * P], xb[:].rearrange("p (k n) -> p k n", k=KD),
                                  f32(xT[b][0][:, :, i * P:(i + 1) * P]), ALU.subtract).then_inc(sm["x_lo"], 1)

            def split_lo(e, f):
                dve.wait_ge(sm["w_hi"], 2 * (NF * e + f + 1))
                dve.tensor_tensor(w1[1][:, f, :, :].rearrange("p k n -> p (k n)"), raw[:, f % RW, 0, :],
                                  f32(w1[0][:, f, :, :]).rearrange("p k n -> p (k n)"), ALU.subtract)\
                    .then_inc(sm["w_lo"], 1)
                dve.tensor_tensor(w2[1][:, f, :], raw[:, f % RW, 1, :], f32(w2[0][:, f, :]), ALU.subtract)\
                    .then_inc(sm["w_lo"], 1)

            def block_steps(e, b, refill):
                m = 2 * e + b
                for f in range(NF):
                    dve.wait_ge(sm["h_hi"], NF * m + f + 1)
                    dve.scalar_tensor_tensor(h[f % 2][1][:], hid[:, :, 0:HB], 0.0, f32(h[f % 2][0][:]),
                                             ALU.max, ALU.subtract).then_inc(sm["h_lo"], 1)
                    if f in TURN:
                        turn_lo(m + 1, 1 - b, TURN[f])
                    if refill and f >= 2:
                        split_lo(e + 1, f - 2)
                dve.wait_ge(sm["used"], NF * (m + 1))
                dve.wait_ge(sm["y_stored"], 16 * m)
                for i in range(2, BT):
                    dve.tensor_copy(ys[:, i, :], acc[i][:]).then_inc(sm["y_dve"], 1)
                if refill:
                    split_lo(e + 1, NF - 2)
                    split_lo(e + 1, NF - 1)

            for i in range(BT):
                turn_lo(0, 0, i)
            for f in range(NF):
                split_lo(0, f)
            with dve.Fori(0, E - 1) as e:
                block_steps(e, 0, False)
                block_steps(e, 1, True)
            block_steps(E - 1, 0, False)
            block_steps(E - 1, 1, False)

        @block.tensor
        def _(pe):
            def turn(m, i, parity, first):
                n = BT * m + i
                r = (parity * BT + i) % 2
                pe.wait_ge(gathered[r], 16 * (BT * m // 2 + i // 2 + 1) if isinstance(m, int) else
                           first * (16 * BT) + 16 * ((parity * BT + i) // 2 + 1))
                wait(pe, sm["x_lo"], n)
                for k in range(KD):
                    q = pe.transpose(xb[:, k * P:(k + 1) * P], xg[r][:, k * P:(k + 1) * P], t["ident"][:])
                q.then_inc(sm["x_turned"], 1)

            for i in range(BT):
                turn(0, i, 0, 0)
            with pe.Fori(0, E) as e:
                for b in range(2):
                    m = 2 * e + b

                    def outputs(f):
                        pe.wait_ge(sm["h_lo"], NF * m + f + 1)
                        if f == 0:
                            pe.wait_ge(sm["y_act"], 2 * m)
                            pe.wait_ge(sm["y_dve"], (BT - 2) * m)
                        for i in range(BT):
                            hh, hl = (x[:].rearrange("p a n -> p (a n)")[:, i * P:(i + 1) * P] for x in h[f % 2])
                            q = split_passes(pe, acc[i][:], (hh, hl), [w[:, f, :] for w in w2], f == 0, f == NF - 1)
                        q.then_inc(sm["used"], 1)

                    pe.wait_ge(sm["x_lo"], BT * (m + 1))
                    for f in range(NF):
                        pe.wait_ge(sm["w_lo"], 2 * (NF * e + f + 1))
                        pe.wait_ge(sm["h_lo"], NF * m + f)
                        for k in range(KD):
                            for a, q in ((0, 0), (0, 1), (1, 0)):
                                for z in range(2):
                                    i = pe.matmul(hid[:, z, 0:HB], w1[a][:, f, k, :],
                                                  xT[b][q][:, k, z * HB:(z + 1) * HB], start=k == 0 and a + q == 0,
                                                  stop=k == KD - 1 and a == 1)
                        i.then_inc(sm["hidden"], 1)
                        if f in TURN:
                            turn(m + 1, TURN[f], 1 - b, e + b)
                        if f:
                            outputs(f - 1)
                    outputs(NF - 1)


def stage_combine(nc, io, t):
    with Scope(nc) as s:
        x2 = s.sb("cb_x2", [P, CH, D])
        y = [[s.sb(f"cb_y{c}{k}", [P, D]) for k in range(TOPK)] for c in range(CH)]
        gi = [[s.sb(f"cb_gi{c}{k}", [P, 1], I32) for k in range(TOPK)] for c in range(CH)]
        x2_loaded = [s.sem(f"x2_loaded{c}") for c in range(CH)]
        gathered = [[s.sem(f"y_gathered{c}{k}") for k in range(TOPK)] for c in range(CH)]
        stored = [s.sem(f"out_stored{c}") for c in range(CH)]
        idx_col, part, done, passed_dve, passed_pool = (
            s.sem("cb_" + n) for n in ("idx_col", "part", "done", "passed_dve", "passed_pool"))
        block = s.ctx.enter_context(nc.Block())
        steps = NT // CH

        @block.sync
        def _(sp):
            with sp.Fori(0, steps) as j:
                for c in range(CH):
                    sp.wait_ge(stored[c], 16 * j)
                    sp.dma_start(x2[:, c, :], io["x2"][CH * j + c]).then_inc(x2_loaded[c], 16)

        @block.scalar
        def _(act):
            with act.Fori(0, steps) as j:
                for c in range(CH):
                    act.wait_ge(done, CH * j + c + 1)
                    act.dma_start(io["out_tiles"][CH * j + c], x2[:, c, :]).then_inc(stored[c], 16)
            for c in range(CH):
                act.wait_ge(stored[c], 16 * steps)

        @block.gpsimd
        def _(pool):
            with pool.Fori(0, steps) as j:
                for c in range(CH):
                    for k in range(TOPK):
                        n = CH * j + c
                        wait_apart(pool, done, CH * j, passed_pool)
                        pool.tensor_copy(gi[c][k][:], t["where"][:, k, bass.ds(n, 1)]).then_inc(idx_col, 1)
                        wait_apart(pool, idx_col, TOPK * n + k + 1, passed_pool)
                        pool.indirect_dma_start(y[c][k][:], None, io["y"][:, :],
                                                bass.IndirectOffsetOnAxis(gi[c][k][:], 0)).then_inc(gathered[c][k], 16)

        @block.vector
        def _(dve):
            with dve.Fori(0, steps) as j:
                for c in range(CH):
                    n = CH * j + c
                    dve.wait_ge(x2_loaded[c], 16 * j + 16)
                    for k in range(TOPK):
                        if k:
                            dve.wait_ge(part, n + 1)
                        wait_apart(dve, gathered[c][k], 16 * j + 16, passed_dve)
                        i = dve.scalar_tensor_tensor(x2[:, c, :], y[c][k][:], t["gate"][:, k, bass.ds(n, 1)], x2[:, c, :],
                                                     ALU.mult, ALU.add)
                        i.then_inc(part if k == 0 else done, 1)


def decoder_layer(nc, io):
    with Scope(nc) as s:
        t = {}
        t["ident"] = s.sb("ident", [P, P])
        t["identb"] = s.sb("identb", [P, P], BF16)
        t["mask"] = s.sb("mask", [P, P], BF16)
        t["ones"] = s.sb("ones", [P, P])
        t["upper"] = s.sb("upper", [P, P])
        t["avg"] = s.sb("avg", [P, P])
        t["half"] = s.sb("half", [P, 1])
        t["eps"] = s.sb("eps", [P, 1])
        t["gate"] = s.sb("gate", [P, TOPK, NT])
        t["where"] = s.sb("where", [P, TOPK, NT], I32)
        t["slot_token"] = s.sb("slot_token", [P, ST + BT + 1], I32)
        with Scope(nc) as a:
            t["logits"] = a.sb("logits", [P, NT, E])
            t["act"] = a.sb("act", [P, NT, D])
            t["mean1"] = a.sb("mean1", [P, NT, 1])
            t["rstd1"] = a.sb("rstd1", [P, NT, 1])
            for n in ("theta_b", "phi_b", "g_b"):
                t[n] = a.sb(n + "_col", [P, 1])
            t["out_b"] = a.sb("out_b_col", [P, TPB])
            t["gamma"] = a.sb("gamma", [P, D])
            t["beta"] = a.sb("beta", [P, D])
            shapes = {"wo": [P, KD, D], "theta_w": [P, TPB, LAT], "phi_w": [P, TPB, LAT], "g_w": [P, TPB, LAT],
                      "out_w": [P, S], "router_w": [P, KD, E]}
            for n, shape in shapes.items():
                t[n] = [a.sb(f"{n}_{p}", shape, F32R) for p in ("hi", "lo")]
            with Scope(nc) as q:
                t["k"] = q.sb("k", [P, NT, KVW])
                t["v"] = q.sb("v", [P, NT, G, VW])
                t["cos"] = q.sb("cos", [P, TPB, HD])
                t["sin"] = q.sb("sin", [P, TPB, HD])
                with Scope(nc) as w:
                    t["wqkv"] = [w.sb(f"wqkv_{p}", [P, KD, QKV], F32R) for p in ("hi", "lo")]
                    t["split"] = ["wqkv", *shapes]
                    stage_constants(nc, io, t)
                    stage_qkv(nc, io, t)
                stage_attention(nc, t)
            stage_out_proj(nc, io, t)
            stage_cross(nc, io, t)
            stage_route(nc, io, t)
        stage_experts(nc, io, t)
        stage_combine(nc, io, t)


def build(nc, arrays, out):
    io = {}
    for name, (shape, dt) in arrays.items():
        io[name] = nc.dram_tensor(f"in_{name}_dram", shape, dt, kind="ExternalInput").ap()
    x2 = nc.dram_tensor("x2_dram", [NT, P, D], F32, kind="Internal").ap()
    xn3 = nc.dram_tensor("xn3_dram", [B * S, D], F32, kind="Internal").ap()
    y = nc.dram_tensor("y_dram", [SLOTS, D], F32, kind="Internal").ap()
    io["table"] = nc.dram_tensor("slot_table_dram", [SLOTS + TOPK * B * S, 1], I32, kind="Internal").ap()
    io["x2"], io["xn3"], io["y"] = x2, xn3, y
    io["x_tiles"] = io["x"].rearrange("b (u p) d -> (b u) p d", p=P)
    io["ctx_tiles"] = io["ctx"].rearrange("b (u p) d -> b p u d", p=P)
    io["x2_tiles"] = x2.rearrange("(b u) p d -> b p u d", u=TPB)
    io["xn3_tiles"] = xn3.rearrange("(b u p) d -> b p u d", u=TPB, p=P)
    io["y_blocks"] = y.rearrange("(m i p) d -> m p i d", i=BT, p=P)
    io["out_tiles"] = out.rearrange("b (u p) d -> (b u) p d", p=P)
    decoder_layer(nc, io)


def kernel(x, ctx_2048, L0_attn_wq, L0_attn_wk, L0_attn_wv, L0_attn_wo, L0_xattn_theta_w, L0_xattn_theta_b,
           L0_xattn_phi_w, L0_xattn_phi_b, L0_xattn_g_w, L0_xattn_g_b, L0_xattn_ln_gamma, L0_xattn_ln_beta,
           L0_xattn_out_w, L0_xattn_out_b, L0_ffn_Wg, L0_ffn_w1, L0_ffn_w2):
    import numpy as np
    import concourse.bacc as bacc
    from concourse.bass_utils import run_bass_kernel_spmd

    order = np.concatenate([np.arange(0, HD, 2), np.arange(1, HD, 2)])

    def halves(w):
        w = np.asarray(w)
        return w.reshape(D, -1, HD)[:, :, order].reshape(D, -1)

    def contraction_tiles(w):
        w = np.asarray(w)
        return np.ascontiguousarray(w.reshape(-1, P, w.shape[1]).transpose(1, 0, 2))

    inv_freq = (1.0 / 10000.0 ** (np.arange(0, HD, 2, dtype=np.float32) / HD)).astype(np.float32)
    angle = np.arange(S, dtype=np.float32)[:, None] * inv_freq[None, :]
    cos, sin = np.cos(angle).astype(np.float32), np.sin(angle).astype(np.float32)

    def position_tiles(a):
        return np.ascontiguousarray(a.reshape(TPB, P, HD).transpose(1, 0, 2))

    arrays = {
        "x": np.ascontiguousarray(x),
        "ctx": np.ascontiguousarray(ctx_2048),
        "wqkv": contraction_tiles(np.concatenate([halves(L0_attn_wq), halves(L0_attn_wk), np.asarray(L0_attn_wv)], 1)),
        "wo": contraction_tiles(L0_attn_wo),
        "theta_w": contraction_tiles(np.asarray(L0_xattn_theta_w).T),
        "phi_w": contraction_tiles(np.asarray(L0_xattn_phi_w).T),
        "g_w": contraction_tiles(np.asarray(L0_xattn_g_w).T),
        "out_w": np.ascontiguousarray(np.asarray(L0_xattn_out_w).T),
        "router_w": contraction_tiles(L0_ffn_Wg),
        "theta_b": np.ascontiguousarray(L0_xattn_theta_b),
        "phi_b": np.ascontiguousarray(L0_xattn_phi_b),
        "g_b": np.ascontiguousarray(L0_xattn_g_b),
        "out_b": np.ascontiguousarray(np.asarray(L0_xattn_out_b).reshape(TPB, P).T),
        "gamma": np.ascontiguousarray(L0_xattn_ln_gamma),
        "beta": np.ascontiguousarray(L0_xattn_ln_beta),
        "cos": position_tiles(np.concatenate([cos, cos], 1)),
        "sin": position_tiles(np.concatenate([-sin, sin], 1)),
        "w1_tiles": np.ascontiguousarray(np.asarray(L0_ffn_w1).reshape(E, KD, P, NF, P).transpose(0, 3, 2, 1, 4)
                                         .reshape(E * NF, P, D)),
        "w2_tiles": np.ascontiguousarray(np.asarray(L0_ffn_w2).reshape(E * NF, P, D)),
    }
    nc = bacc.Bacc("TRN2", target_bir_lowering=False, num_devices=1)
    out = nc.dram_tensor("out_dram", [B, S, D], F32, kind="ExternalOutput").ap()
    build(nc, {n: (a.shape, mybir.dt.from_np(a.dtype)) for n, a in arrays.items()}, out)
    r = run_bass_kernel_spmd(nc, [{f"in_{n}_dram": a for n, a in arrays.items()}], core_ids=[0])
    return r.results[0]["out_dram"]
```

```python
from contextlib import ExitStack

import concourse.bass as bass
from concourse import mybir

F32 = mybir.dt.float32
F32R = mybir.dt.float32r
BF16 = mybir.dt.bfloat16
I32 = mybir.dt.int32
ALU = mybir.AluOpType
ACT = mybir.ActivationFunctionType
AX = mybir.AxisListType

P = 128
B, S, D = 16, 256, 512
NT = B * S // P
TPB = S // P
KD = D // P
H, G, HD = 32, 8, 16
REP = H // G
KVW = G * HD
QKV = D + 2 * KVW
VW = HD + 8
LAT = 128
E, FF, TOPK = 8, 2048, 2
CAP = (5 * B * S * TOPK) // (4 * E)
NF = FF // P
SLOTS = E * CAP
BLK = CAP // 2
BT = BLK // P
ST = SLOTS // P
EPS = 1e-5
MASKED = -1e30
ONE = 1
CH = 4


def wait(eng, sem, value):
    if not (isinstance(value, int) and value <= 0):
        eng.wait_ge(sem, ONE + value)


def wait_apart(eng, sem, value, passed, start=ONE):
    eng.wait_ge(sem, start + value).then_inc(passed, 1)


def f32(ap):
    return ap.bitcast(F32)


class Scope:

    def __init__(self, nc):
        self.nc = nc
        self.ctx = ExitStack()
        self.sems, self.zero_sems = [], []

    def __enter__(self):
        self.ctx.__enter__()
        return self

    def __exit__(self, *a):
        self.ctx.__exit__(*a)
        if self.sems:
            self.nc.clear_and_free_semaphores(self.sems + self.zero_sems)
            self.nc.all_engine_barrier()

    def sb(self, name, shape, dt=F32):
        return self.ctx.enter_context(self.nc.sbuf_tensor(name, shape, dt))

    def ps(self, name, shape, dt=F32):
        return self.ctx.enter_context(self.nc.psum_tensor(name, shape, dt))

    def sem(self, name):
        self.sems.append(self.nc.alloc_semaphore(name))
        return self.sems[-1]

    def zero_sem(self, name):
        self.zero_sems.append(self.nc.alloc_semaphore(name))
        return self.zero_sems[-1]

    def credit(self):
        engines = (self.nc.gpsimd, self.nc.scalar, self.nc.vector, self.nc.sync)
        for i, sem in enumerate(self.sems):
            engines[i % len(engines)].sem_inc(sem, ONE)
        self.nc.all_engine_barrier()


def split_passes(eng, out, lhs, rhs, first=True, last=True, **kw):
    eng.matmul(out, lhs[0], rhs[0], start=first, stop=False, **kw)
    eng.matmul(out, lhs[0], rhs[1], start=False, stop=False, **kw)
    return eng.matmul(out, lhs[1], rhs[0], start=False, stop=last, **kw)


def stage_constants(nc, io, t):
    with Scope(nc) as s:
        raw = {n: s.sb(f"raw_{n}", list(t[n][0].shape)) for n in t["split"]}
        ident_set, mask_set = s.sem("ident_zeroed"), s.sem("mask_zeroed")
        raw_loaded = s.sem("raw_weights_loaded")
        tables_loaded = s.sem("tables_loaded")
        hi_done, lo_done = s.sem("weights_hi_done"), s.sem("weights_lo_done")
        s.credit()
        block = s.ctx.enter_context(nc.Block())
        names = list(t["split"])

        @block.sync
        def _(sp):
            for n in names:
                sp.dma_start(raw[n][:], io[n]).then_inc(raw_loaded, 16)
            sp.dma_start(t["cos"][:], io["cos"]).then_inc(tables_loaded, 16)
            sp.dma_start(t["sin"][:], io["sin"]).then_inc(tables_loaded, 16)
            for n in ("theta_b", "phi_b", "g_b"):
                sp.dma_start(t[n][:], io[n].rearrange("(p o) -> p o", o=1)).then_inc(tables_loaded, 16)
            sp.dma_start(t["out_b"][:], io["out_b"]).then_inc(tables_loaded, 16)
            sp.dma_start(t["gamma"][:], io["gamma"]).then_inc(tables_loaded, 16)
            sp.dma_start(t["beta"][:], io["beta"]).then_inc(tables_loaded, 16)
            sp.wait_ge(tables_loaded, ONE + 16 * 8)

        @block.gpsimd
        def _(pool):
            pool.memset(t["ident"][:], 0.0).then_inc(ident_set, 1)
            pool.memset(t["identb"][:], 0.0).then_inc(ident_set, 1)
            pool.memset(t["mask"][:], 0.0).then_inc(mask_set, 1)
            pool.memset(t["ones"][:], 1.0)
            pool.memset(t["upper"][:], 1.0).then_inc(mask_set, 1)
            pool.memset(t["avg"][:], 1.0 / P)
            pool.memset(t["half"][:], -0.5)
            pool.memset(t["eps"][:], EPS)
            pool.wait_ge(ident_set, ONE + 2)
            for m in (t["ident"], t["identb"]):
                pool.affine_select(out=m[:], in_=m[:], compare_op=ALU.not_equal, fill=1.0, base=0,
                                   pattern=[[-1, P]], channel_multiplier=1)
            pool.wait_ge(mask_set, ONE + 2)
            pool.affine_select(out=t["mask"][:], in_=t["mask"][:], compare_op=ALU.is_ge, fill=MASKED, base=0,
                               pattern=[[-1, P]], channel_multiplier=1)
            pool.affine_select(out=t["upper"][:], in_=t["upper"][:], compare_op=ALU.is_gt, fill=0.0, base=0,
                               pattern=[[1, P]], channel_multiplier=-1)

        @block.scalar
        def _(act):
            act.wait_ge(raw_loaded, ONE + 16 * len(names))
            for n in names:
                act.activation(t[n][0][:], raw[n][:], ACT.Copy).then_inc(hi_done, 1)

        @block.vector
        def _(dve):
            dve.wait_ge(raw_loaded, ONE + 16 * len(names))
            for i, n in enumerate(names):
                dve.wait_ge(hi_done, ONE + i + 1)
                dve.tensor_tensor(t[n][1][:], raw[n][:], f32(t[n][0][:]), ALU.subtract).then_inc(lo_done, 1)


def stage_qkv(nc, io, t):
    with Scope(nc) as s:
        x = s.sb("qkv_x", [P, CH, D])
        xn = s.sb("qkv_xn", [P, CH, D])
        xh = [s.sb(f"qkv_xh{c}", [P, KD, P], F32R) for c in range(CH)]
        xl = [s.sb(f"qkv_xl{c}", [P, KD, P], F32R) for c in range(CH)]
        st6 = s.sb("qkv_st6", [P, CH, 6])
        mv = s.sb("qkv_mv", [P, CH, 2])
        ve = s.sb("qkv_ve", [P, CH])
        rstd = s.sb("qkv_rstd", [P, CH])
        rc = s.sb("qkv_rc", [P, 2, D + KVW])
        rs = s.sb("qkv_rs", [P, 2, D + KVW])
        xT = [s.ps(f"qkv_xT{c}", [P, D]) for c in range(2)]
        proj = [s.ps(f"qkv_proj{c}", [P, 1024]) for c in range(2)]
        x_loaded = [s.sem(f"x_loaded{c}") for c in range(CH)]
        stats, moments, eps_added, rstd_ready = (s.sem(n) for n in ("stats", "moments", "eps_added", "rstd_ready"))
        xn_ready, xT_ready, xh_ready, xl_ready = (s.sem(n) for n in ("xn_ready", "xT_ready", "xh_ready", "xl_ready"))
        proj_ready, rot_cos, rot_sin, rot_done, v_done = (
            s.sem(n) for n in ("proj_ready", "rot_cos", "rot_sin", "rot_done", "v_done"))
        passed_pool, passed_dve = s.sem("qkv_passed_pool"), s.sem("qkv_passed_dve")
        s.credit()
        block = s.ctx.enter_context(nc.Block())
        steps = NT // CH

        @block.sync
        def _(sp):
            with sp.Fori(0, steps) as j:
                for c in range(CH):
                    sp.wait_ge(xn_ready, ONE + CH * j)
                    sp.dma_start(x[:, c, :], io["x_tiles"][CH * j + c]).then_inc(x_loaded[c], 16)

        @block.gpsimd
        def _(pool):
            with pool.Fori(0, steps) as j:
                for c in range(CH):
                    n = CH * j + c
                    pool.wait_ge(moments, ONE + n + 1)
                    pool.tensor_tensor(ve[:, c:c + 1], mv[:, c, 1:2], t["eps"][:], ALU.add).then_inc(eps_added, 1)
                    pool.wait_ge(eps_added, ONE + n + 1)
                    pool.tensor_tensor(rstd[:, c:c + 1], ve[:, c:c + 1], t["half"][:, 0:1],
                                       ALU.pow).then_inc(rstd_ready, 1)
                for c in range(CH):
                    n = CH * j + c
                    pool.wait_ge(rot_sin, ONE + 2 * n + 2)
                    wait_apart(pool, rot_cos, n + 1, passed_pool)
                    pool.tensor_tensor(t["act"][:, n, :], rc[:, c % 2, 0:D], rs[:, c % 2, 0:D],
                                       ALU.add).then_inc(rot_done, 1)
                    pool.tensor_tensor(t["k"][:, n, :], rc[:, c % 2, D:], rs[:, c % 2, D:],
                                       ALU.add).then_inc(rot_done, 1)

        @block.scalar
        def _(act):
            with act.Fori(0, steps) as j:
                for c in range(CH):
                    n = CH * j + c
                    act.wait_ge(xT_ready, ONE + n + 1)
                    act.wait_ge(proj_ready, ONE + CH * j)
                    act.activation(xh[c][:].rearrange("p k n -> p (k n)"), xT[c % 2][:], ACT.Copy).then_inc(xh_ready, 1)
                for c in range(CH):
                    n = CH * j + c
                    act.wait_ge(rot_sin, ONE + 2 * n + 2)
                    act.activation(t["v"][:, n, :, 0:HD],
                                   proj[c % 2][:, D + KVW:QKV].rearrange("p (g d) -> p g d", g=G),
                                   ACT.Copy).then_inc(v_done, 1)

        @block.vector
        def _(dve):
            dve.memset(t["v"][:], 1.0).then_inc(v_done, 1)
            with dve.Fori(0, steps) as j:
                for c in range(CH):
                    dve.wait_ge(x_loaded[c], ONE + 16 * j + 16)
                    dve.bn_stats(st6[:, c, :], x[:, c, :]).then_inc(stats, 1)
                for c in range(CH):
                    n = CH * j + c
                    wait_apart(dve, stats, n + 1, passed_dve)
                    dve.bn_aggr(mv[:, c, :], st6[:, c, :]).then_inc(moments, 1)
                for c in range(CH):
                    n = CH * j + c
                    dve.wait_ge(rstd_ready, ONE + n + 1)
                    dve.wait_ge(xT_ready, ONE + CH * j)
                    dve.tensor_scalar(xn[:, c, :], x[:, c, :], mv[:, c, 0:1], rstd[:, c:c + 1],
                                      ALU.subtract, ALU.mult).then_inc(xn_ready, 1)
                for c in range(CH):
                    n = CH * j + c
                    dve.wait_ge(xh_ready, ONE + n + 1)
                    dve.tensor_tensor(xl[c][:].rearrange("p k n -> p (k n)"), xT[c % 2][:],
                                      f32(xh[c][:]).rearrange("p k n -> p (k n)"), ALU.subtract).then_inc(xl_ready, 1)
                for c in range(CH):
                    n = CH * j + c
                    qk = proj[c % 2][:, 0:D + KVW].rearrange("p (h d) -> p h d", d=HD)
                    cs = rc[:, c % 2, :].rearrange("p (h d) -> p h d", d=HD)
                    sn = rs[:, c % 2, :].rearrange("p (h d) -> p h d", d=HD)
                    cos = t["cos"][:, c % TPB, :].unsqueeze(1).to_broadcast([P, H + G, HD])
                    dve.wait_ge(proj_ready, ONE + n + 1)
                    if c >= 2:
                        dve.wait_ge(rot_done, ONE + 2 * (n - 1))
                    dve.tensor_tensor(cs, qk, cos, ALU.mult).then_inc(rot_cos, 1)
                    for half in range(2):
                        a, b = half * HD // 2, (1 - half) * HD // 2
                        sin = t["sin"][:, c % TPB, a:a + HD // 2].unsqueeze(1).to_broadcast([P, H + G, HD // 2])
                        dve.tensor_tensor(sn[:, :, a:a + HD // 2], qk[:, :, b:b + HD // 2], sin,
                                          ALU.mult).then_inc(rot_sin, 1)

        @block.tensor
        def _(pe):
            with pe.Fori(0, steps) as j:
                for c in range(CH):
                    n = CH * j + c
                    pe.wait_ge(xn_ready, ONE + n + 1)
                    if c >= 2:
                        pe.wait_ge(xl_ready, ONE + n - 1)
                    for k in range(KD):
                        m = pe.transpose(xT[c % 2][:, k * P:(k + 1) * P], xn[:, c, k * P:(k + 1) * P], t["ident"][:])
                    m.then_inc(xT_ready, 1)
                for c in range(CH):
                    n = CH * j + c
                    pe.wait_ge(xl_ready, ONE + n + 1)
                    if c >= 2:
                        pe.wait_ge(v_done, ONE + n)
                    else:
                        pe.wait_ge(v_done, ONE + CH * j + 1)
                    for half in range(2):
                        a, b = half * 512, min(QKV, half * 512 + 512)
                        for k in range(KD):
                            m = split_passes(pe, proj[c % 2][:, a:b], (xh[c][:, k, :], xl[c][:, k, :]),
                                             [w[:, k, a:b] for w in t["wqkv"]], k == 0, k == KD - 1)
                    m.then_inc(proj_ready, 1)


def stage_attention(nc, t):
    with Scope(nc) as s:
        R = 2
        stk = [s.sb(f"at_stk{r}", [P, TPB, 3 * P], F32R) for r in range(R)]
        qT = [s.sb(f"at_qT{r}", [P, 2, S], F32R) for r in range(R)]
        kz = [s.sb(f"at_kz{r}", [P, 2, S], F32R) for r in range(R)]
        prob = [s.sb(f"at_prob{r}", [P, 3, 512]) for r in range(R)]
        pT = [s.sb(f"at_pT{r}", [P, 3, 512]) for r in range(R)]
        mx = s.sb("at_mx", [P, R, 8])
        nb = s.sb("at_nb", [P, R, 8])
        rinv = s.sb("at_rinv", [P, R, 8])
        sc = [s.ps(f"at_scores{a}", [P, 512]) for a in range(3)]
        tp = [s.ps(f"at_tp{r}", [P, 512]) for r in range(2)]
        ob = s.ps("at_out", [P, 512])
        sk = s.ps("at_stkT", [P, 2, 512])
        names = ("q_hi", "stack_ready", "stackT_ready", "kz_zeroed", "qT_ready", "kz_ready", "scores_ready",
                 "max_ready", "bias_ready", "probs_ready", "probsT_ready", "pT_a", "pT_b", "out_ready", "rinv_ready",
                 "attn_done")
        sm = {n: s.sem("at_" + n) for n in names}
        passed_pool = s.sem("at_passed_pool")
        s.credit()
        block = s.ctx.enter_context(nc.Block())
        o4 = ob[:, 0:TPB * REP * VW].rearrange("p (q h d) -> p q h d", q=TPB, h=REP)

        @block.gpsimd
        def _(pool):
            with pool.Fori(0, B) as b:
                for g in range(G):
                    n = G * b + g
                    r = g % R
                    if g >= R:
                        wait_apart(pool, sm["stackT_ready"], n - 1, passed_pool)
                    else:
                        wait_apart(pool, sm["stackT_ready"], G * b, passed_pool)
                    for u in range(TPB):
                        q = t["act"][:, TPB * b + u, g * REP * HD:(g + 1) * REP * HD].rearrange("p (h d) -> p h d", d=HD)
                        k = t["k"][:, TPB * b + u, g * HD:(g + 1) * HD]
                        qs = stk[r][:, u, 0:2 * P].rearrange("p (h c l d) -> p h c l d", h=REP, c=2, l=2)
                        ks = stk[r][:, u, 2 * P:3 * P].rearrange("p (m l c d) -> p m l c d", m=2, l=2, c=2)
                        q4 = q.unsqueeze(2).to_broadcast([P, REP, 2, HD])
                        k4 = k.unsqueeze(1).unsqueeze(1).to_broadcast([P, 2, 2, HD])
                        pool.tensor_copy(qs[:, :, :, 0, :], q4).then_inc(sm["q_hi"], 1)
                        pool.tensor_copy(ks[:, :, 0, :, :], k4).then_inc(sm["q_hi"], 1)
                        wait_apart(pool, sm["q_hi"], 4 * n + 2 * u + 1, passed_pool)
                        pool.tensor_tensor(qs[:, :, :, 1, :], q4, f32(qs[:, :, :, 0, :]),
                                           ALU.subtract).then_inc(sm["stack_ready"], 1)
                        wait_apart(pool, sm["q_hi"], 4 * n + 2 * u + 2, passed_pool)
                        pool.tensor_tensor(ks[:, :, 1, :, :], k4, f32(ks[:, :, 0, :, :]),
                                           ALU.subtract).then_inc(sm["stack_ready"], 1)

        def slots(eng, slot, first):
            first()
            slot(0, 0, True, True, False)
            with eng.Fori(0, B - 1) as b:
                for k in range(1, G + 1):
                    slot(b + k // G, k % G, True, True, True)
            for k in range(1, G + 1):
                slot(B - 1, k, k < G - 1, k < G, True)

        @block.scalar
        def _(act):
            def operand(n, r):
                act.wait_ge(sm["stackT_ready"], ONE + n + 1)
                act.activation(qT[r][:].rearrange("p m (u n) -> p u m n", u=TPB),
                               sk[:, :, 0:2 * P].rearrange("p u (m n) -> p u m n", m=2), ACT.Copy)\
                    .then_inc(sm["qT_ready"], 1)

            def exps(n, r, a):
                act.wait_ge(sm["bias_ready"], ONE + 3 * n + a + 1)
                w = P if a == 0 else S
                for h in range(512 // w):
                    hb = h if a == 0 else REP + 2 * (a - 1) + h
                    m = act.activation(prob[r][:, a, h * w:(h + 1) * w], sc[a][:, h * w:(h + 1) * w], ACT.Exp,
                                       bias=nb[:, r, hb:hb + 1], scale=HD ** -0.5)
                m.then_inc(sm["probs_ready"], 1)

            def turn(n, r):
                act.wait_ge(sm["probsT_ready"], ONE + 3 * n + 2)
                act.activation(pT[r][:, 1, :], tp[1][:], ACT.Copy).then_inc(sm["pT_b"], 1)

            def slot(b, g, has_next, has_this, has_prev):
                n = G * b + g
                if has_prev:
                    turn(n - 1, (g - 1) % R)
                if has_this:
                    exps(n, g % R, 0)
                    exps(n, g % R, 1)
                if has_next:
                    operand(n + 1, (g + 1) % R)
                if has_this:
                    exps(n, g % R, 2)

            slots(act, slot, lambda: operand(0, 0))

        @block.vector
        def _(dve):
            def operand(n, r):
                dve.wait_ge(sm["qT_ready"], ONE + n + 1)
                for m in range(2):
                    i = dve.tensor_copy(kz[r][64 * m:64 * m + 64, m, :].rearrange("p (u n) -> p u n", u=TPB),
                                        sk[64 * m:64 * m + 64, :, 2 * P:3 * P])
                i.then_inc(sm["kz_ready"], 1)

            def maxima(n, r, a):
                dve.wait_ge(sm["scores_ready"], ONE + 3 * n + a + 1)
                lo, hi = (0, REP) if a == 0 else (REP + 2 * (a - 1), REP + 2 * a)
                dve.tensor_reduce(mx[:, r, lo:hi], sc[a][:].rearrange("p (h k) -> p h k", h=hi - lo), AX.X, ALU.max)\
                    .then_inc(sm["max_ready"], 1)
                dve.wait_ge(sm["max_ready"], ONE + 3 * n + a + 1)
                dve.tensor_scalar(nb[:, r, lo:hi], mx[:, r, lo:hi], -HD ** -0.5, None, ALU.mult)\
                    .then_inc(sm["bias_ready"], 1)

            def turn(n, r, c):
                dve.wait_ge(sm["probsT_ready"], ONE + 3 * n + c + 1)
                dve.tensor_copy(pT[r][:, c, :], tp[0][:]).then_inc(sm["pT_a"], 1)

            def finish(n, r, b, g):
                dve.wait_ge(sm["out_ready"], ONE + n + 1)
                dve.reciprocal(rinv[:, r, :].rearrange("p (q h) -> p q h", q=TPB), o4[:, :, :, HD])\
                    .then_inc(sm["rinv_ready"], 1)
                dve.wait_ge(sm["rinv_ready"], ONE + n + 1)
                w = rinv[:, r, :].rearrange("p (q h) -> p q h", q=TPB).unsqueeze(3).to_broadcast([P, TPB, REP, HD])
                i = dve.tensor_tensor(
                    t["act"][:, bass.ds(TPB * b, TPB), g * REP * HD:(g + 1) * REP * HD].rearrange("p u (h d) -> p u h d", d=HD),
                    o4[:, :, :, 0:HD], w, ALU.mult)
                i.then_inc(sm["attn_done"], 1)

            def slot(b, g, has_next, has_this, has_prev):
                n = G * b + g
                r, q = g % R, (g - 1) % R
                if has_prev:
                    turn(n - 1, q, 0)
                if has_this:
                    maxima(n, r, 0)
                if has_prev:
                    turn(n - 1, q, 2)
                if has_this:
                    maxima(n, r, 1)
                    maxima(n, r, 2)
                if has_next:
                    operand(n + 1, (g + 1) % R)
                if has_prev:
                    pb, pg = (b, g - 1) if g else (b - 1, G - 1)
                    finish(n - 1, q, pb, pg)

            def first():
                for r in range(R):
                    i = dve.memset(f32(kz[r][:]), 0.0)
                i.then_inc(sm["kz_zeroed"], 1)
                dve.wait_ge(sm["kz_zeroed"], ONE + 1)
                operand(0, 0)

            slots(dve, slot, first)

        @block.tensor
        def _(pe):
            def operand(n, r):
                pe.wait_ge(sm["stack_ready"], ONE + 4 * n + 4)
                wait(pe, sm["kz_ready"], n)
                for u in range(TPB):
                    for a in range(3):
                        m = pe.transpose(sk[:, u, a * P:(a + 1) * P], f32(stk[r][:, u, a * P:(a + 1) * P]), t["ident"][:])
                m.then_inc(sm["stackT_ready"], 1)

            def scores(n, r, a):
                if a == 0:
                    pe.wait_ge(sm["kz_ready"], ONE + n + 1)
                    heads, width = REP, P
                else:
                    heads, width = 2, S
                wait(pe, sm["probs_ready"], 3 * n - 2 + a)
                bank = sc[a][:].rearrange("p (h k) -> p h k", h=heads)
                pe.matmul(bank[:, :, width - P:width], t["identb"][:],
                          t["mask"][:].unsqueeze(1).to_broadcast([P, heads, P]), start=True, stop=False,
                          skip_group_check=True)
                for pair in ((0, 1) if a == 0 else (a - 1,)):
                    out = sc[a][:, pair * S:(pair + 1) * S] if a == 0 else sc[a][:]
                    lhs = qT[r][:, pair, 0:P] if a == 0 else qT[r][:, pair, P:S]
                    m = pe.matmul(out.rearrange("p (z k) -> p z k", z=2), lhs, kz[r][:, :, 0:width],
                                  start=False, stop=True, skip_group_check=True)
                m.then_inc(sm["scores_ready"], 1)

            def turn(n, r, c):
                pe.wait_ge(sm["probs_ready"], ONE + 3 * n + c + 1)
                if c == 1:
                    wait(pe, sm["pT_b"], n)
                else:
                    wait(pe, sm["pT_a"], 2 * n + c // 2)
                for k in range(4):
                    m = pe.transpose(tp[c % 2][:, k * P:(k + 1) * P], prob[r][:, c, k * P:(k + 1) * P], t["ident"][:])
                m.then_inc(sm["probsT_ready"], 1)

            def values(n, r, b, g):
                pe.wait_ge(sm["pT_a"], ONE + 2 * n + 2)
                pe.wait_ge(sm["pT_b"], ONE + n + 1)
                wait(pe, sm["attn_done"], n)
                v = [t["v"][:, TPB * b + u, g, :] for u in range(TPB)]
                for h in range(REP):
                    pe.matmul(o4[:, 0, h, :], pT[r][:, 0, h * P:(h + 1) * P], v[0], start=True, stop=True)
                    for u in range(TPB):
                        k = (2 * (h % 2) + u) * P
                        m = pe.matmul(o4[:, 1, h, :], pT[r][:, 1 + h // 2, k:k + P], v[u], start=u == 0,
                                      stop=u == TPB - 1)
                m.then_inc(sm["out_ready"], 1)

            def slot(b, g, has_next, has_this, has_prev):
                n = G * b + g
                if has_prev:
                    turn(n - 1, (g - 1) % R, 0)
                    turn(n - 1, (g - 1) % R, 1)
                if has_this:
                    scores(n, g % R, 0)
                if has_prev:
                    turn(n - 1, (g - 1) % R, 2)
                if has_this:
                    scores(n, g % R, 1)
                if has_next:
                    operand(n + 1, (g + 1) % R)
                if has_this:
                    scores(n, g % R, 2)
                if has_prev:
                    pb, pg = (b, g - 1) if g else (b - 1, G - 1)
                    values(n - 1, (g - 1) % R, pb, pg)

            slots(pe, slot, lambda: operand(0, 0))


def stage_out_proj(nc, io, t):
    with Scope(nc) as s:
        x = s.sb("op_x", [P, CH, D])
        at = [s.sb(f"op_at{c}", [P, D]) for c in range(CH)]
        ah = [s.sb(f"op_ah{c}", [P, KD, P], F32R) for c in range(CH)]
        al = [s.sb(f"op_al{c}", [P, KD, P], F32R) for c in range(CH)]
        st6 = s.sb("op_st6", [P, CH, 6])
        mv = s.sb("op_mv", [P, CH, 2])
        ve = s.sb("op_ve", [P, CH])
        aT = [s.ps(f"op_aT{c}", [P, D]) for c in range(CH)]
        y = [s.ps(f"op_y{c}", [P, D]) for c in range(CH)]
        x_loaded = [s.sem(f"op_x_loaded{c}") for c in range(CH)]
        names = ("copied", "turned", "hi", "lo", "y_ready", "x1_done", "stats", "moments", "eps", "rstd_ready",
                 "mean_kept", "passed_pool", "passed_dve")
        sm = {n: s.sem("op_" + n) for n in names}
        s.credit()
        block = s.ctx.enter_context(nc.Block())
        steps = NT // CH

        @block.sync
        def _(sp):
            with sp.Fori(0, steps) as j:
                for c in range(CH):
                    sp.wait_ge(sm["x1_done"], ONE + CH * j)
                    sp.dma_start(x[:, c, :], io["x_tiles"][CH * j + c]).then_inc(x_loaded[c], 16)

        @block.gpsimd
        def _(pool):
            with pool.Fori(0, steps) as j:
                for c in range(CH):
                    n = CH * j + c
                    wait_apart(pool, sm["turned"], CH * j, sm["passed_pool"])
                    pool.tensor_copy(at[c][:], t["act"][:, n, :]).then_inc(sm["copied"], 1)
                for c in range(CH):
                    n = CH * j + c
                    pool.wait_ge(sm["moments"], ONE + n + 1)
                    pool.tensor_tensor(ve[:, c:c + 1], mv[:, c, 1:2], t["eps"][:], ALU.add).then_inc(sm["eps"], 1)
                    wait_apart(pool, sm["eps"], n + 1, sm["passed_pool"])
                    pool.tensor_tensor(t["rstd1"][:, n, :], ve[:, c:c + 1], t["half"][:],
                                       ALU.pow).then_inc(sm["rstd_ready"], 1)
                    pool.tensor_copy(t["mean1"][:, n, :], mv[:, c, 0:1]).then_inc(sm["mean_kept"], 1)

        @block.scalar
        def _(act):
            with act.Fori(0, steps) as j:
                for c in range(CH):
                    n = CH * j + c
                    act.wait_ge(sm["turned"], ONE + n + 1)
                    act.wait_ge(sm["y_ready"], ONE + CH * j)
                    act.activation(ah[c][:].rearrange("p k n -> p (k n)"), aT[c][:], ACT.Copy).then_inc(sm["hi"], 1)

        @block.vector
        def _(dve):
            with dve.Fori(0, steps) as j:
                for c in range(CH):
                    n = CH * j + c
                    dve.wait_ge(sm["hi"], ONE + n + 1)
                    dve.tensor_tensor(al[c][:].rearrange("p k n -> p (k n)"), aT[c][:],
                                      f32(ah[c][:]).rearrange("p k n -> p (k n)"), ALU.subtract).then_inc(sm["lo"], 1)
                for c in range(CH):
                    n = CH * j + c
                    dve.wait_ge(x_loaded[c], ONE + 16 * j + 16)
                    wait_apart(dve, sm["y_ready"], n + 1, sm["passed_dve"])
                    dve.tensor_tensor(t["act"][:, n, :], y[c][:], x[:, c, :], ALU.add).then_inc(sm["x1_done"], 1)
                for c in range(CH):
                    n = CH * j + c
                    wait_apart(dve, sm["x1_done"], n + 1, sm["passed_dve"])
                    dve.bn_stats(st6[:, c, :], t["act"][:, n, :]).then_inc(sm["stats"], 1)
                for c in range(CH):
                    n = CH * j + c
                    dve.wait_ge(sm["mean_kept"], ONE + CH * j)
                    wait_apart(dve, sm["stats"], n + 1, sm["passed_dve"])
                    dve.bn_aggr(mv[:, c, :], st6[:, c, :]).then_inc(sm["moments"], 1)

        @block.tensor
        def _(pe):
            with pe.Fori(0, steps) as j:
                for c in range(CH):
                    n = CH * j + c
                    pe.wait_ge(sm["copied"], ONE + n + 1)
                    pe.wait_ge(sm["lo"], ONE + CH * j)
                    for k in range(KD):
                        m = pe.transpose(aT[c][:, k * P:(k + 1) * P], at[c][:, k * P:(k + 1) * P], t["ident"][:])
                    m.then_inc(sm["turned"], 1)
                for c in range(CH):
                    n = CH * j + c
                    pe.wait_ge(sm["lo"], ONE + n + 1)
                    pe.wait_ge(sm["x1_done"], ONE + CH * j)
                    for k in range(KD):
                        m = split_passes(pe, y[c][:], (ah[c][:, k, :], al[c][:, k, :]),
                                         [w[:, k, :] for w in t["wo"]], k == 0, k == KD - 1)
                    m.then_inc(sm["y_ready"], 1)


def stage_cross(nc, io, t):
    CB = 2
    NTT = D // P
    SCORE_BANK = (3, 0, 1, 2)
    with Scope(nc) as s:
        ctx_in = [s.sb(f"cx_ctx{c}", [P, TPB, D]) for c in range(CB)]
        res = [s.sb(f"cx_res{c}", [P, TPB, D]) for c in range(CB)]
        xin = [s.sb(f"cx_xin{c}", [P, TPB, D]) for c in range(CB)]
        R1 = [s.sb(f"cx_r1_{c}", [P, 8, D], F32R) for c in range(CB)]
        R2 = [s.sb(f"cx_r2_{c}", [P, 6, D], F32R) for c in range(CB)]
        R3 = [s.sb(f"cx_r3_{c}", [P, 4, D], F32R) for c in range(CB)]
        prob = [s.sb(f"cx_prob{c}", [P, NTT, D]) for c in range(CB)]
        lgT = [s.sb(f"cx_lgT{c}", [E, TPB, P]) for c in range(CB)]
        bank = [[s.ps(f"cx_bank{c}_{i}", [P, 512]) for i in range(4)] for c in range(CB)]
        st6 = s.sb("cx_st6", [P, CB, TPB, 6])
        mv = s.sb("cx_mv", [P, CB, TPB, 2])
        ve = s.sb("cx_ve", [P, CB, TPB])
        rstd = s.sb("cx_rstd", [P, CB, TPB])
        mx = s.sb("cx_mx", [P, CB, NTT])
        nmx = s.sb("cx_nmx", [P, CB, NTT])
        rsum = s.sb("cx_rsum", [P, CB, NTT])
        rinv = s.sb("cx_rinv", [P, CB, NTT])
        pst = s.sb("cx_pst", [P, CB, 6])
        pmv = s.sb("cx_pmv", [P, CB, 2])
        psq = s.sb("cx_psq", [P, CB])
        gmv = s.sb("cx_gmv", [P, CB, 2])
        gsq = s.sb("cx_gsq", [P, CB])
        gve = s.sb("cx_gve", [P, CB])
        gvar = s.sb("cx_gvar", [P, CB])
        grstd = s.sb("cx_grstd", [P, CB])
        ctx_loaded = [s.sem(f"ctx_loaded{c}") for c in range(CB)]
        stored = [s.sem(f"cx_stored{c}") for c in range(CB)]
        names = ("xin", "ctx_hi", "ctx_lo", "ctx_res", "xin_hi", "xin_lo", "theta", "phi", "g", "theta_hi", "theta_lo",
                 "phi_hi", "phi_lo", "g_hi", "g_lo", "scores", "max", "neg_max", "exp", "rinv", "norm", "turned",
                 "pT_hi", "pT_lo", "tx", "tx_kept", "row_stats", "row_moments", "row_sq", "row_m2", "all_moments",
                 "gmv", "gsq", "gvar", "gve", "grstd", "centred", "scaled", "h_hi", "h_lo", "out", "x2", "stats",
                 "moments", "eps", "rstd", "xn3", "x3T", "x3_hi", "x3_lo", "lgT", "lgT_kept", "logits",
                 "logits_kept", "passed_dve", "passed_pe", "passed_pool")
        sm = {n: s.sem("cx_" + n) for n in names}
        s.credit()
        block = s.ctx.enter_context(nc.Block())
        steps = B // CB
        chains = range(CB)
        r2_of = {"theta": 0, "phi": 2, "g": 4}
        bank_of = {"theta": 2, "phi": 3, "g": 2}
        bias_of = {"theta": "theta_b", "phi": "phi_b", "g": None}

        def turns(eng, front, middle, tail):
            front(0)
            with eng.Fori(0, steps - 1) as j:
                middle(j)
                tail(j, True)
            middle(steps - 1)
            tail(steps - 1, False)

        @block.sync
        def _(sp):
            def load(j):
                for c in chains:
                    wait(sp, sm["ctx_res"], CB * j + c + 1 - CB)
                    sp.dma_start(ctx_in[c][:], io["ctx_tiles"][CB * j + c]).then_inc(ctx_loaded[c], 16)

            def store(j):
                for c in chains:
                    n = CB * j + c
                    sp.wait_ge(sm["x2"], ONE + TPB * (n + 1))
                    sp.dma_start(io["x2_tiles"][n], res[c][:]).then_inc(stored[c], 16)
                for c in chains:
                    n = CB * j + c
                    sp.wait_ge(sm["xn3"], ONE + TPB * (n + 1))
                    sp.dma_start(io["xn3_tiles"][n], prob[c][:, 0:TPB, :]).then_inc(stored[c], 16)

            def tail(j, ahead):
                if ahead:
                    load(j + 1)
                store(j)

            turns(sp, load, lambda j: None, tail)
            for c in chains:
                sp.wait_ge(stored[c], ONE + 32 * steps)

        @block.gpsimd
        def _(pool):
            def front(j):
                for c in chains:
                    n = CB * j + c
                    wait_apart(pool, sm["ctx_hi"], n + 1, sm["passed_pool"])
                    pool.tensor_tensor(R1[c][:, 2:4, :], ctx_in[c][:], f32(R1[c][:, 0:2, :]),
                                       ALU.subtract).then_inc(sm["ctx_lo"], 1)

            def middle(j):
                for c in chains:
                    n = CB * j + c
                    wait_apart(pool, stored[c], 32 * j, sm["passed_pool"])
                    pool.tensor_tensor(res[c][:], ctx_in[c][:], t["act"][:, bass.ds(TPB * n, TPB), :],
                                       ALU.add).then_inc(sm["ctx_res"], 1)

            def tail(j, ahead):
                for c in chains:
                    n = CB * j + c
                    pool.wait_ge(sm["gvar"], ONE + n + 1)
                    pool.tensor_tensor(gve[:, c:c + 1], gvar[:, c:c + 1], t["eps"][:], ALU.add).then_inc(sm["gve"], 1)
                    pool.wait_ge(sm["gve"], ONE + n + 1)
                    pool.tensor_tensor(grstd[:, c:c + 1], gve[:, c:c + 1], t["half"][:], ALU.pow)\
                        .then_inc(sm["grstd"], 1)
                if ahead:
                    front(j + 1)
                for c in chains:
                    n = CB * j + c
                    pool.wait_ge(sm["moments"], ONE + TPB * (n + 1))
                    pool.tensor_tensor(ve[:, c, :], mv[:, c, :, 1], t["eps"][:].to_broadcast([P, TPB]),
                                       ALU.add).then_inc(sm["eps"], 1)
                    pool.wait_ge(sm["eps"], ONE + n + 1)
                    pool.tensor_tensor(rstd[:, c, :], ve[:, c, :], t["half"][:].to_broadcast([P, TPB]),
                                       ALU.pow).then_inc(sm["rstd"], 1)

            turns(pool, front, middle, tail)

        @block.scalar
        def _(act):
            def ctx_hi(j):
                for c in chains:
                    n = CB * j + c
                    act.wait_ge(ctx_loaded[c], ONE + 16 * j + 16)
                    wait(act, sm["tx"], n + 1 - CB)
                    act.activation(R1[c][:, 0:2, :], ctx_in[c][:], ACT.Copy).then_inc(sm["ctx_hi"], 1)

            def xin_hi(j):
                for c in chains:
                    n = CB * j + c
                    act.wait_ge(sm["xin"], ONE + TPB * (n + 1))
                    wait(act, sm["tx"], n + 1 - CB)
                    act.activation(R1[c][:, 4:6, :], xin[c][:], ACT.Copy).then_inc(sm["xin_hi"], 1)

            def latent_hi(j, name):
                r2, at, bias = r2_of[name], bank_of[name], bias_of[name]
                for c in chains:
                    n = CB * j + c
                    act.wait_ge(sm[name], ONE + n + 1)
                    if bias:
                        act.activation(R2[c][:, r2, :], bank[c][at][:], ACT.Identity, bias=t[bias][:])\
                            .then_inc(sm[name + "_hi"], 1)
                    else:
                        act.activation(R2[c][:, r2, :], bank[c][at][:], ACT.Copy).then_inc(sm[name + "_hi"], 1)

            def front(j):
                ctx_hi(j)
                xin_hi(j)
                for name in ("theta", "phi", "g"):
                    latent_hi(j, name)

            def middle(j):
                for c in chains:
                    n = CB * j + c
                    act.wait_ge(stored[c], ONE + 32 * j)
                    for i in range(NTT):
                        act.wait_ge(sm["neg_max"], ONE + NTT * n + i + 1)
                        act.activation(prob[c][:, i, :], bank[c][SCORE_BANK[i]][:], ACT.Exp, bias=nmx[:, c, i:i + 1],
                                       accum_out=rsum[:, c, i:i + 1]).then_inc(sm["exp"], 1)
                for c in chains:
                    n = CB * j + c
                    for i in range(NTT):
                        act.wait_ge(sm["turned"], ONE + NTT * n + i + 1)
                        act.activation(R1[c][:, i, :], bank[c][i][:], ACT.Copy).then_inc(sm["pT_hi"], 1)
                for c in chains:
                    n = CB * j + c
                    act.wait_ge(sm["tx"], ONE + n + 1)
                    act.activation(prob[c][:, 0, :], bank[c][0][:], ACT.Identity, bias=t["g_b"][:])\
                        .then_inc(sm["tx_kept"], 1)

            def tail(j, ahead):
                if ahead:
                    ctx_hi(j + 1)
                    xin_hi(j + 1)
                for c in chains:
                    n = CB * j + c
                    act.wait_ge(sm["scaled"], ONE + n + 1)
                    act.activation(R3[c][:, 0, :], prob[c][:, 2, :], ACT.Relu).then_inc(sm["h_hi"], 1)
                if ahead:
                    latent_hi(j + 1, "phi")
                    latent_hi(j + 1, "theta")
                for c in chains:
                    n = CB * j + c
                    for u in range(TPB):
                        act.wait_ge(sm["x3T"], ONE + TPB * n + u + 1)
                        act.activation(R3[c][:, u, :], bank[c][u][:], ACT.Copy).then_inc(sm["x3_hi"], 1)
                if ahead:
                    latent_hi(j + 1, "g")
                for c in chains:
                    n = CB * j + c
                    act.wait_ge(sm["lgT"], ONE + n + 1)
                    act.activation(lgT[c][:], bank[c][0][0:E, 0:TPB * P].rearrange("e (u n) -> e u n", u=TPB),
                                   ACT.Copy).then_inc(sm["lgT_kept"], 1)

            turns(act, front, middle, tail)

        @block.vector
        def _(dve):
            def norm_input(j, c):
                n = CB * j + c
                for u in range(TPB):
                    dve.tensor_scalar(xin[c][:, u, :], t["act"][:, TPB * n + u, :],
                                      t["mean1"][:, TPB * n + u, :], t["rstd1"][:, TPB * n + u, :],
                                      ALU.subtract, ALU.mult).then_inc(sm["xin"], 1)

            def xin_lo(j, c):
                n = CB * j + c
                dve.wait_ge(sm["xin_hi"], ONE + n + 1)
                dve.tensor_tensor(R1[c][:, 6:8, :], xin[c][:], f32(R1[c][:, 4:6, :]), ALU.subtract)\
                    .then_inc(sm["xin_lo"], 1)

            def latent_lo(j, name):
                r2, at, bias = r2_of[name], bank_of[name], bias_of[name]
                for c in chains:
                    n = CB * j + c
                    dve.wait_ge(sm[name + "_hi"], ONE + n + 1)
                    if bias:
                        dve.scalar_tensor_tensor(R2[c][:, r2 + 1, :], bank[c][at][:], t[bias][:],
                                                 f32(R2[c][:, r2, :]), ALU.add, ALU.subtract)\
                            .then_inc(sm[name + "_lo"], 1)
                    else:
                        dve.tensor_tensor(R2[c][:, r2 + 1, :], bank[c][at][:], f32(R2[c][:, r2, :]),
                                          ALU.subtract).then_inc(sm[name + "_lo"], 1)

            def front(j):
                for c in chains:
                    norm_input(j, c)
                for c in chains:
                    xin_lo(j, c)
                for name in ("theta", "phi", "g"):
                    latent_lo(j, name)

            def middle(j):
                for c in chains:
                    n = CB * j + c
                    for i in range(NTT):
                        dve.wait_ge(sm["scores"], ONE + NTT * n + i + 1)
                        dve.tensor_reduce(mx[:, c, i:i + 1], bank[c][SCORE_BANK[i]][:], AX.X, ALU.max)\
                            .then_inc(sm["max"], 1)
                        dve.wait_ge(sm["max"], ONE + NTT * n + i + 1)
                        dve.tensor_scalar(nmx[:, c, i:i + 1], mx[:, c, i:i + 1], -1.0, None, ALU.mult)\
                            .then_inc(sm["neg_max"], 1)
                for c in chains:
                    n = CB * j + c
                    for i in range(NTT):
                        dve.wait_ge(sm["exp"], ONE + NTT * n + i + 1)
                        dve.reciprocal(rinv[:, c, i:i + 1], rsum[:, c, i:i + 1]).then_inc(sm["rinv"], 1)
                        dve.wait_ge(sm["rinv"], ONE + NTT * n + i + 1)
                        dve.tensor_scalar(prob[c][:, i, :], prob[c][:, i, :], rinv[:, c, i:i + 1], None, ALU.mult)\
                            .then_inc(sm["norm"], 1)
                for c in chains:
                    n = CB * j + c
                    for i in range(NTT):
                        dve.wait_ge(sm["pT_hi"], ONE + NTT * n + i + 1)
                        dve.tensor_tensor(R1[c][:, NTT + i, :], bank[c][i][:], f32(R1[c][:, i, :]), ALU.subtract)\
                            .then_inc(sm["pT_lo"], 1)

            def tail(j, ahead):
                if ahead:
                    for c in chains:
                        norm_input(j + 1, c)
                for c in chains:
                    n = CB * j + c
                    dve.wait_ge(sm["tx_kept"], ONE + n + 1)
                    dve.bn_stats(pst[:, c, :], prob[c][:, 0, :]).then_inc(sm["row_stats"], 1)
                    wait_apart(dve, sm["row_stats"], n + 1, sm["passed_dve"])
                    dve.bn_aggr(pmv[:, c, :], pst[:, c, :]).then_inc(sm["row_moments"], 1)
                    dve.wait_ge(sm["row_moments"], ONE + n + 1)
                    dve.tensor_tensor(psq[:, c:c + 1], pmv[:, c, 0:1], pmv[:, c, 0:1], ALU.mult)\
                        .then_inc(sm["row_sq"], 1)
                    dve.wait_ge(sm["row_sq"], ONE + n + 1)
                    dve.tensor_tensor(pmv[:, c, 1:2], pmv[:, c, 1:2], psq[:, c:c + 1], ALU.add)\
                        .then_inc(sm["row_m2"], 1)
                if ahead:
                    for c in chains:
                        xin_lo(j + 1, c)
                for c in chains:
                    n = CB * j + c
                    dve.wait_ge(sm["all_moments"], ONE + n + 1)
                    dve.tensor_copy(gmv[:, c, :], bank[c][1][:, 0:2]).then_inc(sm["gmv"], 1)
                    dve.wait_ge(sm["gmv"], ONE + n + 1)
                    dve.tensor_tensor(gsq[:, c:c + 1], gmv[:, c, 0:1], gmv[:, c, 0:1], ALU.mult)\
                        .then_inc(sm["gsq"], 1)
                    dve.wait_ge(sm["gsq"], ONE + n + 1)
                    dve.tensor_tensor(gvar[:, c:c + 1], gmv[:, c, 1:2], gsq[:, c:c + 1], ALU.subtract)\
                        .then_inc(sm["gvar"], 1)
                for c in chains:
                    n = CB * j + c
                    dve.scalar_tensor_tensor(prob[c][:, 1, :], prob[c][:, 0, :], gmv[:, c, 0:1], t["gamma"][:],
                                             ALU.subtract, ALU.mult).then_inc(sm["centred"], 1)
                for c in chains:
                    n = CB * j + c
                    dve.wait_ge(sm["grstd"], ONE + n + 1)
                    dve.wait_ge(sm["centred"], ONE + n + 1)
                    dve.scalar_tensor_tensor(prob[c][:, 2, :], prob[c][:, 1, :], grstd[:, c:c + 1], t["beta"][:],
                                             ALU.mult, ALU.add).then_inc(sm["scaled"], 1)
                for c in chains:
                    n = CB * j + c
                    dve.wait_ge(sm["h_hi"], ONE + n + 1)
                    dve.scalar_tensor_tensor(R3[c][:, 1, :], prob[c][:, 2, :], 0.0, f32(R3[c][:, 0, :]),
                                             ALU.max, ALU.subtract).then_inc(sm["h_lo"], 1)
                for c in chains:
                    n = CB * j + c
                    dve.wait_ge(sm["ctx_res"], ONE + n + 1)
                    for u in range(TPB):
                        dve.wait_ge(sm["out"], ONE + TPB * n + u + 1)
                        dve.scalar_tensor_tensor(res[c][:, u, :], bank[c][u][:], t["out_b"][:, u:u + 1],
                                                 res[c][:, u, :], ALU.add, ALU.add).then_inc(sm["x2"], 1)
                for c in chains:
                    n = CB * j + c
                    for u in range(TPB):
                        dve.wait_ge(sm["x2"], ONE + TPB * n + u + 1)
                        dve.bn_stats(st6[:, c, u, :], res[c][:, u, :]).then_inc(sm["stats"], 1)
                    wait_apart(dve, sm["stats"], TPB * (n + 1), sm["passed_dve"])
                    for u in range(TPB):
                        dve.bn_aggr(mv[:, c, u, :], st6[:, c, u, :]).then_inc(sm["moments"], 1)
                if ahead:
                    latent_lo(j + 1, "phi")
                for c in chains:
                    n = CB * j + c
                    dve.wait_ge(sm["rstd"], ONE + n + 1)
                    for u in range(TPB):
                        dve.tensor_scalar(prob[c][:, u, :], res[c][:, u, :], mv[:, c, u, 0:1], rstd[:, c, u:u + 1],
                                          ALU.subtract, ALU.mult).then_inc(sm["xn3"], 1)
                if ahead:
                    latent_lo(j + 1, "theta")
                for c in chains:
                    n = CB * j + c
                    for u in range(TPB):
                        dve.wait_ge(sm["x3_hi"], ONE + TPB * n + u + 1)
                        dve.tensor_tensor(R3[c][:, 2 + u, :], bank[c][u][:], f32(R3[c][:, u, :]),
                                          ALU.subtract).then_inc(sm["x3_lo"], 1)
                if ahead:
                    latent_lo(j + 1, "g")
                for c in chains:
                    n = CB * j + c
                    wait_apart(dve, sm["logits"], n + 1, sm["passed_dve"])
                    dve.tensor_copy(t["logits"][:, bass.ds(TPB * n, TPB), :],
                                    bank[c][1][:, 0:TPB * E].rearrange("p (u e) -> p u e", u=TPB))\
                        .then_inc(sm["logits_kept"], 1)

            turns(dve, front, middle, tail)

        @block.tensor
        def _(pe):
            def theta(j):
                for c in chains:
                    n = CB * j + c
                    pe.wait_ge(sm["ctx_lo"], ONE + n + 1)
                    for k in range(TPB):
                        m = split_passes(pe, bank[c][2][:], [w[:, k, :] for w in t["theta_w"]],
                                         (R1[c][:, k, :], R1[c][:, 2 + k, :]), k == 0, k == TPB - 1)
                    m.then_inc(sm["theta"], 1)

            def phi(j):
                for c in chains:
                    n = CB * j + c
                    pe.wait_ge(sm["xin_lo"], ONE + n + 1)
                    for k in range(TPB):
                        m = split_passes(pe, bank[c][3][:], [w[:, k, :] for w in t["phi_w"]],
                                         (R1[c][:, 4 + k, :], R1[c][:, 6 + k, :]), k == 0, k == TPB - 1)
                    m.then_inc(sm["phi"], 1)

            def g(j):
                for c in chains:
                    n = CB * j + c
                    pe.wait_ge(sm["theta_lo"], ONE + n + 1)
                    for i in range(NTT):
                        for k in range(TPB):
                            m = split_passes(pe, bank[c][2][:, i * P:(i + 1) * P],
                                             (R1[c][:, 4 + k, i * P:(i + 1) * P], R1[c][:, 6 + k, i * P:(i + 1) * P]),
                                             [w[:, k, :] for w in t["g_w"]], k == 0, k == TPB - 1)
                    m.then_inc(sm["g"], 1)

            def front(j):
                theta(j)
                phi(j)
                g(j)

            def middle(j):
                for c in chains:
                    n = CB * j + c
                    pe.wait_ge(sm["phi_lo"], ONE + n + 1)
                    for i in range(NTT):
                        if i == 1:
                            wait(pe, sm["lgT_kept"], n + 1 - CB)
                            wait(pe, sm["logits_kept"], n + 1 - CB)
                        if i == 3:
                            pe.wait_ge(sm["g_lo"], ONE + n + 1)
                        m = split_passes(pe, bank[c][SCORE_BANK[i]][:],
                                         (R2[c][:, 0, i * P:(i + 1) * P], R2[c][:, 1, i * P:(i + 1) * P]),
                                         (R2[c][:, 2, :], R2[c][:, 3, :]))
                        m.then_inc(sm["scores"], 1)
                for c in chains:
                    n = CB * j + c
                    for i in range(NTT):
                        pe.wait_ge(sm["norm"], ONE + NTT * (n + 1))
                        for k in range(NTT):
                            m = pe.transpose(bank[c][i][:, k * P:(k + 1) * P], prob[c][:, k, i * P:(i + 1) * P],
                                             t["ident"][:])
                        m.then_inc(sm["turned"], 1)
                for c in chains:
                    n = CB * j + c
                    for i in range(NTT):
                        pe.wait_ge(sm["pT_lo"], ONE + NTT * n + i + 1)
                        m = split_passes(pe, bank[c][0][:],
                                         (R2[c][:, 4, i * P:(i + 1) * P], R2[c][:, 5, i * P:(i + 1) * P]),
                                         (R1[c][:, i, :], R1[c][:, NTT + i, :]), i == 0, i == NTT - 1)
                    m.then_inc(sm["tx"], 1)

            def tail(j, ahead):
                for c in chains:
                    n = CB * j + c
                    pe.wait_ge(sm["row_m2"], ONE + n + 1)
                    pe.matmul(bank[c][1][:, 0:2], t["avg"][:], pmv[:, c, :], start=True, stop=True)\
                        .then_inc(sm["all_moments"], 1)
                if ahead:
                    phi(j + 1)
                for c in chains:
                    n = CB * j + c
                    pe.wait_ge(sm["h_lo"], ONE + n + 1)
                    for u in range(TPB):
                        split_passes(pe, bank[c][u][:], [w[:, u * P:(u + 1) * P] for w in t["out_w"]],
                                     (R3[c][:, 0, :], R3[c][:, 1, :])).then_inc(sm["out"], 1)
                if ahead:
                    theta(j + 1)
                    g(j + 1)
                for c in chains:
                    n = CB * j + c
                    for u in range(TPB):
                        pe.wait_ge(sm["xn3"], ONE + TPB * n + u + 1)
                        for k in range(KD):
                            m = pe.transpose(bank[c][u][:, k * P:(k + 1) * P], prob[c][:, u, k * P:(k + 1) * P],
                                             t["ident"][:])
                        m.then_inc(sm["x3T"], 1)
                for c in chains:
                    n = CB * j + c
                    pe.wait_ge(sm["x3_lo"], ONE + TPB * (n + 1))
                    for k in range(KD):
                        m = split_passes(pe, bank[c][0][0:E, 0:TPB * P].rearrange("e (u n) -> e u n", u=TPB),
                                         [w[:, k, :] for w in t["router_w"]],
                                         [R3[c][:, q:q + TPB, k * P:(k + 1) * P] for q in (0, 2)], k == 0, k == KD - 1)
                    m.then_inc(sm["lgT"], 1)
                for c in chains:
                    n = CB * j + c
                    wait_apart(pe, sm["lgT_kept"], n + 1, sm["passed_pe"])
                    for u in range(TPB):
                        m = pe.transpose(bank[c][1][:, u * E:(u + 1) * E], lgT[c][:, u, :], t["ident"][0:E, 0:E])
                    m.then_inc(sm["logits"], 1)

            turns(pe, front, middle, tail)


def stage_route(nc, io, t):
    with Scope(nc) as s:
        W = [P, NT, E]
        lg = t["logits"]
        red = s.sb("rt_red", [P, 4, NT])
        ex = s.sb("rt_ex", W)
        prob = s.sb("rt_prob", W)
        eq = s.sb("rt_eq", W)
        hot = [s.sb(f"rt_hot{k}", W) for k in range(TOPK)]
        chosen = s.sb("rt_chosen", W)
        scan = [s.sb(f"rt_scan{k}", W) for k in range(2)]
        total = s.sb("rt_total", W)
        place = s.sb("rt_place", W)
        kept = s.sb("rt_kept", W)
        tmp = s.sb("rt_tmp", W)
        ei = s.sb("rt_ei", [P, E], I32)
        ef = s.sb("rt_ef", [P, E])
        em = s.sb("rt_em", [P, E])
        ec = s.sb("rt_ec", [P, E])
        token = s.sb("rt_token", [P, NT], I32)
        tokenf = s.sb("rt_tokenf", [P, NT])
        dump = s.sb("rt_dump", [P, NT])
        has = s.sb("rt_has", [P, NT])
        slot = s.sb("rt_slot", [P, NT])
        scat = s.sb("rt_scat", [P, TOPK, NT], I32)
        zero = s.sb("rt_zero", [ST, P], I32)
        tab = s.sb("rt_tab", [ST, P], I32)
        tabf = s.sb("rt_tabf", [ST, P])
        pp = s.ps("rt_pp", [P, 512])
        pt = s.ps("rt_pt", [P, 512])
        names = ("iota", "zeroed", "cleared", "exp_in", "exp", "dve", "counts", "scatter_idx",
                 "table_loaded", "table_f", "table_T", "idx")
        sm = {n: s.sem("rt_" + n) for n in names}
        scattered = s.zero_sem("rt_scattered")
        s.credit()
        block = s.ctx.enter_context(nc.Block())

        @block.sync
        def _(sp):
            sp.wait_ge(sm["zeroed"], ONE + 1)
            sp.dma_start(io["table"][0:SLOTS, :].rearrange("(a b) o -> a (b o)", b=P), zero[:])\
                .then_inc(sm["cleared"], 16)
            sp.wait_ge(scattered, 16 * TOPK * NT)
            sp.dma_start(tab[:], io["table"][0:SLOTS, :].rearrange("(a b) o -> a (b o)", b=P))\
                .then_inc(sm["table_loaded"], 16)
            sp.wait_ge(sm["table_loaded"], ONE + 16)

        @block.gpsimd
        def _(pool):
            pool.iota(ei[:], pattern=[[1, E]], base=0, channel_multiplier=0).then_inc(sm["iota"], 1)
            pool.iota(token[:], pattern=[[P, NT]], base=0, channel_multiplier=1).then_inc(sm["iota"], 1)
            pool.memset(zero[:], 0).then_inc(sm["zeroed"], 1)
            pool.wait_ge(sm["cleared"], ONE + 16)
            for k in range(TOPK):
                pool.wait_ge(sm["scatter_idx"], ONE + k + 1)
                for n in range(NT):
                    pool.indirect_dma_start(io["table"][:, :], bass.IndirectOffsetOnAxis(scat[:, k, n:n + 1], 0),
                                            token[:, n:n + 1], None).then_inc(scattered, 16)

        @block.scalar
        def _(act):
            act.wait_ge(sm["exp_in"], ONE + 1)
            act.activation(ex[:], ex[:], ACT.Exp).then_inc(sm["exp"], 1)

        @block.vector
        def _(dve):
            count = [0]

            def link(i):
                count[0] += 1
                i.then_inc(sm["dve"], 1)
                dve.wait_ge(sm["dve"], ONE + count[0])

            def tiles(ap):
                return ap.unsqueeze(2).to_broadcast(W)

            def experts(ap):
                return ap.unsqueeze(1).to_broadcast(W)

            TT, TS, RED = dve.tensor_tensor, dve.tensor_scalar, dve.tensor_reduce
            link(RED(red[:, 0, :], lg[:], AX.X, ALU.max))
            TT(ex[:], lg[:], tiles(red[:, 0, :]), ALU.subtract).then_inc(sm["exp_in"], 1)
            dve.wait_ge(sm["iota"], ONE + 2)
            dve.tensor_copy(ef[:], ei[:])
            link(dve.tensor_copy(tokenf[:], token[:]))
            TS(em[:], ef[:], float(-E), None, ALU.add)
            TS(ec[:], ef[:], float(CAP), None, ALU.mult)
            dve.wait_ge(sm["exp"], ONE + 1)
            link(RED(red[:, 1, :], ex[:], AX.X, ALU.add))
            link(dve.reciprocal(red[:, 2, :], red[:, 1, :]))
            link(TT(prob[:], ex[:], tiles(red[:, 2, :]), ALU.mult))
            for k in range(TOPK):
                link(RED(t["gate"][:, k, :], prob[:], AX.X, ALU.max))
                link(TT(eq[:], prob[:], tiles(t["gate"][:, k, :]), ALU.is_equal))
                link(TT(eq[:], eq[:], experts(em[:]), ALU.mult))
                link(RED(red[:, 3, :], eq[:], AX.X, ALU.min))
                link(TT(hot[k][:], tiles(red[:, 3, :]), experts(em[:]), ALU.is_equal))
                if k == 0:
                    link(dve.scalar_tensor_tensor(prob[:], hot[k][:], -2.0, prob[:], ALU.mult, ALU.add))
            TT(chosen[:], hot[0][:], hot[1][:], ALU.add).then_inc(sm["counts"], 1)
            dve.wait_ge(sm["counts"], ONE + 2)
            flat = [x[:].rearrange("p a e -> p (a e)") for x in (total, scan[0])]
            dve.tensor_copy(flat[0], pp[:, NT * E:2 * NT * E])
            link(dve.tensor_copy(flat[1], pp[:, NT * E:2 * NT * E]))
            step, a = 1, 0
            while step < NT:
                TT(scan[1 - a][:, step:, :], scan[a][:, step:, :], scan[a][:, :NT - step, :], ALU.add)
                link(dve.tensor_copy(scan[1 - a][:, :step, :], scan[a][:, :step, :]))
                step, a = 2 * step, 1 - a
            link(TT(place[:], scan[a][:], total[:], ALU.subtract))
            link(TT(place[:], place[:], pp[:, 0:NT * E].rearrange("p (a e) -> p a e", e=E), ALU.add))
            TS(kept[:], place[:], float(CAP), None, ALU.is_lt)
            link(TT(place[:], place[:], experts(ec[:]), ALU.add))
            link(TT(place[:], place[:], kept[:], ALU.mult))
            for k in range(TOPK):
                link(TT(tmp[:], hot[k][:], kept[:], ALU.mult))
                link(RED(has[:], tmp[:], AX.X, ALU.add))
                link(TT(tmp[:], hot[k][:], place[:], ALU.mult))
                link(RED(slot[:], tmp[:], AX.X, ALU.add))
                link(TS(dump[:], tokenf[:], float(SLOTS + k * B * S), None, ALU.add))
                TT(t["gate"][:, k, :], t["gate"][:, k, :], has[:], ALU.mult)
                dve.tensor_copy(t["where"][:, k, :], slot[:])
                link(TS(has[:], has[:], -1.0, 1.0, ALU.mult, ALU.add))
                link(TT(dump[:], dump[:], has[:], ALU.mult))
                link(TT(slot[:], slot[:], dump[:], ALU.add))
                dve.tensor_copy(scat[:, k, :], slot[:]).then_inc(sm["scatter_idx"], 1)
                dve.wait_ge(sm["scatter_idx"], ONE + k + 1)
            dve.memset(t["slot_token"][:], 0).then_inc(sm["table_f"], 1)
            dve.wait_ge(sm["table_loaded"], ONE + 16)
            dve.tensor_copy(tabf[:], tab[:]).then_inc(sm["table_f"], 1)
            dve.wait_ge(sm["table_T"], ONE + 1)
            dve.tensor_copy(t["slot_token"][:, 0:ST], pt[:, 0:ST]).then_inc(sm["idx"], 1)

        @block.tensor
        def _(pe):
            pe.wait_ge(sm["counts"], ONE + 1)
            c = chosen[:].rearrange("p a e -> p (a e)")
            pe.matmul(pp[:, 0:NT * E], t["upper"][:], c, start=True, stop=True)
            pe.matmul(pp[:, NT * E:2 * NT * E], t["ones"][:], c, start=True, stop=True).then_inc(sm["counts"], 1)
            pe.wait_ge(sm["table_f"], ONE + 2)
            pe.transpose(pt[:, 0:ST], tabf[:], t["ident"][0:ST, 0:ST]).then_inc(sm["table_T"], 1)


def stage_experts(nc, io, t):
    with Scope(nc) as s:
        RW = 2
        HB = BLK // 2
        w1 = [s.sb(f"ex_w1_{p}", [P, NF, KD, P], F32R) for p in "hl"]
        w2 = [s.sb(f"ex_w2_{p}", [P, NF, D], F32R) for p in "hl"]
        raw = s.sb("ex_raw", [P, RW, 2, D])
        xT = [[s.sb(f"ex_xT{b}{p}", [P, KD, BLK], F32R) for p in "hl"] for b in range(2)]
        h = [[s.sb(f"ex_h{r}{p}", [P, 2, HB], F32R) for p in "hl"] for r in range(2)]
        xg = [s.sb(f"ex_xg{r}", [P, D]) for r in range(2)]
        gi = [s.sb(f"ex_gi{r}", [P, 1], I32) for r in range(2)]
        ys = s.sb("ex_ys", [P, BT, D])
        hid = s.ps("ex_hid", [P, 2, 512])
        acc = [s.ps(f"ex_acc{i}", [P, D]) for i in range(BT)]
        xb = s.ps("ex_xb", [P, D])
        raw_loaded = [s.sem(f"raw_loaded{r}") for r in range(RW)]
        gathered = [s.zero_sem(f"gathered{r}") for r in range(2)]
        names = ("w_hi", "w_lo", "idx_col", "x_turned", "x_hi", "x_lo", "hidden", "h_hi", "h_lo", "used",
                 "y_act", "y_dve", "y_stored", "passed_pool")
        sm = {n: s.sem("ex_" + n) for n in names}
        s.credit()
        block = s.ctx.enter_context(nc.Block())

        TURN = {3 * i: i for i in range(BT)}

        @block.sync
        def _(sp):
            with sp.Fori(0, E) as e:
                for f in range(NF):
                    sp.wait_ge(sm["w_lo"], ONE + (2 * (NF * e + f - RW) + 2 if f >= RW else 2 * NF * e))
                    sp.dma_start(raw[:, f % RW, 0, :], io["w1_tiles"][NF * e + f]).then_inc(raw_loaded[f % RW], 16)
                    sp.dma_start(raw[:, f % RW, 1, :], io["w2_tiles"][NF * e + f]).then_inc(raw_loaded[f % RW], 16)

        @block.gpsimd
        def _(pool):
            def gather(n, r, first):
                if not first:
                    wait_apart(pool, sm["x_turned"], n - 1, sm["passed_pool"])
                pool.tensor_copy(gi[r][:], t["slot_token"][:, bass.ds(n, 1)]).then_inc(sm["idx_col"], 1)
                wait_apart(pool, sm["idx_col"], n + 1, sm["passed_pool"])
                pool.indirect_dma_start(xg[r][:], None, io["xn3"][:, :], bass.IndirectOffsetOnAxis(gi[r][:], 0))\
                    .then_inc(gathered[r], 16)

            gather(0, 0, True)
            gather(1, 1, True)
            with pool.Fori(0, (ST + BT - 3) // 2 + 1) as j:
                for r in range(2):
                    gather(2 * j + 2 + r, r, False)
            for r in range(2):
                pool.wait_ge(gathered[r], 16 * (ST + BT + 1) // 2)

        @block.scalar
        def _(act):
            def turn_hi(m, b, i):
                act.wait_ge(sm["x_turned"], ONE + BT * m + i + 1)
                act.activation(xT[b][0][:, :, i * P:(i + 1) * P], xb[:].rearrange("p (k n) -> p k n", k=KD), ACT.Copy)\
                    .then_inc(sm["x_hi"], 1)

            def split_hi(e, f):
                act.wait_ge(raw_loaded[f % RW], ONE + (32 * ((NF * e + f - f % RW) // RW + 1) if isinstance(e, int) else
                            e * (32 * NF // RW) + 32 * (f // RW + 1)))
                wait(act, sm["used"], 2 * NF * e - NF + f + 1 if not isinstance(e, int) or e else 0)
                act.activation(w1[0][:, f, :, :].rearrange("p k n -> p (k n)"), raw[:, f % RW, 0, :], ACT.Copy)\
                    .then_inc(sm["w_hi"], 1)
                act.activation(w2[0][:, f, :], raw[:, f % RW, 1, :], ACT.Copy).then_inc(sm["w_hi"], 1)

            def block_steps(e, b, refill):
                m = 2 * e + b
                for f in range(NF):
                    act.wait_ge(sm["hidden"], ONE + NF * m + f + 1)
                    act.activation(h[f % 2][0][:], hid[:, :, 0:HB], ACT.Relu).then_inc(sm["h_hi"], 1)
                    if f in TURN:
                        turn_hi(m + 1, 1 - b, TURN[f])
                    if refill and f >= 2:
                        split_hi(e + 1, f - 2)
                act.wait_ge(sm["used"], ONE + NF * (m + 1))
                act.wait_ge(sm["y_stored"], ONE + 16 * m)
                for i in range(0, 2):
                    act.activation(ys[:, i, :], acc[i][:], ACT.Copy).then_inc(sm["y_act"], 1)
                if refill:
                    split_hi(e + 1, NF - 2)
                    split_hi(e + 1, NF - 1)
                act.wait_ge(sm["y_dve"], ONE + 3 * (m + 1))
                act.wait_ge(sm["y_act"], ONE + 2 * (m + 1))
                act.dma_start(io["y_blocks"][m], ys[:]).then_inc(sm["y_stored"], 16)

            for i in range(BT):
                turn_hi(0, 0, i)
            for f in range(NF):
                split_hi(0, f)
            with act.Fori(0, E - 1) as e:
                block_steps(e, 0, False)
                block_steps(e, 1, True)
            block_steps(E - 1, 0, False)
            block_steps(E - 1, 1, False)
            act.wait_ge(sm["y_stored"], ONE + 16 * 2 * E)

        @block.vector
        def _(dve):
            def turn_lo(m, b, i):
                dve.wait_ge(sm["x_hi"], ONE + BT * m + i + 1)
                dve.tensor_tensor(xT[b][1][:, :, i * P:(i + 1) * P], xb[:].rearrange("p (k n) -> p k n", k=KD),
                                  f32(xT[b][0][:, :, i * P:(i + 1) * P]), ALU.subtract).then_inc(sm["x_lo"], 1)

            def split_lo(e, f):
                dve.wait_ge(sm["w_hi"], ONE + 2 * (NF * e + f + 1))
                dve.tensor_tensor(w1[1][:, f, :, :].rearrange("p k n -> p (k n)"), raw[:, f % RW, 0, :],
                                  f32(w1[0][:, f, :, :]).rearrange("p k n -> p (k n)"), ALU.subtract)\
                    .then_inc(sm["w_lo"], 1)
                dve.tensor_tensor(w2[1][:, f, :], raw[:, f % RW, 1, :], f32(w2[0][:, f, :]), ALU.subtract)\
                    .then_inc(sm["w_lo"], 1)

            def block_steps(e, b, refill):
                m = 2 * e + b
                for f in range(NF):
                    dve.wait_ge(sm["h_hi"], ONE + NF * m + f + 1)
                    dve.scalar_tensor_tensor(h[f % 2][1][:], hid[:, :, 0:HB], 0.0, f32(h[f % 2][0][:]),
                                             ALU.max, ALU.subtract).then_inc(sm["h_lo"], 1)
                    if f in TURN:
                        turn_lo(m + 1, 1 - b, TURN[f])
                    if refill and f >= 2:
                        split_lo(e + 1, f - 2)
                dve.wait_ge(sm["used"], ONE + NF * (m + 1))
                dve.wait_ge(sm["y_stored"], ONE + 16 * m)
                for i in range(2, BT):
                    dve.tensor_copy(ys[:, i, :], acc[i][:]).then_inc(sm["y_dve"], 1)
                if refill:
                    split_lo(e + 1, NF - 2)
                    split_lo(e + 1, NF - 1)

            for i in range(BT):
                turn_lo(0, 0, i)
            for f in range(NF):
                split_lo(0, f)
            with dve.Fori(0, E - 1) as e:
                block_steps(e, 0, False)
                block_steps(e, 1, True)
            block_steps(E - 1, 0, False)
            block_steps(E - 1, 1, False)

        @block.tensor
        def _(pe):
            def turn(m, i, parity, first):
                n = BT * m + i
                r = (parity * BT + i) % 2
                pe.wait_ge(gathered[r], 16 * (BT * m // 2 + i // 2 + 1) if isinstance(m, int) else
                           first * (16 * BT) + 16 * ((parity * BT + i) // 2 + 1))
                wait(pe, sm["x_lo"], n)
                for k in range(KD):
                    q = pe.transpose(xb[:, k * P:(k + 1) * P], xg[r][:, k * P:(k + 1) * P], t["ident"][:])
                q.then_inc(sm["x_turned"], 1)

            for i in range(BT):
                turn(0, i, 0, 0)
            with pe.Fori(0, E) as e:
                for b in range(2):
                    m = 2 * e + b

                    def outputs(f):
                        pe.wait_ge(sm["h_lo"], ONE + NF * m + f + 1)
                        if f == 0:
                            pe.wait_ge(sm["y_act"], ONE + 2 * m)
                            pe.wait_ge(sm["y_dve"], ONE + (BT - 2) * m)
                        for i in range(BT):
                            hh, hl = (x[:].rearrange("p a n -> p (a n)")[:, i * P:(i + 1) * P] for x in h[f % 2])
                            q = split_passes(pe, acc[i][:], (hh, hl), [w[:, f, :] for w in w2], f == 0, f == NF - 1)
                        q.then_inc(sm["used"], 1)

                    pe.wait_ge(sm["x_lo"], ONE + BT * (m + 1))
                    for f in range(NF):
                        pe.wait_ge(sm["w_lo"], ONE + 2 * (NF * e + f + 1))
                        pe.wait_ge(sm["h_lo"], ONE + NF * m + f)
                        for k in range(KD):
                            for a, q in ((0, 0), (0, 1), (1, 0)):
                                for z in range(2):
                                    i = pe.matmul(hid[:, z, 0:HB], w1[a][:, f, k, :],
                                                  xT[b][q][:, k, z * HB:(z + 1) * HB], start=k == 0 and a + q == 0,
                                                  stop=k == KD - 1 and a == 1)
                        i.then_inc(sm["hidden"], 1)
                        if f in TURN:
                            turn(m + 1, TURN[f], 1 - b, e + b)
                        if f:
                            outputs(f - 1)
                    outputs(NF - 1)


def stage_combine(nc, io, t):
    with Scope(nc) as s:
        x2 = s.sb("cb_x2", [P, CH, D])
        y = [[s.sb(f"cb_y{c}{k}", [P, D]) for k in range(TOPK)] for c in range(CH)]
        gi = [[s.sb(f"cb_gi{c}{k}", [P, 1], I32) for k in range(TOPK)] for c in range(CH)]
        x2_loaded = [s.sem(f"x2_loaded{c}") for c in range(CH)]
        gathered = [[s.zero_sem(f"y_gathered{c}{k}") for k in range(TOPK)] for c in range(CH)]
        stored = [s.sem(f"out_stored{c}") for c in range(CH)]
        idx_col, part, done, passed_dve, passed_pool = (
            s.sem("cb_" + n) for n in ("idx_col", "part", "done", "passed_dve", "passed_pool"))
        s.credit()
        block = s.ctx.enter_context(nc.Block())
        steps = NT // CH

        @block.sync
        def _(sp):
            with sp.Fori(0, steps) as j:
                for c in range(CH):
                    sp.wait_ge(stored[c], ONE + 16 * j)
                    sp.dma_start(x2[:, c, :], io["x2"][CH * j + c]).then_inc(x2_loaded[c], 16)

        @block.scalar
        def _(act):
            with act.Fori(0, steps) as j:
                for c in range(CH):
                    act.wait_ge(done, ONE + CH * j + c + 1)
                    act.dma_start(io["out_tiles"][CH * j + c], x2[:, c, :]).then_inc(stored[c], 16)
            for c in range(CH):
                act.wait_ge(stored[c], ONE + 16 * steps)

        @block.gpsimd
        def _(pool):
            with pool.Fori(0, steps) as j:
                for c in range(CH):
                    for k in range(TOPK):
                        n = CH * j + c
                        wait_apart(pool, done, CH * j, passed_pool)
                        pool.tensor_copy(gi[c][k][:], t["where"][:, k, bass.ds(n, 1)]).then_inc(idx_col, 1)
                        wait_apart(pool, idx_col, TOPK * n + k + 1, passed_pool)
                        pool.indirect_dma_start(y[c][k][:], None, io["y"][:, :],
                                                bass.IndirectOffsetOnAxis(gi[c][k][:], 0)).then_inc(gathered[c][k], 16)

        @block.vector
        def _(dve):
            with dve.Fori(0, steps) as j:
                for c in range(CH):
                    n = CH * j + c
                    dve.wait_ge(x2_loaded[c], ONE + 16 * j + 16)
                    for k in range(TOPK):
                        if k:
                            dve.wait_ge(part, ONE + n + 1)
                        wait_apart(dve, gathered[c][k], 16 * j + 16, passed_dve, start=0)
                        i = dve.scalar_tensor_tensor(x2[:, c, :], y[c][k][:], t["gate"][:, k, bass.ds(n, 1)], x2[:, c, :],
                                                     ALU.mult, ALU.add)
                        i.then_inc(part if k == 0 else done, 1)


def decoder_layer(nc, io):
    with Scope(nc) as s:
        t = {}
        t["ident"] = s.sb("ident", [P, P])
        t["identb"] = s.sb("identb", [P, P], BF16)
        t["mask"] = s.sb("mask", [P, P], BF16)
        t["ones"] = s.sb("ones", [P, P])
        t["upper"] = s.sb("upper", [P, P])
        t["avg"] = s.sb("avg", [P, P])
        t["half"] = s.sb("half", [P, 1])
        t["eps"] = s.sb("eps", [P, 1])
        t["gate"] = s.sb("gate", [P, TOPK, NT])
        t["where"] = s.sb("where", [P, TOPK, NT], I32)
        t["slot_token"] = s.sb("slot_token", [P, ST + BT + 1], I32)
        with Scope(nc) as a:
            t["logits"] = a.sb("logits", [P, NT, E])
            t["act"] = a.sb("act", [P, NT, D])
            t["mean1"] = a.sb("mean1", [P, NT, 1])
            t["rstd1"] = a.sb("rstd1", [P, NT, 1])
            for n in ("theta_b", "phi_b", "g_b"):
                t[n] = a.sb(n + "_col", [P, 1])
            t["out_b"] = a.sb("out_b_col", [P, TPB])
            t["gamma"] = a.sb("gamma", [P, D])
            t["beta"] = a.sb("beta", [P, D])
            shapes = {"theta_w": [P, TPB, LAT], "phi_w": [P, TPB, LAT], "g_w": [P, TPB, LAT],
                      "out_w": [P, S], "router_w": [P, KD, E]}
            for n, shape in shapes.items():
                t[n] = [a.sb(f"{n}_{p}", shape, F32R) for p in ("hi", "lo")]
            with Scope(nc) as o:
                t["wo"] = [o.sb(f"wo_{p}", [P, KD, D], F32R) for p in ("hi", "lo")]
                with Scope(nc) as q:
                    t["k"] = q.sb("k", [P, NT, KVW])
                    t["v"] = q.sb("v", [P, NT, G, VW])
                    t["cos"] = q.sb("cos", [P, TPB, HD])
                    t["sin"] = q.sb("sin", [P, TPB, HD])
                    with Scope(nc) as w:
                        t["wqkv"] = [w.sb(f"wqkv_{p}", [P, KD, QKV], F32R) for p in ("hi", "lo")]
                        t["split"] = ["wqkv", "wo", *shapes]
                        stage_constants(nc, io, t)
                        stage_qkv(nc, io, t)
                    stage_attention(nc, t)
                stage_out_proj(nc, io, t)
            stage_cross(nc, io, t)
            stage_route(nc, io, t)
        stage_experts(nc, io, t)
        stage_combine(nc, io, t)


def build(nc, arrays, out):
    io = {}
    for name, (shape, dt) in arrays.items():
        io[name] = nc.dram_tensor(f"in_{name}_dram", shape, dt, kind="ExternalInput").ap()
    x2 = nc.dram_tensor("x2_dram", [NT, P, D], F32, kind="Internal").ap()
    xn3 = nc.dram_tensor("xn3_dram", [B * S, D], F32, kind="Internal").ap()
    y = nc.dram_tensor("y_dram", [SLOTS, D], F32, kind="Internal").ap()
    io["table"] = nc.dram_tensor("slot_table_dram", [SLOTS + TOPK * B * S, 1], I32, kind="Internal").ap()
    io["x2"], io["xn3"], io["y"] = x2, xn3, y
    io["x_tiles"] = io["x"].rearrange("b (u p) d -> (b u) p d", p=P)
    io["ctx_tiles"] = io["ctx"].rearrange("b (u p) d -> b p u d", p=P)
    io["x2_tiles"] = x2.rearrange("(b u) p d -> b p u d", u=TPB)
    io["xn3_tiles"] = xn3.rearrange("(b u p) d -> b p u d", u=TPB, p=P)
    io["y_blocks"] = y.rearrange("(m i p) d -> m p i d", i=BT, p=P)
    io["out_tiles"] = out.rearrange("b (u p) d -> (b u) p d", p=P)
    decoder_layer(nc, io)


def kernel(x, ctx_2048, L0_attn_wq, L0_attn_wk, L0_attn_wv, L0_attn_wo, L0_xattn_theta_w, L0_xattn_theta_b,
           L0_xattn_phi_w, L0_xattn_phi_b, L0_xattn_g_w, L0_xattn_g_b, L0_xattn_ln_gamma, L0_xattn_ln_beta,
           L0_xattn_out_w, L0_xattn_out_b, L0_ffn_Wg, L0_ffn_w1, L0_ffn_w2):
    import numpy as np
    import concourse.bacc as bacc
    from concourse.bass_utils import run_bass_kernel_spmd

    order = np.concatenate([np.arange(0, HD, 2), np.arange(1, HD, 2)])

    def halves(w):
        w = np.asarray(w)
        return w.reshape(D, -1, HD)[:, :, order].reshape(D, -1)

    def contraction_tiles(w):
        w = np.asarray(w)
        return np.ascontiguousarray(w.reshape(-1, P, w.shape[1]).transpose(1, 0, 2))

    inv_freq = (1.0 / 10000.0 ** (np.arange(0, HD, 2, dtype=np.float32) / HD)).astype(np.float32)
    angle = np.arange(S, dtype=np.float32)[:, None] * inv_freq[None, :]
    cos, sin = np.cos(angle).astype(np.float32), np.sin(angle).astype(np.float32)

    def position_tiles(a):
        return np.ascontiguousarray(a.reshape(TPB, P, HD).transpose(1, 0, 2))

    arrays = {
        "x": np.ascontiguousarray(x),
        "ctx": np.ascontiguousarray(ctx_2048),
        "wqkv": contraction_tiles(np.concatenate([halves(L0_attn_wq), halves(L0_attn_wk), np.asarray(L0_attn_wv)], 1)),
        "wo": contraction_tiles(L0_attn_wo),
        "theta_w": contraction_tiles(np.asarray(L0_xattn_theta_w).T),
        "phi_w": contraction_tiles(np.asarray(L0_xattn_phi_w).T),
        "g_w": contraction_tiles(np.asarray(L0_xattn_g_w).T),
        "out_w": np.ascontiguousarray(np.asarray(L0_xattn_out_w).T),
        "router_w": contraction_tiles(L0_ffn_Wg),
        "theta_b": np.ascontiguousarray(L0_xattn_theta_b),
        "phi_b": np.ascontiguousarray(L0_xattn_phi_b),
        "g_b": np.ascontiguousarray(L0_xattn_g_b),
        "out_b": np.ascontiguousarray(np.asarray(L0_xattn_out_b).reshape(TPB, P).T),
        "gamma": np.ascontiguousarray(L0_xattn_ln_gamma),
        "beta": np.ascontiguousarray(L0_xattn_ln_beta),
        "cos": position_tiles(np.concatenate([cos, cos], 1)),
        "sin": position_tiles(np.concatenate([-sin, sin], 1)),
        "w1_tiles": np.ascontiguousarray(np.asarray(L0_ffn_w1).reshape(E, KD, P, NF, P).transpose(0, 3, 2, 1, 4)
                                         .reshape(E * NF, P, D)),
        "w2_tiles": np.ascontiguousarray(np.asarray(L0_ffn_w2).reshape(E * NF, P, D)),
    }
    nc = bacc.Bacc("TRN2", target_bir_lowering=False, num_devices=1)
    out = nc.dram_tensor("out_dram", [B, S, D], F32, kind="ExternalOutput").ap()
    build(nc, {n: (a.shape, mybir.dt.from_np(a.dtype)) for n, a in arrays.items()}, out)
    r = run_bass_kernel_spmd(nc, [{f"in_{n}_dram": a for n, a in arrays.items()}], core_ids=[0])
    return r.results[0]["out_dram"]
```

```python
from contextlib import ExitStack

import concourse.bass as bass
from concourse import mybir

F32 = mybir.dt.float32
F32R = mybir.dt.float32r
BF16 = mybir.dt.bfloat16
I32 = mybir.dt.int32
ALU = mybir.AluOpType
ACT = mybir.ActivationFunctionType
AX = mybir.AxisListType

P = 128
B, S, D = 16, 256, 512
NT = B * S // P
TPB = S // P
KD = D // P
H, G, HD = 32, 8, 16
REP = H // G
KVW = G * HD
QKV = D + 2 * KVW
VW = HD + 8
LAT = 128
E, FF, TOPK = 8, 2048, 2
CAP = (5 * B * S * TOPK) // (4 * E)
NF = FF // P
SLOTS = E * CAP
BLK = CAP // 2
BT = BLK // P
ST = SLOTS // P
EPS = 1e-5
MASKED = -1e30
ONE = 1
CH = 4


def wait(eng, sem, value):
    if not (isinstance(value, int) and value <= 0):
        eng.wait_ge(sem, ONE + value)


def wait_apart(eng, sem, value, passed, start=ONE):
    if not (isinstance(value, int) and value <= 0):
        eng.wait_ge(sem, start + value).then_inc(passed, 1)


def f32(ap):
    return ap.bitcast(F32)


class Scope:

    def __init__(self, nc):
        self.nc = nc
        self.ctx = ExitStack()
        self.sems, self.zero_sems = [], []

    def __enter__(self):
        self.ctx.__enter__()
        return self

    def __exit__(self, *a):
        self.ctx.__exit__(*a)
        if self.sems:
            self.nc.clear_and_free_semaphores(self.sems + self.zero_sems)
            self.nc.all_engine_barrier()

    def sb(self, name, shape, dt=F32):
        return self.ctx.enter_context(self.nc.sbuf_tensor(name, shape, dt))

    def ps(self, name, shape, dt=F32):
        return self.ctx.enter_context(self.nc.psum_tensor(name, shape, dt))

    def sem(self, name):
        self.sems.append(self.nc.alloc_semaphore(name))
        return self.sems[-1]

    def zero_sem(self, name):
        self.zero_sems.append(self.nc.alloc_semaphore(name))
        return self.zero_sems[-1]

    def credit(self):
        engines = (self.nc.gpsimd, self.nc.scalar, self.nc.vector, self.nc.sync)
        for i, sem in enumerate(self.sems):
            engines[i % len(engines)].sem_inc(sem, ONE)
        self.nc.all_engine_barrier()


def split_passes(eng, out, lhs, rhs, first=True, last=True, **kw):
    eng.matmul(out, lhs[0], rhs[0], start=first, stop=False, **kw)
    eng.matmul(out, lhs[0], rhs[1], start=False, stop=False, **kw)
    return eng.matmul(out, lhs[1], rhs[0], start=False, stop=last, **kw)


def stage_constants(nc, io, t):
    with Scope(nc) as s:
        raw = {n: s.sb(f"raw_{n}", list(t[n][0].shape)) for n in t["split"]}
        ident_set, mask_set = s.sem("ident_zeroed"), s.sem("mask_zeroed")
        raw_loaded = {n: s.sem(f"raw_{n}_loaded") for n in t["split"]}
        tables_loaded = s.sem("tables_loaded")
        hi_done, lo_done = s.sem("weights_hi_done"), s.sem("weights_lo_done")
        s.credit()
        block = s.ctx.enter_context(nc.Block())
        names = list(t["split"])

        @block.sync
        def _(sp):
            for n in names:
                sp.dma_start(raw[n][:], io[n]).then_inc(raw_loaded[n], 16)
            for c in range(CH):
                sp.dma_start(t["x"][:, c, :], io["x_tiles"][c]).then_inc(tables_loaded, 16)
            sp.dma_start(t["cos"][:], io["cos"]).then_inc(tables_loaded, 16)
            sp.dma_start(t["sin"][:], io["sin"]).then_inc(tables_loaded, 16)
            for n in ("theta_b", "phi_b", "g_b"):
                sp.dma_start(t[n][:], io[n].rearrange("(p o) -> p o", o=1)).then_inc(tables_loaded, 16)
            sp.dma_start(t["out_b"][:], io["out_b"]).then_inc(tables_loaded, 16)
            sp.dma_start(t["gamma"][:], io["gamma"]).then_inc(tables_loaded, 16)
            sp.dma_start(t["beta"][:], io["beta"]).then_inc(tables_loaded, 16)
            sp.wait_ge(tables_loaded, ONE + 16 * (8 + CH))

        @block.gpsimd
        def _(pool):
            pool.memset(t["ident"][:], 0.0).then_inc(ident_set, 1)
            pool.memset(t["identb"][:], 0.0).then_inc(ident_set, 1)
            pool.memset(t["mask"][:], 0.0).then_inc(mask_set, 1)
            pool.memset(t["ones"][:], 1.0)
            pool.memset(t["upper"][:], 1.0).then_inc(mask_set, 1)
            pool.memset(t["avg"][:], 1.0 / P)
            pool.memset(t["half"][:], -0.5)
            pool.memset(t["eps"][:], EPS)
            pool.memset(t["v"][:], 1.0)
            pool.wait_ge(ident_set, ONE + 2)
            for m in (t["ident"], t["identb"]):
                pool.affine_select(out=m[:], in_=m[:], compare_op=ALU.not_equal, fill=1.0, base=0,
                                   pattern=[[-1, P]], channel_multiplier=1)
            pool.wait_ge(mask_set, ONE + 2)
            pool.affine_select(out=t["mask"][:], in_=t["mask"][:], compare_op=ALU.is_ge, fill=MASKED, base=0,
                               pattern=[[-1, P]], channel_multiplier=1)
            pool.affine_select(out=t["upper"][:], in_=t["upper"][:], compare_op=ALU.is_gt, fill=0.0, base=0,
                               pattern=[[1, P]], channel_multiplier=-1)

        @block.scalar
        def _(act):
            for n in names:
                act.wait_ge(raw_loaded[n], ONE + 16)
                act.activation(t[n][0][:], raw[n][:], ACT.Copy).then_inc(hi_done, 1)

        @block.vector
        def _(dve):
            for i, n in enumerate(names):
                dve.wait_ge(raw_loaded[n], ONE + 16)
                dve.wait_ge(hi_done, ONE + i + 1)
                dve.tensor_tensor(t[n][1][:], raw[n][:], f32(t[n][0][:]), ALU.subtract).then_inc(lo_done, 1)


def stage_qkv(nc, io, t):
    with Scope(nc) as s:
        x = t["x"]
        xn = s.sb("qkv_xn", [P, CH, D])
        xh = [s.sb(f"qkv_xh{c}", [P, KD, P], F32R) for c in range(CH)]
        xl = [s.sb(f"qkv_xl{c}", [P, KD, P], F32R) for c in range(CH)]
        st6 = s.sb("qkv_st6", [P, CH, 6])
        mv = s.sb("qkv_mv", [P, CH, 2])
        ve = s.sb("qkv_ve", [P, CH])
        rstd = s.sb("qkv_rstd", [P, CH])
        rc = s.sb("qkv_rc", [P, 2, D + KVW])
        rs = s.sb("qkv_rs", [P, 2, D + KVW])
        xT = [s.ps(f"qkv_xT{c}", [P, D]) for c in range(2)]
        proj = [s.ps(f"qkv_proj{c}", [P, 1024]) for c in range(2)]
        x_loaded = [s.sem(f"x_loaded{c}") for c in range(CH)]
        stats, moments, eps_added, rstd_ready = (s.sem(n) for n in ("stats", "moments", "eps_added", "rstd_ready"))
        xn_ready, xT_ready, xh_ready, xl_ready = (s.sem(n) for n in ("xn_ready", "xT_ready", "xh_ready", "xl_ready"))
        proj_ready, rot_cos, rot_sin, rot_done, v_done = (
            s.sem(n) for n in ("proj_ready", "rot_cos", "rot_sin", "rot_done", "v_done"))
        passed_pool, passed_dve = s.sem("qkv_passed_pool"), s.sem("qkv_passed_dve")
        s.credit()
        block = s.ctx.enter_context(nc.Block())
        steps = NT // CH

        def turns(eng, first, turn):
            first()
            turn(0, True, True)
            with eng.Fori(1, steps - 2) as j:
                turn(j, True, True)
            turn(steps - 2, True, False)
            turn(steps - 1, False, False)

        @block.sync
        def _(sp):
            def load(j):
                for c in range(CH):
                    n = CH * j + c
                    wait(sp, xn_ready, n - CH + 1)
                    sp.dma_start(x[:, c, :], io["x_tiles"][n]).then_inc(x_loaded[c], 16)

            with sp.Fori(1, steps) as j:
                load(j)

        @block.gpsimd
        def _(pool):
            def rstd_of(n, c):
                pool.wait_ge(moments, ONE + n + 1)
                pool.tensor_tensor(ve[:, c:c + 1], mv[:, c, 1:2], t["eps"][:], ALU.add).then_inc(eps_added, 1)
                pool.wait_ge(eps_added, ONE + n + 1)
                pool.tensor_tensor(rstd[:, c:c + 1], ve[:, c:c + 1], t["half"][:, 0:1],
                                   ALU.pow).then_inc(rstd_ready, 1)

            def first():
                for n in range(2 * CH):
                    rstd_of(n, n % CH)

            def turn(j, split_next, norm_next):
                for c in range(CH):
                    n = CH * j + c
                    pool.wait_ge(rot_sin, ONE + 2 * n + 2)
                    wait_apart(pool, rot_cos, n + 1, passed_pool)
                    pool.tensor_tensor(t["act"][:, n, :], rc[:, c % 2, 0:D], rs[:, c % 2, 0:D],
                                       ALU.add).then_inc(rot_done, 1)
                    pool.tensor_tensor(t["k"][:, n, :], rc[:, c % 2, D:], rs[:, c % 2, D:],
                                       ALU.add).then_inc(rot_done, 1)
                    if norm_next:
                        rstd_of(n + 2 * CH, c)

            turns(pool, first, turn)

        @block.scalar
        def _(act):
            def split_hi(n, c):
                act.wait_ge(xT_ready, ONE + n + 1)
                wait(act, proj_ready, n - CH + 1)
                act.activation(xh[c][:].rearrange("p k n -> p (k n)"), xT[c % 2][:], ACT.Copy).then_inc(xh_ready, 1)

            def first():
                for c in range(CH):
                    split_hi(c, c)

            def turn(j, split_next, norm_next):
                for c in range(CH):
                    n = CH * j + c
                    act.wait_ge(rot_sin, ONE + 2 * n + 2)
                    act.activation(t["v"][:, n, :, 0:HD],
                                   proj[c % 2][:, D + KVW:QKV].rearrange("p (g d) -> p g d", g=G),
                                   ACT.Copy).then_inc(v_done, 1)
                    if split_next:
                        split_hi(n + CH, c)

            turns(act, first, turn)

        @block.vector
        def _(dve):
            def statistics(j, c):
                n = CH * j + c
                wait(dve, x_loaded[c], 16 * j)
                dve.bn_stats(st6[:, c, :], x[:, c, :]).then_inc(stats, 1)
                wait_apart(dve, stats, n + 1, passed_dve)
                dve.bn_aggr(mv[:, c, :], st6[:, c, :]).then_inc(moments, 1)

            def normalise(j, c):
                n = CH * j + c
                dve.wait_ge(rstd_ready, ONE + n + 1)
                wait(dve, xT_ready, n - CH + 1)
                dve.tensor_scalar(xn[:, c, :], x[:, c, :], mv[:, c, 0:1], rstd[:, c:c + 1],
                                  ALU.subtract, ALU.mult).then_inc(xn_ready, 1)

            def split_lo(n, c):
                dve.wait_ge(xh_ready, ONE + n + 1)
                dve.tensor_tensor(xl[c][:].rearrange("p k n -> p (k n)"), xT[c % 2][:],
                                  f32(xh[c][:]).rearrange("p k n -> p (k n)"), ALU.subtract).then_inc(xl_ready, 1)

            def first():
                for c in range(CH):
                    statistics(0, c)
                for c in range(CH):
                    normalise(0, c)
                for c in range(CH):
                    split_lo(c, c)
                    statistics(1, c)
                for c in range(CH):
                    normalise(1, c)

            def turn(j, split_next, norm_next):
                for c in range(CH):
                    n = CH * j + c
                    qk = proj[c % 2][:, 0:D + KVW].rearrange("p (h d) -> p h d", d=HD)
                    cs = rc[:, c % 2, :].rearrange("p (h d) -> p h d", d=HD)
                    sn = rs[:, c % 2, :].rearrange("p (h d) -> p h d", d=HD)
                    cos = t["cos"][:, c % TPB, :].unsqueeze(1).to_broadcast([P, H + G, HD])
                    dve.wait_ge(proj_ready, ONE + n + 1)
                    wait(dve, rot_done, 2 * (n - 1))
                    dve.tensor_tensor(cs, qk, cos, ALU.mult).then_inc(rot_cos, 1)
                    for half in range(2):
                        a, b = half * HD // 2, (1 - half) * HD // 2
                        sin = t["sin"][:, c % TPB, a:a + HD // 2].unsqueeze(1).to_broadcast([P, H + G, HD // 2])
                        dve.tensor_tensor(sn[:, :, a:a + HD // 2], qk[:, :, b:b + HD // 2], sin,
                                          ALU.mult).then_inc(rot_sin, 1)
                    if norm_next and c:
                        normalise(j + 2, c - 1)
                    if split_next:
                        split_lo(n + CH, c)
                    if norm_next:
                        statistics(j + 2, c)
                if norm_next:
                    normalise(j + 2, CH - 1)

            turns(dve, first, turn)

        @block.tensor
        def _(pe):
            def transposes(n, c):
                pe.wait_ge(xn_ready, ONE + n + 1)
                wait(pe, xl_ready, n - 1)
                for k in range(KD):
                    m = pe.transpose(xT[c % 2][:, k * P:(k + 1) * P], xn[:, c, k * P:(k + 1) * P], t["ident"][:])
                m.then_inc(xT_ready, 1)

            def first():
                for c in range(CH):
                    transposes(c, c)

            def turn(j, split_next, norm_next):
                for c in range(CH):
                    n = CH * j + c
                    pe.wait_ge(xl_ready, ONE + n + 1)
                    wait(pe, v_done, n - 1)
                    for half in range(2):
                        a, b = half * 512, min(QKV, half * 512 + 512)
                        for k in range(KD):
                            m = split_passes(pe, proj[c % 2][:, a:b], (xh[c][:, k, :], xl[c][:, k, :]),
                                             [w[:, k, a:b] for w in t["wqkv"]], k == 0, k == KD - 1)
                    m.then_inc(proj_ready, 1)
                    if split_next:
                        transposes(n + CH, c)

            turns(pe, first, turn)


def stage_attention(nc, t):
    with Scope(nc) as s:
        R = 2
        stk = [s.sb(f"at_stk{r}", [P, TPB, 3 * P], F32R) for r in range(R)]
        qT = [s.sb(f"at_qT{r}", [P, 2, S], F32R) for r in range(R)]
        kz = [s.sb(f"at_kz{r}", [P, 2, S], F32R) for r in range(R)]
        prob = [s.sb(f"at_prob{r}", [P, 3, 512]) for r in range(R)]
        pT = [s.sb(f"at_pT{r}", [P, 3, 512]) for r in range(R)]
        nb = s.sb("at_nb", [P, R, 8])
        rinv = s.sb("at_rinv", [P, R, 8])
        sc = [s.ps(f"at_scores{a}", [P, 512]) for a in range(3)]
        tp = [s.ps(f"at_tp{r}", [P, 512]) for r in range(2)]
        ob = s.ps("at_out", [P, 512])
        sk = s.ps("at_stkT", [P, 2, 512])
        names = ("q_hi", "stack_ready", "stackT_ready", "kz_zeroed", "qT_ready", "kz_ready", "scores_ready",
                 "bias_ready", "probs_ready", "probsT_ready", "pT_a", "pT_b", "out_ready", "rinv_ready",
                 "attn_done")
        sm = {n: s.sem("at_" + n) for n in names}
        passed_pool = s.sem("at_passed_pool")
        s.credit()
        block = s.ctx.enter_context(nc.Block())
        o4 = ob[:, 0:TPB * REP * VW].rearrange("p (q h d) -> p q h d", q=TPB, h=REP)

        @block.gpsimd
        def _(pool):
            with pool.Fori(0, B) as b:
                for g in range(G):
                    n = G * b + g
                    r = g % R
                    if g >= R:
                        wait_apart(pool, sm["stackT_ready"], n - 1, passed_pool)
                    else:
                        wait_apart(pool, sm["stackT_ready"], G * b, passed_pool)
                    for u in range(TPB):
                        q = t["act"][:, TPB * b + u, g * REP * HD:(g + 1) * REP * HD].rearrange("p (h d) -> p h d", d=HD)
                        k = t["k"][:, TPB * b + u, g * HD:(g + 1) * HD]
                        qs = stk[r][:, u, 0:2 * P].rearrange("p (h c l d) -> p h c l d", h=REP, c=2, l=2)
                        ks = stk[r][:, u, 2 * P:3 * P].rearrange("p (m l c d) -> p m l c d", m=2, l=2, c=2)
                        q4 = q.unsqueeze(2).to_broadcast([P, REP, 2, HD])
                        k4 = k.unsqueeze(1).unsqueeze(1).to_broadcast([P, 2, 2, HD])
                        pool.tensor_copy(qs[:, :, :, 0, :], q4).then_inc(sm["q_hi"], 1)
                        pool.tensor_copy(ks[:, :, 0, :, :], k4).then_inc(sm["q_hi"], 1)
                        wait_apart(pool, sm["q_hi"], 4 * n + 2 * u + 1, passed_pool)
                        pool.tensor_tensor(qs[:, :, :, 1, :], q4, f32(qs[:, :, :, 0, :]),
                                           ALU.subtract).then_inc(sm["stack_ready"], 1)
                        wait_apart(pool, sm["q_hi"], 4 * n + 2 * u + 2, passed_pool)
                        pool.tensor_tensor(ks[:, :, 1, :, :], k4, f32(ks[:, :, 0, :, :]),
                                           ALU.subtract).then_inc(sm["stack_ready"], 1)

        def slots(eng, slot, first):
            first()
            slot(0, 0, True, True, False)
            with eng.Fori(0, B - 1) as b:
                for k in range(1, G + 1):
                    slot(b + k // G, k % G, True, True, True)
            for k in range(1, G + 1):
                slot(B - 1, k, k < G - 1, k < G, True)

        @block.scalar
        def _(act):
            def operand(n, r):
                act.wait_ge(sm["stackT_ready"], ONE + n + 1)
                act.activation(qT[r][:].rearrange("p m (u n) -> p u m n", u=TPB),
                               sk[:, :, 0:2 * P].rearrange("p u (m n) -> p u m n", m=2), ACT.Copy,
                               scale=HD ** -0.5)\
                    .then_inc(sm["qT_ready"], 1)

            def exps(n, r, a):
                act.wait_ge(sm["bias_ready"], ONE + 3 * n + a + 1)
                w = P if a == 0 else S
                for h in range(512 // w):
                    hb = h if a == 0 else REP + 2 * (a - 1) + h
                    m = act.activation(prob[r][:, a, h * w:(h + 1) * w], sc[a][:, h * w:(h + 1) * w], ACT.Exp,
                                       bias=nb[:, r, hb:hb + 1])
                m.then_inc(sm["probs_ready"], 1)

            def turn(n, r):
                act.wait_ge(sm["probsT_ready"], ONE + 3 * n + 2)
                act.activation(pT[r][:, 1, :], tp[1][:], ACT.Copy).then_inc(sm["pT_b"], 1)

            def slot(b, g, has_next, has_this, has_prev):
                n = G * b + g
                if has_prev:
                    turn(n - 1, (g - 1) % R)
                if has_this:
                    exps(n, g % R, 0)
                    exps(n, g % R, 1)
                if has_next:
                    operand(n + 1, (g + 1) % R)
                if has_this:
                    exps(n, g % R, 2)

            slots(act, slot, lambda: operand(0, 0))

        @block.vector
        def _(dve):
            def operand(n, r):
                dve.wait_ge(sm["qT_ready"], ONE + n + 1)
                for m in range(2):
                    i = dve.tensor_copy(kz[r][64 * m:64 * m + 64, m, :].rearrange("p (u n) -> p u n", u=TPB),
                                        sk[64 * m:64 * m + 64, :, 2 * P:3 * P])
                i.then_inc(sm["kz_ready"], 1)

            def maxima(n, r, a):
                dve.wait_ge(sm["scores_ready"], ONE + 3 * n + a + 1)
                lo, hi = (0, REP) if a == 0 else (REP + 2 * (a - 1), REP + 2 * a)
                dve.tensor_reduce(nb[:, r, lo:hi], sc[a][:].rearrange("p (h k) -> p h k", h=hi - lo), AX.X, ALU.max,
                                  negate=True).then_inc(sm["bias_ready"], 1)

            def turn(n, r, c):
                dve.wait_ge(sm["probsT_ready"], ONE + 3 * n + c + 1)
                dve.tensor_copy(pT[r][:, c, :], tp[0][:]).then_inc(sm["pT_a"], 1)

            def finish(n, r, b, g):
                dve.wait_ge(sm["out_ready"], ONE + n + 1)
                dve.reciprocal(rinv[:, r, :].rearrange("p (q h) -> p q h", q=TPB), o4[:, :, :, HD])\
                    .then_inc(sm["rinv_ready"], 1)
                dve.wait_ge(sm["rinv_ready"], ONE + n + 1)
                w = rinv[:, r, :].rearrange("p (q h) -> p q h", q=TPB).unsqueeze(3).to_broadcast([P, TPB, REP, HD])
                i = dve.tensor_tensor(
                    t["act"][:, bass.ds(TPB * b, TPB), g * REP * HD:(g + 1) * REP * HD].rearrange("p u (h d) -> p u h d", d=HD),
                    o4[:, :, :, 0:HD], w, ALU.mult)
                i.then_inc(sm["attn_done"], 1)

            def slot(b, g, has_next, has_this, has_prev):
                n = G * b + g
                r, q = g % R, (g - 1) % R
                if has_prev:
                    turn(n - 1, q, 0)
                if has_this:
                    maxima(n, r, 0)
                if has_prev:
                    turn(n - 1, q, 2)
                if has_this:
                    maxima(n, r, 1)
                    maxima(n, r, 2)
                if has_next:
                    operand(n + 1, (g + 1) % R)
                if has_prev:
                    pb, pg = (b, g - 1) if g else (b - 1, G - 1)
                    finish(n - 1, q, pb, pg)

            def first():
                for r in range(R):
                    i = dve.memset(f32(kz[r][:]), 0.0)
                i.then_inc(sm["kz_zeroed"], 1)
                dve.wait_ge(sm["kz_zeroed"], ONE + 1)
                operand(0, 0)

            slots(dve, slot, first)

        @block.tensor
        def _(pe):
            def operand(n, r):
                pe.wait_ge(sm["stack_ready"], ONE + 4 * n + 4)
                wait(pe, sm["kz_ready"], n)
                for u in range(TPB):
                    for a in range(3):
                        m = pe.transpose(sk[:, u, a * P:(a + 1) * P], f32(stk[r][:, u, a * P:(a + 1) * P]), t["ident"][:])
                m.then_inc(sm["stackT_ready"], 1)

            def scores(n, r, a):
                if a == 0:
                    pe.wait_ge(sm["kz_ready"], ONE + n + 1)
                    heads, width = REP, P
                else:
                    heads, width = 2, S
                wait(pe, sm["probs_ready"], 3 * n - 2 + a)
                bank = sc[a][:].rearrange("p (h k) -> p h k", h=heads)
                pe.matmul(bank[:, :, width - P:width], t["identb"][:],
                          t["mask"][:].unsqueeze(1).to_broadcast([P, heads, P]), start=True, stop=False,
                          skip_group_check=True)
                for pair in ((0, 1) if a == 0 else (a - 1,)):
                    out = sc[a][:, pair * S:(pair + 1) * S] if a == 0 else sc[a][:]
                    lhs = qT[r][:, pair, 0:P] if a == 0 else qT[r][:, pair, P:S]
                    m = pe.matmul(out.rearrange("p (z k) -> p z k", z=2), lhs, kz[r][:, :, 0:width],
                                  start=False, stop=True, skip_group_check=True)
                m.then_inc(sm["scores_ready"], 1)

            def turn(n, r, c):
                pe.wait_ge(sm["probs_ready"], ONE + 3 * n + c + 1)
                if c == 1:
                    wait(pe, sm["pT_b"], n)
                else:
                    wait(pe, sm["pT_a"], 2 * n + c // 2)
                for k in range(4):
                    m = pe.transpose(tp[c % 2][:, k * P:(k + 1) * P], prob[r][:, c, k * P:(k + 1) * P], t["ident"][:])
                m.then_inc(sm["probsT_ready"], 1)

            def values(n, r, b, g):
                pe.wait_ge(sm["pT_a"], ONE + 2 * n + 2)
                pe.wait_ge(sm["pT_b"], ONE + n + 1)
                wait(pe, sm["attn_done"], n)
                v = [t["v"][:, TPB * b + u, g, :] for u in range(TPB)]
                for h in range(REP):
                    pe.matmul(o4[:, 0, h, :], pT[r][:, 0, h * P:(h + 1) * P], v[0], start=True, stop=True)
                    for u in range(TPB):
                        k = (2 * (h % 2) + u) * P
                        m = pe.matmul(o4[:, 1, h, :], pT[r][:, 1 + h // 2, k:k + P], v[u], start=u == 0,
                                      stop=u == TPB - 1)
                m.then_inc(sm["out_ready"], 1)

            def slot(b, g, has_next, has_this, has_prev):
                n = G * b + g
                if has_prev:
                    turn(n - 1, (g - 1) % R, 0)
                    turn(n - 1, (g - 1) % R, 1)
                if has_this:
                    scores(n, g % R, 0)
                if has_prev:
                    turn(n - 1, (g - 1) % R, 2)
                if has_this:
                    scores(n, g % R, 1)
                if has_next:
                    operand(n + 1, (g + 1) % R)
                if has_this:
                    scores(n, g % R, 2)
                if has_prev:
                    pb, pg = (b, g - 1) if g else (b - 1, G - 1)
                    values(n - 1, (g - 1) % R, pb, pg)

            slots(pe, slot, lambda: operand(0, 0))


def stage_out_proj(nc, io, t):
    with Scope(nc) as s:
        x = s.sb("op_x", [P, CH, D])
        at = [s.sb(f"op_at{c}", [P, D]) for c in range(CH)]
        ah = [s.sb(f"op_ah{c}", [P, KD, P], F32R) for c in range(CH)]
        al = [s.sb(f"op_al{c}", [P, KD, P], F32R) for c in range(CH)]
        st6 = s.sb("op_st6", [P, CH, 6])
        mv = s.sb("op_mv", [P, CH, 2])
        ve = s.sb("op_ve", [P, CH])
        aT = [s.ps(f"op_aT{c}", [P, D]) for c in range(CH)]
        y = [s.ps(f"op_y{c}", [P, D]) for c in range(CH)]
        x_loaded = [s.sem(f"op_x_loaded{c}") for c in range(CH)]
        names = ("copied", "turned", "hi", "lo", "y_ready", "x1_done", "stats", "moments", "eps", "rstd_ready",
                 "mean_kept", "passed_pool", "passed_dve")
        sm = {n: s.sem("op_" + n) for n in names}
        s.credit()
        block = s.ctx.enter_context(nc.Block())
        steps = NT // CH

        def turns(eng, first, turn):
            first()
            turn(0, True)
            with eng.Fori(1, steps - 1) as j:
                turn(j, True)
            turn(steps - 1, False)

        @block.sync
        def _(sp):
            def load(j):
                for c in range(CH):
                    n = CH * j + c
                    wait(sp, sm["x1_done"], n - CH + 1)
                    sp.dma_start(x[:, c, :], io["x_tiles"][n]).then_inc(x_loaded[c], 16)

            load(0)
            with sp.Fori(1, steps) as j:
                load(j)

        @block.gpsimd
        def _(pool):
            def copy(n, c):
                wait_apart(pool, sm["turned"], n - CH + 1, sm["passed_pool"])
                pool.tensor_copy(at[c][:], t["act"][:, n, :]).then_inc(sm["copied"], 1)

            def turn(j, ahead):
                for c in range(CH):
                    n = CH * j + c
                    if ahead:
                        copy(n + 2 * CH, c)
                    pool.wait_ge(sm["moments"], ONE + n + 1)
                    pool.tensor_tensor(ve[:, c:c + 1], mv[:, c, 1:2], t["eps"][:], ALU.add).then_inc(sm["eps"], 1)
                    wait_apart(pool, sm["eps"], n + 1, sm["passed_pool"])
                    pool.tensor_tensor(t["rstd1"][:, n, :], ve[:, c:c + 1], t["half"][:],
                                       ALU.pow).then_inc(sm["rstd_ready"], 1)
                    pool.tensor_copy(t["mean1"][:, n, :], mv[:, c, 0:1]).then_inc(sm["mean_kept"], 1)

            for n in range(2 * CH):
                copy(n, n % CH)
            with pool.Fori(0, steps - 2) as j:
                turn(j, True)
            turn(steps - 2, False)
            turn(steps - 1, False)

        @block.scalar
        def _(act):
            def split_hi(n, c):
                act.wait_ge(sm["turned"], ONE + n + 1)
                wait(act, sm["y_ready"], n - CH + 1)
                act.activation(ah[c][:].rearrange("p k n -> p (k n)"), aT[c][:], ACT.Copy).then_inc(sm["hi"], 1)

            def first():
                for c in range(CH):
                    split_hi(c, c)

            def turn(j, ahead):
                if ahead:
                    for c in range(CH):
                        split_hi(CH * (j + 1) + c, c)

            turns(act, first, turn)

        @block.vector
        def _(dve):
            def split_lo(n, c):
                dve.wait_ge(sm["hi"], ONE + n + 1)
                dve.tensor_tensor(al[c][:].rearrange("p k n -> p (k n)"), aT[c][:],
                                  f32(ah[c][:]).rearrange("p k n -> p (k n)"), ALU.subtract).then_inc(sm["lo"], 1)

            def first():
                for c in range(CH):
                    split_lo(c, c)

            def turn(j, ahead):
                for c in range(CH):
                    n = CH * j + c
                    dve.wait_ge(x_loaded[c], ONE + 16 * j + 16)
                    wait_apart(dve, sm["y_ready"], n + 1, sm["passed_dve"])
                    dve.tensor_tensor(t["act"][:, n, :], y[c][:], x[:, c, :], ALU.add).then_inc(sm["x1_done"], 1)
                    if ahead:
                        split_lo(n + CH, c)
                    wait_apart(dve, sm["x1_done"], n + 1, sm["passed_dve"])
                    dve.bn_stats(st6[:, c, :], t["act"][:, n, :]).then_inc(sm["stats"], 1)
                    wait(dve, sm["mean_kept"], n - CH + 1)
                    wait_apart(dve, sm["stats"], n + 1, sm["passed_dve"])
                    dve.bn_aggr(mv[:, c, :], st6[:, c, :]).then_inc(sm["moments"], 1)

            turns(dve, first, turn)

        @block.tensor
        def _(pe):
            def transposes(n, c):
                pe.wait_ge(sm["copied"], ONE + n + 1)
                wait(pe, sm["lo"], n - CH + 1)
                for k in range(KD):
                    m = pe.transpose(aT[c][:, k * P:(k + 1) * P], at[c][:, k * P:(k + 1) * P], t["ident"][:])
                m.then_inc(sm["turned"], 1)

            def first():
                for c in range(CH):
                    transposes(c, c)

            def turn(j, ahead):
                for c in range(CH):
                    n = CH * j + c
                    pe.wait_ge(sm["lo"], ONE + n + 1)
                    wait(pe, sm["x1_done"], n - CH + 1)
                    for k in range(KD):
                        m = split_passes(pe, y[c][:], (ah[c][:, k, :], al[c][:, k, :]),
                                         [w[:, k, :] for w in t["wo"]], k == 0, k == KD - 1)
                    m.then_inc(sm["y_ready"], 1)
                    if ahead:
                        transposes(n + CH, c)

            turns(pe, first, turn)


def stage_cross(nc, io, t):
    CB = 2
    NTT = D // P
    SCORE_BANK = (3, 0, 1, 2)
    with Scope(nc) as s:
        ctx_in = [s.sb(f"cx_ctx{c}", [P, TPB, D]) for c in range(CB)]
        res = [s.sb(f"cx_res{c}", [P, TPB, D]) for c in range(CB)]
        xin = [s.sb(f"cx_xin{c}", [P, TPB, D]) for c in range(CB)]
        R1 = [s.sb(f"cx_r1_{c}", [P, 8, D], F32R) for c in range(CB)]
        R2 = [s.sb(f"cx_r2_{c}", [P, 6, D], F32R) for c in range(CB)]
        R3 = [s.sb(f"cx_r3_{c}", [P, 4, D], F32R) for c in range(CB)]
        prob = [s.sb(f"cx_prob{c}", [P, NTT, D]) for c in range(CB)]
        lgT = [s.sb(f"cx_lgT{c}", [E, TPB, P]) for c in range(CB)]
        bank = [[s.ps(f"cx_bank{c}_{i}", [P, 512]) for i in range(4)] for c in range(CB)]
        st6 = s.sb("cx_st6", [P, CB, TPB, 6])
        mv = s.sb("cx_mv", [P, CB, TPB, 2])
        ve = s.sb("cx_ve", [P, CB, TPB])
        rstd = s.sb("cx_rstd", [P, CB, TPB])
        nmx = s.sb("cx_nmx", [P, CB, NTT])
        rsum = s.sb("cx_rsum", [P, CB, NTT])
        rinv = s.sb("cx_rinv", [P, CB, NTT])
        pst = s.sb("cx_pst", [P, CB, 6])
        pmv = s.sb("cx_pmv", [P, CB, 2])
        psq = s.sb("cx_psq", [P, CB])
        gmv = s.sb("cx_gmv", [P, CB, 2])
        gsq = s.sb("cx_gsq", [P, CB])
        gve = s.sb("cx_gve", [P, CB])
        gvar = s.sb("cx_gvar", [P, CB])
        grstd = s.sb("cx_grstd", [P, CB])
        ctx_loaded = [s.sem(f"ctx_loaded{c}") for c in range(CB)]
        stored = [s.sem(f"cx_stored{c}") for c in range(CB)]
        names = ("xin", "ctx_hi", "ctx_lo", "ctx_res", "xin_hi", "xin_lo", "theta", "phi", "g", "theta_hi", "theta_lo",
                 "phi_hi", "phi_lo", "g_hi", "g_lo", "scores", "neg_max", "exp", "rinv", "norm", "turned",
                 "pT_hi", "pT_lo", "tx", "tx_kept", "row_stats", "row_moments", "row_sq", "row_m2", "all_moments",
                 "gmv", "gsq", "gvar", "gve", "grstd", "centred", "scaled", "h_hi", "h_lo", "out", "x2", "stats",
                 "moments", "eps", "rstd", "xn3", "x3T", "x3_hi", "x3_lo", "lgT", "lgT_kept", "logits",
                 "logits_kept", "passed_dve", "passed_pe", "passed_pool")
        sm = {n: s.sem("cx_" + n) for n in names}
        s.credit()
        block = s.ctx.enter_context(nc.Block())
        steps = B // CB
        chains = range(CB)
        r2_of = {"theta": 0, "phi": 2, "g": 4}
        bank_of = {"theta": 2, "phi": 3, "g": 2}
        bias_of = {"theta": "theta_b", "phi": "phi_b", "g": None}

        def turns(eng, front, middle, tail):
            front(0)
            with eng.Fori(0, steps - 1) as j:
                middle(j)
                tail(j, True)
            middle(steps - 1)
            tail(steps - 1, False)

        @block.sync
        def _(sp):
            def load(j):
                for c in chains:
                    wait(sp, sm["ctx_res"], CB * j + c + 1 - CB)
                    sp.dma_start(ctx_in[c][:], io["ctx_tiles"][CB * j + c]).then_inc(ctx_loaded[c], 16)

            def store(j):
                for c in chains:
                    n = CB * j + c
                    sp.wait_ge(sm["x2"], ONE + TPB * (n + 1))
                    sp.dma_start(io["x2_tiles"][n], res[c][:]).then_inc(stored[c], 16)
                for c in chains:
                    n = CB * j + c
                    sp.wait_ge(sm["xn3"], ONE + TPB * (n + 1))
                    sp.dma_start(io["xn3_tiles"][n], prob[c][:, 0:TPB, :]).then_inc(stored[c], 16)

            def tail(j, ahead):
                if ahead:
                    load(j + 1)
                store(j)

            turns(sp, load, lambda j: None, tail)
            for c in chains:
                sp.wait_ge(stored[c], ONE + 32 * steps)

        @block.gpsimd
        def _(pool):
            def front(j):
                for c in chains:
                    n = CB * j + c
                    wait_apart(pool, sm["ctx_hi"], n + 1, sm["passed_pool"])
                    pool.tensor_tensor(R1[c][:, 2:4, :], ctx_in[c][:], f32(R1[c][:, 0:2, :]),
                                       ALU.subtract).then_inc(sm["ctx_lo"], 1)

            def middle(j):
                for c in chains:
                    n = CB * j + c
                    wait_apart(pool, stored[c], 32 * j, sm["passed_pool"])
                    pool.tensor_tensor(res[c][:], ctx_in[c][:], t["act"][:, bass.ds(TPB * n, TPB), :],
                                       ALU.add).then_inc(sm["ctx_res"], 1)

            def tail(j, ahead):
                for c in chains:
                    n = CB * j + c
                    pool.wait_ge(sm["gvar"], ONE + n + 1)
                    pool.tensor_tensor(gve[:, c:c + 1], gvar[:, c:c + 1], t["eps"][:], ALU.add).then_inc(sm["gve"], 1)
                    pool.wait_ge(sm["gve"], ONE + n + 1)
                    pool.tensor_tensor(grstd[:, c:c + 1], gve[:, c:c + 1], t["half"][:], ALU.pow)\
                        .then_inc(sm["grstd"], 1)
                if ahead:
                    front(j + 1)
                for c in chains:
                    n = CB * j + c
                    pool.wait_ge(sm["moments"], ONE + TPB * (n + 1))
                    pool.tensor_tensor(ve[:, c, :], mv[:, c, :, 1], t["eps"][:].to_broadcast([P, TPB]),
                                       ALU.add).then_inc(sm["eps"], 1)
                    pool.wait_ge(sm["eps"], ONE + n + 1)
                    pool.tensor_tensor(rstd[:, c, :], ve[:, c, :], t["half"][:].to_broadcast([P, TPB]),
                                       ALU.pow).then_inc(sm["rstd"], 1)

            turns(pool, front, middle, tail)

        @block.scalar
        def _(act):
            def ctx_hi(j):
                for c in chains:
                    n = CB * j + c
                    act.wait_ge(ctx_loaded[c], ONE + 16 * j + 16)
                    wait(act, sm["tx"], n + 1 - CB)
                    act.activation(R1[c][:, 0:2, :], ctx_in[c][:], ACT.Copy).then_inc(sm["ctx_hi"], 1)

            def xin_hi(j, c):
                n = CB * j + c
                act.wait_ge(sm["xin"], ONE + TPB * (n + 1))
                wait(act, sm["tx"], n + 1 - CB)
                act.activation(R1[c][:, 4:6, :], xin[c][:], ACT.Copy).then_inc(sm["xin_hi"], 1)

            def latent_hi(j, name):
                r2, at, bias = r2_of[name], bank_of[name], bias_of[name]
                for c in chains:
                    n = CB * j + c
                    act.wait_ge(sm[name], ONE + n + 1)
                    if bias:
                        act.activation(R2[c][:, r2, :], bank[c][at][:], ACT.Identity, bias=t[bias][:])\
                            .then_inc(sm[name + "_hi"], 1)
                    else:
                        act.activation(R2[c][:, r2, :], bank[c][at][:], ACT.Copy).then_inc(sm[name + "_hi"], 1)

            def front(j):
                ctx_hi(j)
                for c in chains:
                    xin_hi(j, c)
                for name in ("phi", "g", "theta"):
                    latent_hi(j, name)

            def middle(j):
                for c in chains:
                    n = CB * j + c
                    act.wait_ge(stored[c], ONE + 32 * j)
                    for i in range(NTT):
                        act.wait_ge(sm["neg_max"], ONE + NTT * n + i + 1)
                        act.activation(prob[c][:, i, :], bank[c][SCORE_BANK[i]][:], ACT.Exp, bias=nmx[:, c, i:i + 1],
                                       accum_out=rsum[:, c, i:i + 1]).then_inc(sm["exp"], 1)
                for c in chains:
                    n = CB * j + c
                    for i in range(NTT):
                        act.wait_ge(sm["turned"], ONE + NTT * n + i + 1)
                        act.activation(R1[c][:, i, :], bank[c][i][:], ACT.Copy).then_inc(sm["pT_hi"], 1)

            def tail(j, ahead):
                for c in chains:
                    n = CB * j + c
                    act.wait_ge(sm["tx"], ONE + n + 1)
                    act.activation(prob[c][:, 0, :], bank[c][0][:], ACT.Identity, bias=t["g_b"][:])\
                        .then_inc(sm["tx_kept"], 1)
                    if ahead:
                        xin_hi(j + 1, c)
                if ahead:
                    ctx_hi(j + 1)
                    latent_hi(j + 1, "phi")
                for c in chains:
                    n = CB * j + c
                    act.wait_ge(sm["scaled"], ONE + n + 1)
                    act.activation(R3[c][:, 0, :], prob[c][:, 2, :], ACT.Relu).then_inc(sm["h_hi"], 1)
                if ahead:
                    latent_hi(j + 1, "g")
                    latent_hi(j + 1, "theta")
                for c in chains:
                    n = CB * j + c
                    for u in range(TPB):
                        act.wait_ge(sm["x3T"], ONE + TPB * n + u + 1)
                        act.activation(R3[c][:, u, :], bank[c][u][:], ACT.Copy).then_inc(sm["x3_hi"], 1)
                for c in chains:
                    n = CB * j + c
                    act.wait_ge(sm["lgT"], ONE + n + 1)
                    act.activation(lgT[c][:], bank[c][0][0:E, 0:TPB * P].rearrange("e (u n) -> e u n", u=TPB),
                                   ACT.Copy).then_inc(sm["lgT_kept"], 1)

            turns(act, front, middle, tail)

        @block.vector
        def _(dve):
            def norm_input(j, c):
                n = CB * j + c
                for u in range(TPB):
                    dve.tensor_scalar(xin[c][:, u, :], t["act"][:, TPB * n + u, :],
                                      t["mean1"][:, TPB * n + u, :], t["rstd1"][:, TPB * n + u, :],
                                      ALU.subtract, ALU.mult).then_inc(sm["xin"], 1)

            def xin_lo(j, c):
                n = CB * j + c
                dve.wait_ge(sm["xin_hi"], ONE + n + 1)
                dve.tensor_tensor(R1[c][:, 6:8, :], xin[c][:], f32(R1[c][:, 4:6, :]), ALU.subtract)\
                    .then_inc(sm["xin_lo"], 1)

            def latent_lo(j, name):
                r2, at, bias = r2_of[name], bank_of[name], bias_of[name]
                for c in chains:
                    n = CB * j + c
                    dve.wait_ge(sm[name + "_hi"], ONE + n + 1)
                    if bias:
                        dve.scalar_tensor_tensor(R2[c][:, r2 + 1, :], bank[c][at][:], t[bias][:],
                                                 f32(R2[c][:, r2, :]), ALU.add, ALU.subtract)\
                            .then_inc(sm[name + "_lo"], 1)
                    else:
                        dve.tensor_tensor(R2[c][:, r2 + 1, :], bank[c][at][:], f32(R2[c][:, r2, :]),
                                          ALU.subtract).then_inc(sm[name + "_lo"], 1)

            def front(j):
                for c in chains:
                    norm_input(j, c)
                for c in chains:
                    xin_lo(j, c)
                for name in ("phi", "g", "theta"):
                    latent_lo(j, name)

            def middle(j):
                def maximum(c, i):
                    n = CB * j + c
                    dve.wait_ge(sm["scores"], ONE + NTT * n + i + 1)
                    dve.tensor_reduce(nmx[:, c, i:i + 1], bank[c][SCORE_BANK[i]][:], AX.X, ALU.max, negate=True)\
                        .then_inc(sm["neg_max"], 1)

                def normalise(c, i):
                    n = CB * j + c
                    dve.wait_ge(sm["exp"], ONE + NTT * n + i + 1)
                    dve.reciprocal(rinv[:, c, i:i + 1], rsum[:, c, i:i + 1]).then_inc(sm["rinv"], 1)
                    dve.wait_ge(sm["rinv"], ONE + NTT * n + i + 1)
                    dve.tensor_scalar(prob[c][:, i, :], prob[c][:, i, :], rinv[:, c, i:i + 1], None, ALU.mult)\
                        .then_inc(sm["norm"], 1)

                for i in range(NTT):
                    maximum(0, i)
                for c in chains:
                    for i in range(NTT):
                        if c + 1 < CB:
                            maximum(c + 1, i)
                        normalise(c, i)
                for c in chains:
                    n = CB * j + c
                    for i in range(NTT):
                        dve.wait_ge(sm["pT_hi"], ONE + NTT * n + i + 1)
                        dve.tensor_tensor(R1[c][:, NTT + i, :], bank[c][i][:], f32(R1[c][:, i, :]), ALU.subtract)\
                            .then_inc(sm["pT_lo"], 1)

            def tail(j, ahead):
                if ahead:
                    for c in chains:
                        norm_input(j + 1, c)
                for c in chains:
                    n = CB * j + c
                    dve.wait_ge(sm["tx_kept"], ONE + n + 1)
                    dve.bn_stats(pst[:, c, :], prob[c][:, 0, :]).then_inc(sm["row_stats"], 1)
                    wait_apart(dve, sm["row_stats"], n + 1, sm["passed_dve"])
                    dve.bn_aggr(pmv[:, c, :], pst[:, c, :]).then_inc(sm["row_moments"], 1)
                    dve.wait_ge(sm["row_moments"], ONE + n + 1)
                    dve.tensor_tensor(psq[:, c:c + 1], pmv[:, c, 0:1], pmv[:, c, 0:1], ALU.mult)\
                        .then_inc(sm["row_sq"], 1)
                    dve.wait_ge(sm["row_sq"], ONE + n + 1)
                    dve.tensor_tensor(pmv[:, c, 1:2], pmv[:, c, 1:2], psq[:, c:c + 1], ALU.add)\
                        .then_inc(sm["row_m2"], 1)
                    if ahead:
                        xin_lo(j + 1, c)
                for c in chains:
                    n = CB * j + c
                    dve.wait_ge(sm["all_moments"], ONE + n + 1)
                    dve.tensor_copy(gmv[:, c, :], bank[c][1][:, 0:2]).then_inc(sm["gmv"], 1)
                    dve.wait_ge(sm["gmv"], ONE + n + 1)
                    dve.tensor_tensor(gsq[:, c:c + 1], gmv[:, c, 0:1], gmv[:, c, 0:1], ALU.mult)\
                        .then_inc(sm["gsq"], 1)
                    dve.wait_ge(sm["gsq"], ONE + n + 1)
                    dve.tensor_tensor(gvar[:, c:c + 1], gmv[:, c, 1:2], gsq[:, c:c + 1], ALU.subtract)\
                        .then_inc(sm["gvar"], 1)
                for c in chains:
                    n = CB * j + c
                    dve.scalar_tensor_tensor(prob[c][:, 1, :], prob[c][:, 0, :], gmv[:, c, 0:1], t["gamma"][:],
                                             ALU.subtract, ALU.mult).then_inc(sm["centred"], 1)
                for c in chains:
                    n = CB * j + c
                    dve.wait_ge(sm["grstd"], ONE + n + 1)
                    dve.wait_ge(sm["centred"], ONE + n + 1)
                    dve.scalar_tensor_tensor(prob[c][:, 2, :], prob[c][:, 1, :], grstd[:, c:c + 1], t["beta"][:],
                                             ALU.mult, ALU.add).then_inc(sm["scaled"], 1)
                if ahead:
                    latent_lo(j + 1, "phi")
                for c in chains:
                    n = CB * j + c
                    dve.wait_ge(sm["h_hi"], ONE + n + 1)
                    dve.scalar_tensor_tensor(R3[c][:, 1, :], prob[c][:, 2, :], 0.0, f32(R3[c][:, 0, :]),
                                             ALU.max, ALU.subtract).then_inc(sm["h_lo"], 1)
                if ahead:
                    latent_lo(j + 1, "g")
                for c in chains:
                    n = CB * j + c
                    dve.wait_ge(sm["ctx_res"], ONE + n + 1)
                    for u in range(TPB):
                        dve.wait_ge(sm["out"], ONE + TPB * n + u + 1)
                        dve.scalar_tensor_tensor(res[c][:, u, :], bank[c][u][:], t["out_b"][:, u:u + 1],
                                                 res[c][:, u, :], ALU.add, ALU.add).then_inc(sm["x2"], 1)
                for c in chains:
                    n = CB * j + c
                    for u in range(TPB):
                        dve.wait_ge(sm["x2"], ONE + TPB * n + u + 1)
                        dve.bn_stats(st6[:, c, u, :], res[c][:, u, :]).then_inc(sm["stats"], 1)
                    wait_apart(dve, sm["stats"], TPB * (n + 1), sm["passed_dve"])
                    for u in range(TPB):
                        dve.bn_aggr(mv[:, c, u, :], st6[:, c, u, :]).then_inc(sm["moments"], 1)
                for c in chains:
                    n = CB * j + c
                    dve.wait_ge(sm["rstd"], ONE + n + 1)
                    for u in range(TPB):
                        dve.tensor_scalar(prob[c][:, u, :], res[c][:, u, :], mv[:, c, u, 0:1], rstd[:, c, u:u + 1],
                                          ALU.subtract, ALU.mult).then_inc(sm["xn3"], 1)
                if ahead:
                    latent_lo(j + 1, "theta")
                for c in chains:
                    n = CB * j + c
                    for u in range(TPB):
                        dve.wait_ge(sm["x3_hi"], ONE + TPB * n + u + 1)
                        dve.tensor_tensor(R3[c][:, 2 + u, :], bank[c][u][:], f32(R3[c][:, u, :]),
                                          ALU.subtract).then_inc(sm["x3_lo"], 1)
                for c in chains:
                    n = CB * j + c
                    wait_apart(dve, sm["logits"], n + 1, sm["passed_dve"])
                    dve.tensor_copy(t["logits"][:, bass.ds(TPB * n, TPB), :],
                                    bank[c][1][:, 0:TPB * E].rearrange("p (u e) -> p u e", u=TPB))\
                        .then_inc(sm["logits_kept"], 1)

            turns(dve, front, middle, tail)

        @block.tensor
        def _(pe):
            def theta(j):
                for c in chains:
                    n = CB * j + c
                    pe.wait_ge(sm["ctx_lo"], ONE + n + 1)
                    pe.wait_ge(sm["g_lo"], ONE + n + 1)
                    for k in range(TPB):
                        m = split_passes(pe, bank[c][2][:], [w[:, k, :] for w in t["theta_w"]],
                                         (R1[c][:, k, :], R1[c][:, 2 + k, :]), k == 0, k == TPB - 1)
                    m.then_inc(sm["theta"], 1)

            def phi(j):
                for c in chains:
                    n = CB * j + c
                    pe.wait_ge(sm["xin_lo"], ONE + n + 1)
                    for k in range(TPB):
                        m = split_passes(pe, bank[c][3][:], [w[:, k, :] for w in t["phi_w"]],
                                         (R1[c][:, 4 + k, :], R1[c][:, 6 + k, :]), k == 0, k == TPB - 1)
                    m.then_inc(sm["phi"], 1)

            def g(j):
                for c in chains:
                    n = CB * j + c
                    for i in range(NTT):
                        for k in range(TPB):
                            m = split_passes(pe, bank[c][2][:, i * P:(i + 1) * P],
                                             (R1[c][:, 4 + k, i * P:(i + 1) * P], R1[c][:, 6 + k, i * P:(i + 1) * P]),
                                             [w[:, k, :] for w in t["g_w"]], k == 0, k == TPB - 1)
                    m.then_inc(sm["g"], 1)

            def front(j):
                phi(j)
                g(j)
                theta(j)

            def middle(j):
                for c in chains:
                    n = CB * j + c
                    pe.wait_ge(sm["theta_lo"], ONE + n + 1)
                    pe.wait_ge(sm["phi_lo"], ONE + n + 1)
                    for i in range(NTT):
                        if i == 1:
                            wait(pe, sm["lgT_kept"], n + 1 - CB)
                            wait(pe, sm["logits_kept"], n + 1 - CB)
                        m = split_passes(pe, bank[c][SCORE_BANK[i]][:],
                                         (R2[c][:, 0, i * P:(i + 1) * P], R2[c][:, 1, i * P:(i + 1) * P]),
                                         (R2[c][:, 2, :], R2[c][:, 3, :]))
                        m.then_inc(sm["scores"], 1)
                for c in chains:
                    n = CB * j + c
                    for i in range(NTT):
                        pe.wait_ge(sm["norm"], ONE + NTT * (n + 1))
                        for k in range(NTT):
                            m = pe.transpose(bank[c][i][:, k * P:(k + 1) * P], prob[c][:, k, i * P:(i + 1) * P],
                                             t["ident"][:])
                        m.then_inc(sm["turned"], 1)
                for c in chains:
                    n = CB * j + c
                    for i in range(NTT):
                        pe.wait_ge(sm["pT_lo"], ONE + NTT * n + i + 1)
                        m = split_passes(pe, bank[c][0][:],
                                         (R2[c][:, 4, i * P:(i + 1) * P], R2[c][:, 5, i * P:(i + 1) * P]),
                                         (R1[c][:, i, :], R1[c][:, NTT + i, :]), i == 0, i == NTT - 1)
                    m.then_inc(sm["tx"], 1)

            def tail(j, ahead):
                for c in chains:
                    n = CB * j + c
                    pe.wait_ge(sm["row_m2"], ONE + n + 1)
                    pe.matmul(bank[c][1][:, 0:2], t["avg"][:], pmv[:, c, :], start=True, stop=True)\
                        .then_inc(sm["all_moments"], 1)
                if ahead:
                    phi(j + 1)
                    g(j + 1)
                for c in chains:
                    n = CB * j + c
                    pe.wait_ge(sm["h_lo"], ONE + n + 1)
                    for u in range(TPB):
                        split_passes(pe, bank[c][u][:], [w[:, u * P:(u + 1) * P] for w in t["out_w"]],
                                     (R3[c][:, 0, :], R3[c][:, 1, :])).then_inc(sm["out"], 1)
                if ahead:
                    theta(j + 1)
                for c in chains:
                    n = CB * j + c
                    for u in range(TPB):
                        pe.wait_ge(sm["xn3"], ONE + TPB * n + u + 1)
                        for k in range(KD):
                            m = pe.transpose(bank[c][u][:, k * P:(k + 1) * P], prob[c][:, u, k * P:(k + 1) * P],
                                             t["ident"][:])
                        m.then_inc(sm["x3T"], 1)
                for c in chains:
                    n = CB * j + c
                    pe.wait_ge(sm["x3_lo"], ONE + TPB * (n + 1))
                    for k in range(KD):
                        m = split_passes(pe, bank[c][0][0:E, 0:TPB * P].rearrange("e (u n) -> e u n", u=TPB),
                                         [w[:, k, :] for w in t["router_w"]],
                                         [R3[c][:, q:q + TPB, k * P:(k + 1) * P] for q in (0, 2)], k == 0, k == KD - 1)
                    m.then_inc(sm["lgT"], 1)
                for c in chains:
                    n = CB * j + c
                    wait_apart(pe, sm["lgT_kept"], n + 1, sm["passed_pe"])
                    for u in range(TPB):
                        m = pe.transpose(bank[c][1][:, u * E:(u + 1) * E], lgT[c][:, u, :], t["ident"][0:E, 0:E])
                    m.then_inc(sm["logits"], 1)

            turns(pe, front, middle, tail)


def stage_route(nc, io, t):
    with Scope(nc) as s:
        W = [P, NT, E]
        lg = t["logits"]
        red = s.sb("rt_red", [P, 4, NT])
        ex = s.sb("rt_ex", W)
        prob = s.sb("rt_prob", W)
        eq = s.sb("rt_eq", W)
        hot = [s.sb(f"rt_hot{k}", W) for k in range(TOPK)]
        chosen = s.sb("rt_chosen", W)
        scan = [s.sb(f"rt_scan{k}", W) for k in range(2)]
        total = s.sb("rt_total", W)
        place = s.sb("rt_place", W)
        kept = s.sb("rt_kept", W)
        tmp = s.sb("rt_tmp", W)
        ei = s.sb("rt_ei", [P, E], I32)
        ef = s.sb("rt_ef", [P, E])
        em = s.sb("rt_em", [P, E])
        ec = s.sb("rt_ec", [P, E])
        tokenf = s.sb("rt_tokenf", [P, NT])
        dump = s.sb("rt_dump", [P, NT])
        has = s.sb("rt_has", [P, NT])
        slot = s.sb("rt_slot", [P, NT])
        gate = s.sb("rt_gate", [P, TOPK, NT])
        empty = s.sb("rt_empty", [ST, P, 2], I32)
        pp = s.ps("rt_pp", [P, 512])
        names = ("iota", "empty", "cleared", "exp_in", "exp", "dve", "counts")
        sm = {n: s.sem("rt_" + n) for n in names}
        s.credit()
        block = s.ctx.enter_context(nc.Block())

        @block.sync
        def _(sp):
            sp.wait_ge(sm["empty"], ONE + 2)
            sp.dma_start(io["table"][0:SLOTS, :].rearrange("(a b) o -> a (b o)", b=P),
                         empty[:].rearrange("a b o -> a (b o)")).then_inc(sm["cleared"], 16)
            sp.wait_ge(sm["cleared"], ONE + 16)

        @block.gpsimd
        def _(pool):
            pool.iota(ei[:], pattern=[[1, E]], base=0, channel_multiplier=0).then_inc(sm["iota"], 1)
            for k in range(TOPK):
                pool.iota(t["choice"][:, k, :, 0], pattern=[[P, NT]], base=0, channel_multiplier=1)\
                    .then_inc(sm["iota"], 1)
            pool.iota(empty[:, :, 0], pattern=[[0, P]], base=B * S, channel_multiplier=0).then_inc(sm["empty"], 1)
            pool.iota(empty[:, :, 1], pattern=[[0, P]], base=0, channel_multiplier=0).then_inc(sm["empty"], 1)

        @block.scalar
        def _(act):
            act.wait_ge(sm["exp_in"], ONE + 1)
            act.activation(ex[:], ex[:], ACT.Exp).then_inc(sm["exp"], 1)

        @block.vector
        def _(dve):
            count = [0]

            def link(i):
                count[0] += 1
                i.then_inc(sm["dve"], 1)
                dve.wait_ge(sm["dve"], ONE + count[0])

            def tiles(ap):
                return ap.unsqueeze(2).to_broadcast(W)

            def experts(ap):
                return ap.unsqueeze(1).to_broadcast(W)

            TT, TS, RED = dve.tensor_tensor, dve.tensor_scalar, dve.tensor_reduce
            link(RED(red[:, 0, :], lg[:], AX.X, ALU.max))
            TT(ex[:], lg[:], tiles(red[:, 0, :]), ALU.subtract).then_inc(sm["exp_in"], 1)
            dve.wait_ge(sm["iota"], ONE + 1 + TOPK)
            dve.tensor_copy(ef[:], ei[:])
            link(dve.tensor_copy(tokenf[:], t["choice"][:, 0, :, 0]))
            TS(em[:], ef[:], float(-E), None, ALU.add)
            TS(ec[:], ef[:], float(CAP), None, ALU.mult)
            dve.wait_ge(sm["exp"], ONE + 1)
            link(RED(red[:, 1, :], ex[:], AX.X, ALU.add))
            link(dve.reciprocal(red[:, 2, :], red[:, 1, :]))
            link(TT(prob[:], ex[:], tiles(red[:, 2, :]), ALU.mult))
            for k in range(TOPK):
                link(RED(gate[:, k, :], prob[:], AX.X, ALU.max))
                link(TT(eq[:], prob[:], tiles(gate[:, k, :]), ALU.is_equal))
                link(TT(eq[:], eq[:], experts(em[:]), ALU.mult))
                link(RED(red[:, 3, :], eq[:], AX.X, ALU.min))
                link(TT(hot[k][:], tiles(red[:, 3, :]), experts(em[:]), ALU.is_equal))
                if k == 0:
                    link(dve.scalar_tensor_tensor(prob[:], hot[k][:], -2.0, prob[:], ALU.mult, ALU.add))
            TT(chosen[:], hot[0][:], hot[1][:], ALU.add).then_inc(sm["counts"], 1)
            dve.wait_ge(sm["counts"], ONE + 2)
            flat = [x[:].rearrange("p a e -> p (a e)") for x in (total, scan[0])]
            dve.tensor_copy(flat[0], pp[:, NT * E:2 * NT * E])
            link(dve.tensor_copy(flat[1], pp[:, NT * E:2 * NT * E]))
            step, a = 1, 0
            while step < NT:
                TT(scan[1 - a][:, step:, :], scan[a][:, step:, :], scan[a][:, :NT - step, :], ALU.add)
                link(dve.tensor_copy(scan[1 - a][:, :step, :], scan[a][:, :step, :]))
                step, a = 2 * step, 1 - a
            link(TT(place[:], scan[a][:], total[:], ALU.subtract))
            link(TT(place[:], place[:], pp[:, 0:NT * E].rearrange("p (a e) -> p a e", e=E), ALU.add))
            TS(kept[:], place[:], float(CAP), None, ALU.is_lt)
            link(TT(place[:], place[:], experts(ec[:]), ALU.add))
            link(TT(place[:], place[:], kept[:], ALU.mult))
            for k in range(TOPK):
                link(TT(tmp[:], hot[k][:], kept[:], ALU.mult))
                link(RED(has[:], tmp[:], AX.X, ALU.add))
                link(TT(tmp[:], hot[k][:], place[:], ALU.mult))
                link(RED(slot[:], tmp[:], AX.X, ALU.add))
                link(TS(dump[:], tokenf[:], float(SLOTS + k * B * S), None, ALU.add))
                dve.tensor_copy(t["choice"][:, k, :, 1].bitcast(F32), gate[:, k, :])
                link(TS(has[:], has[:], -1.0, 1.0, ALU.mult, ALU.add))
                link(TT(dump[:], dump[:], has[:], ALU.mult))
                link(TT(slot[:], slot[:], dump[:], ALU.add))
                link(dve.tensor_copy(t["choice_slot"][:, k, :], slot[:]))

        @block.tensor
        def _(pe):
            pe.wait_ge(sm["counts"], ONE + 1)
            c = chosen[:].rearrange("p a e -> p (a e)")
            pe.matmul(pp[:, 0:NT * E], t["upper"][:], c, start=True, stop=True)
            pe.matmul(pp[:, NT * E:2 * NT * E], t["ones"][:], c, start=True, stop=True).then_inc(sm["counts"], 1)


def stage_experts(nc, io, t):
    with Scope(nc) as s:
        RW = 2
        HB = BLK // 2
        w1 = [s.sb(f"ex_w1_{p}", [P, NF, KD, P], F32R) for p in "hl"]
        w2 = [s.sb(f"ex_w2_{p}", [P, NF, D], F32R) for p in "hl"]
        raw = s.sb("ex_raw", [P, RW, 2, D])
        xT = [[s.sb(f"ex_xT{b}{p}", [P, KD, BLK], F32R) for p in "hl"] for b in range(2)]
        h = [[s.sb(f"ex_h{r}{p}", [P, 2, HB], F32R) for p in "hl"] for r in range(2)]
        xg = [s.sb(f"ex_xg{r}", [P, D]) for r in range(2)]
        gi = [s.sb(f"ex_gi{r}", [P, 1], I32) for r in range(2)]
        ys = s.sb("ex_ys", [P, BT, D])
        rows_in = s.sb("ex_rows_in", [P, BT], I32)
        rows_out = s.sb("ex_rows_out", [P, BT], I32)
        slot_gather = s.sb("ex_slot_gather", [P, ST + BT + 2], I32)
        slot_scatter = s.sb("ex_slot_scatter", [P, ST], I32)
        slot_gate = s.sb("ex_slot_gate", [P, ST])
        filled = s.sb("ex_filled", [P, ST])
        tab = ys[0:ST, 0, 0:2 * P].bitcast(I32)
        tabf = ys[0:ST, 1, 0:2 * P].rearrange("a (o b) -> a o b", o=2)
        hid = s.ps("ex_hid", [P, 2, 512])
        acc = [s.ps(f"ex_acc{i}", [P, D]) for i in range(BT)]
        xb = s.ps("ex_xb", [P, D])
        raw_loaded = [s.sem(f"raw_loaded{r}") for r in range(RW)]
        gathered = [s.zero_sem(f"gathered{r}") for r in range(2)]
        early = [s.zero_sem(f"gathered_early{i}") for i in range(2, BT)]
        early_of_ring = [len(range(2 + (2 + r) % 2, BT, 2)) for r in range(2)]
        choices_out, rows_loaded, rows_stored = (
            s.zero_sem("ex_" + n) for n in ("choices_out", "rows_loaded", "rows_stored"))
        names = ("table_loaded", "table_f", "table_T", "padded", "filled", "slots_ready", "w_hi", "w_lo", "idx_col",
                 "row_cols", "x_turned", "x_hi", "x_lo", "hidden", "h_hi", "h_lo", "used", "rows_done",
                 "passed_pool", "passed_dve")
        sm = {n: s.sem("ex_" + n) for n in names}
        s.credit()
        block = s.ctx.enter_context(nc.Block())

        TURN = {3 * i: i for i in range(BT)}

        def turning_bank(m, i):
            return acc[i] if isinstance(m, int) and m == 0 else xb

        def refilled(e, b, f):
            if b == 1 and f >= 2 and not (isinstance(e, int) and e == E - 1):
                return e + 1, f - 2
            if b == 0 and f < 2 and not (isinstance(e, int) and e == 0):
                return e, NF - 2 + f
            return None

        def experts(eng, expert):
            expert(0)
            with eng.Fori(1, E - 1) as e:
                expert(e)
            expert(E - 1)

        @block.sync
        def _(sp):
            def load(e, f):
                wait(sp, sm["w_lo"], 2 * (NF * e + f - RW) + 2 if f >= RW else 2 * NF * e)
                sp.dma_start(raw[:, f % RW, 0, :], io["w1_tiles"][NF * e + f]).then_inc(raw_loaded[f % RW], 16)
                sp.dma_start(raw[:, f % RW, 1, :], io["w2_tiles"][NF * e + f]).then_inc(raw_loaded[f % RW], 16)

            for f in range(NF):
                load(0, f)
            sp.wait_ge(choices_out, 16 * TOPK * NT)
            sp.dma_start(tab, io["table"][0:SLOTS, :].rearrange("(a b) o -> a (b o)", b=P))\
                .then_inc(sm["table_loaded"], 16)
            with sp.Fori(1, E) as e:
                for f in range(NF):
                    load(e, f)

        @block.gpsimd
        def _(pool):
            def gather(n, r, first):
                if not first:
                    wait_apart(pool, sm["x_turned"], n - 1, sm["passed_pool"])
                pool.tensor_copy(gi[r][:], slot_gather[:, bass.ds(n, 1)]).then_inc(sm["idx_col"], 1)
                wait_apart(pool, sm["idx_col"], n + 1, sm["passed_pool"])
                pool.indirect_dma_start(xg[r][:], None, io["xn3"][:, :], bass.IndirectOffsetOnAxis(gi[r][:], 0))\
                    .then_inc(gathered[r], 16)

            for k in range(TOPK):
                for n in range(NT):
                    pool.indirect_dma_start(io["table"][:, :],
                                            bass.IndirectOffsetOnAxis(t["choice_slot"][:, k, n:n + 1], 0),
                                            t["choice"][:, k, n, :], None).then_inc(choices_out, 16)
            pool.wait_ge(sm["slots_ready"], ONE + 1)
            gather(0, 0, True)
            gather(1, 1, True)
            for i in range(2, BT):
                pool.tensor_copy(rows_in[:, i:i + 1], slot_gather[:, i:i + 1]).then_inc(sm["idx_col"], 1)
                pool.wait_ge(sm["idx_col"], ONE + i + 1)
                pool.indirect_dma_start(ys[:, i, :], None, io["xn3"][:, :],
                                        bass.IndirectOffsetOnAxis(rows_in[:, i:i + 1], 0)).then_inc(early[i - 2], 16)
            for i in range(BT, BT + 2):
                gather(i, i % 2, False)
            with pool.Fori(0, E) as e:
                for b in range(2):
                    m = 2 * e + b
                    pool.tensor_copy(rows_in[:], slot_gather[:, bass.ds(BT * m, BT)]).then_inc(sm["row_cols"], 1)
                    pool.tensor_copy(rows_out[:], slot_scatter[:, bass.ds(BT * m, BT)]).then_inc(sm["row_cols"], 1)
                    wait_apart(pool, sm["row_cols"], 2 * m + 2, sm["passed_pool"])
                    for i in range(BT):
                        pool.indirect_dma_start(ys[:, i, :], None, io["out_rows"][:, :],
                                                bass.IndirectOffsetOnAxis(rows_in[:, i:i + 1], 0))\
                            .then_inc(rows_loaded, 16)
                    for i in range(BT):
                        gather(BT * (m + 1) + 2 + i, (BT * (1 - b) + i) % 2, False)
                    for i in range(BT):
                        wait_apart(pool, sm["rows_done"], BT * (m + 1) + i + 1, sm["passed_pool"])
                        pool.indirect_dma_start(io["out_rows"][:, :],
                                                bass.IndirectOffsetOnAxis(rows_out[:, i:i + 1], 0), ys[:, i, :], None,
                                                bounds_check=B * S - 1, oob_is_err=False).then_inc(rows_stored, 16)
                    wait_apart(pool, rows_stored, 16 * BT * (m + 1), sm["passed_pool"], start=0)
            for r in range(2):
                pool.wait_ge(gathered[r], 16 * ((ST + BT + 2 + 1 - r) // 2 - early_of_ring[r]))
        @block.scalar
        def _(act):
            def turn_hi(m, b, i):
                act.wait_ge(sm["x_turned"], ONE + BT * m + i + 1)
                act.activation(xT[b][0][:, :, i * P:(i + 1) * P],
                               turning_bank(m, i)[:].rearrange("p (k n) -> p k n", k=KD), ACT.Copy)\
                    .then_inc(sm["x_hi"], 1)

            def split_hi(e, f):
                act.wait_ge(raw_loaded[f % RW], ONE + (32 * ((NF * e + f - f % RW) // RW + 1) if isinstance(e, int) else
                            e * (32 * NF // RW) + 32 * (f // RW + 1)))
                wait(act, sm["used"], 2 * NF * e - NF + f + 1 if not isinstance(e, int) or e else 0)
                act.activation(w1[0][:, f, :, :].rearrange("p k n -> p (k n)"), raw[:, f % RW, 0, :], ACT.Copy)\
                    .then_inc(sm["w_hi"], 1)
                act.activation(w2[0][:, f, :], raw[:, f % RW, 1, :], ACT.Copy).then_inc(sm["w_hi"], 1)

            def expert(e):
                for b in range(2):
                    m = 2 * e + b
                    for f in range(NF):
                        act.wait_ge(sm["hidden"], ONE + NF * m + f + 1)
                        act.activation(h[f % 2][0][:], hid[:, :, 0:HB], ACT.Relu).then_inc(sm["h_hi"], 1)
                        if f in TURN:
                            turn_hi(m + 1, 1 - b, TURN[f])
                        if refilled(e, b, f):
                            split_hi(*refilled(e, b, f))

            for f in range(NF):
                split_hi(0, f)
            for i in range(BT):
                turn_hi(0, 0, i)
            experts(act, expert)

        @block.vector
        def _(dve):
            def turn_lo(m, b, i):
                dve.wait_ge(sm["x_hi"], ONE + BT * m + i + 1)
                dve.tensor_tensor(xT[b][1][:, :, i * P:(i + 1) * P],
                                  turning_bank(m, i)[:].rearrange("p (k n) -> p k n", k=KD),
                                  f32(xT[b][0][:, :, i * P:(i + 1) * P]), ALU.subtract).then_inc(sm["x_lo"], 1)

            def split_lo(e, f):
                dve.wait_ge(sm["w_hi"], ONE + 2 * (NF * e + f + 1))
                dve.tensor_tensor(w1[1][:, f, :, :].rearrange("p k n -> p (k n)"), raw[:, f % RW, 0, :],
                                  f32(w1[0][:, f, :, :]).rearrange("p k n -> p (k n)"), ALU.subtract)\
                    .then_inc(sm["w_lo"], 1)
                dve.tensor_tensor(w2[1][:, f, :], raw[:, f % RW, 1, :], f32(w2[0][:, f, :]), ALU.subtract)\
                    .then_inc(sm["w_lo"], 1)

            def add_rows(m):
                wait_apart(dve, rows_loaded, 16 * BT * (m + 1), sm["passed_dve"], start=0)
                wait_apart(dve, sm["used"], NF * (m + 1), sm["passed_dve"])
                for i in range(BT):
                    dve.scalar_tensor_tensor(ys[:, i, :], acc[i][:], slot_gate[:, bass.ds(BT * m + i, 1)], ys[:, i, :],
                                             ALU.mult, ALU.add).then_inc(sm["rows_done"], 1)

            def expert(e):
                for b in range(2):
                    m = 2 * e + b
                    for f in range(NF):
                        dve.wait_ge(sm["h_hi"], ONE + NF * m + f + 1)
                        dve.scalar_tensor_tensor(h[f % 2][1][:], hid[:, :, 0:HB], 0.0, f32(h[f % 2][0][:]),
                                                 ALU.max, ALU.subtract).then_inc(sm["h_lo"], 1)
                        if f == 0 and not (isinstance(m, int) and m == 0):
                            add_rows(m - 1)
                        if f in TURN:
                            turn_lo(m + 1, 1 - b, TURN[f])
                        if refilled(e, b, f):
                            split_lo(*refilled(e, b, f))

            for f in range(NF):
                split_lo(0, f)
            dve.memset(slot_gather[:], 0).then_inc(sm["padded"], 1)
            dve.wait_ge(sm["table_loaded"], ONE + 16)
            pairs = tab.rearrange("a (b o) -> a b o", o=2)
            dve.tensor_copy(tabf[:, 0, :], pairs[:, :, 0]).then_inc(sm["table_f"], 1)
            dve.tensor_copy(tabf[:, 1, :], pairs[:, :, 1].bitcast(F32)).then_inc(sm["table_f"], 1)
            dve.wait_ge(sm["table_T"], ONE + 1)
            dve.tensor_scalar(filled[:], xb[:, 0:ST], float(B * S), None, ALU.is_lt).then_inc(sm["filled"], 1)
            dve.tensor_copy(slot_scatter[:], xb[:, 0:ST])
            dve.tensor_copy(slot_gate[:], xb[:, ST:2 * ST]).then_inc(sm["rows_done"], BT)
            dve.wait_ge(sm["padded"], ONE + 1)
            dve.wait_ge(sm["filled"], ONE + 1)
            dve.tensor_tensor(slot_gather[:, 0:ST], xb[:, 0:ST], filled[:], ALU.mult).then_inc(sm["slots_ready"], 1)
            dve.wait_ge(sm["slots_ready"], ONE + 1)
            for i in range(BT):
                turn_lo(0, 0, i)
            experts(dve, expert)
            add_rows(2 * E - 1)

        @block.tensor
        def _(pe):
            def turn(m, i, parity, first):
                n = BT * m + i
                r = (parity * BT + i) % 2
                source = xg[r]
                if isinstance(n, int) and 2 <= n < BT:
                    source = ys[:, n, :]
                    pe.wait_ge(early[n - 2], 16)
                elif isinstance(n, int):
                    pe.wait_ge(gathered[r], 16 * (n // 2 + 1 - (early_of_ring[r] if n >= BT else 0)))
                else:
                    pe.wait_ge(gathered[r], first * (16 * BT) + 16 * ((parity * BT + i) // 2 + 1 - early_of_ring[r]))
                bank = turning_bank(m, i)
                if bank is xb:
                    wait(pe, sm["x_lo"], n)
                for k in range(KD):
                    q = pe.transpose(bank[:, k * P:(k + 1) * P], source[:, k * P:(k + 1) * P], t["ident"][:])
                q.then_inc(sm["x_turned"], 1)

            pe.wait_ge(sm["table_f"], ONE + 2)
            for o in range(2):
                q = pe.transpose(xb[:, o * ST:(o + 1) * ST], tabf[:, o, :], t["ident"][0:ST, 0:ST])
            q.then_inc(sm["table_T"], 1)
            pe.wait_ge(sm["slots_ready"], ONE + 1)
            for i in range(BT):
                turn(0, i, 0, 0)
            def outputs(m, f):
                pe.wait_ge(sm["h_lo"], ONE + NF * m + f + 1)
                for i in range(BT):
                    if f == 0:
                        pe.wait_ge(sm["rows_done"], ONE + BT * m + i + 1)
                    hh, hl = (x[:].rearrange("p a n -> p (a n)")[:, i * P:(i + 1) * P] for x in h[f % 2])
                    q = split_passes(pe, acc[i][:], (hh, hl), [w[:, f, :] for w in w2], f == 0, f == NF - 1)
                q.then_inc(sm["used"], 1)

            def expert(e):
                for b in range(2):
                    m = 2 * e + b
                    pe.wait_ge(sm["x_lo"], ONE + BT * (m + 1))
                    for f in range(NF):
                        pe.wait_ge(sm["w_lo"], ONE + 2 * (NF * e + f + 1))
                        pe.wait_ge(sm["h_lo"], ONE + NF * m + f)
                        for k in range(KD):
                            for a, q in ((0, 0), (0, 1), (1, 0)):
                                for z in range(2):
                                    i = pe.matmul(hid[:, z, 0:HB], w1[a][:, f, k, :],
                                                  xT[b][q][:, k, z * HB:(z + 1) * HB], start=k == 0 and a + q == 0,
                                                  stop=k == KD - 1 and a == 1)
                        i.then_inc(sm["hidden"], 1)
                        if f in TURN:
                            turn(m + 1, TURN[f], 1 - b, e + b)
                        if f:
                            outputs(m, f - 1)
                        elif not (isinstance(m, int) and m == 0):
                            outputs(m - 1, NF - 1)

            experts(pe, expert)
            outputs(2 * E - 1, NF - 1)


def decoder_layer(nc, io):
    with Scope(nc) as s:
        t = {}
        t["ident"] = s.sb("ident", [P, P])
        t["identb"] = s.sb("identb", [P, P], BF16)
        t["mask"] = s.sb("mask", [P, P], BF16)
        t["ones"] = s.sb("ones", [P, P])
        t["upper"] = s.sb("upper", [P, P])
        t["avg"] = s.sb("avg", [P, P])
        t["half"] = s.sb("half", [P, 1])
        t["eps"] = s.sb("eps", [P, 1])
        t["choice"] = s.sb("choice", [P, TOPK, NT, 2], I32)
        t["choice_slot"] = s.sb("choice_slot", [P, TOPK, NT], I32)
        with Scope(nc) as a:
            t["logits"] = a.sb("logits", [P, NT, E])
            t["act"] = a.sb("act", [P, NT, D])
            t["mean1"] = a.sb("mean1", [P, NT, 1])
            t["rstd1"] = a.sb("rstd1", [P, NT, 1])
            for n in ("theta_b", "phi_b", "g_b"):
                t[n] = a.sb(n + "_col", [P, 1])
            t["out_b"] = a.sb("out_b_col", [P, TPB])
            t["gamma"] = a.sb("gamma", [P, D])
            t["beta"] = a.sb("beta", [P, D])
            shapes = {"theta_w": [P, TPB, LAT], "phi_w": [P, TPB, LAT], "g_w": [P, TPB, LAT],
                      "out_w": [P, S], "router_w": [P, KD, E]}
            for n, shape in shapes.items():
                t[n] = [a.sb(f"{n}_{p}", shape, F32R) for p in ("hi", "lo")]
            with Scope(nc) as o:
                t["wo"] = [o.sb(f"wo_{p}", [P, KD, D], F32R) for p in ("hi", "lo")]
                with Scope(nc) as q:
                    t["k"] = q.sb("k", [P, NT, KVW])
                    t["v"] = q.sb("v", [P, NT, G, VW])
                    t["cos"] = q.sb("cos", [P, TPB, HD])
                    t["sin"] = q.sb("sin", [P, TPB, HD])
                    with Scope(nc) as w:
                        t["wqkv"] = [w.sb(f"wqkv_{p}", [P, KD, QKV], F32R) for p in ("hi", "lo")]
                        t["x"] = w.sb("x_in", [P, CH, D])
                        t["split"] = ["wqkv", "wo", *shapes]
                        stage_constants(nc, io, t)
                        stage_qkv(nc, io, t)
                    stage_attention(nc, t)
                stage_out_proj(nc, io, t)
            stage_cross(nc, io, t)
            stage_route(nc, io, t)
        stage_experts(nc, io, t)


def build(nc, arrays, out):
    io = {}
    for name, (shape, dt) in arrays.items():
        io[name] = nc.dram_tensor(f"in_{name}_dram", shape, dt, kind="ExternalInput").ap()
    xn3 = nc.dram_tensor("xn3_dram", [B * S, D], F32, kind="Internal").ap()
    io["table"] = nc.dram_tensor("slot_table_dram", [SLOTS + TOPK * B * S, 2], I32, kind="Internal").ap()
    io["xn3"] = xn3
    io["x_tiles"] = io["x"].rearrange("b (u p) d -> (b u) p d", p=P)
    io["ctx_tiles"] = io["ctx"].rearrange("b (u p) d -> b p u d", p=P)
    io["x2_tiles"] = out.rearrange("b (u p) d -> b p u d", p=P)
    io["xn3_tiles"] = xn3.rearrange("(b u p) d -> b p u d", u=TPB, p=P)
    io["out_rows"] = out.rearrange("b s d -> (b s) d")
    decoder_layer(nc, io)


def kernel(x, ctx_2048, L0_attn_wq, L0_attn_wk, L0_attn_wv, L0_attn_wo, L0_xattn_theta_w, L0_xattn_theta_b,
           L0_xattn_phi_w, L0_xattn_phi_b, L0_xattn_g_w, L0_xattn_g_b, L0_xattn_ln_gamma, L0_xattn_ln_beta,
           L0_xattn_out_w, L0_xattn_out_b, L0_ffn_Wg, L0_ffn_w1, L0_ffn_w2):
    import numpy as np
    import concourse.bacc as bacc
    from concourse.bass_utils import run_bass_kernel_spmd

    order = np.concatenate([np.arange(0, HD, 2), np.arange(1, HD, 2)])

    def halves(w):
        w = np.asarray(w)
        return w.reshape(D, -1, HD)[:, :, order].reshape(D, -1)

    def contraction_tiles(w):
        w = np.asarray(w)
        return np.ascontiguousarray(w.reshape(-1, P, w.shape[1]).transpose(1, 0, 2))

    inv_freq = (1.0 / 10000.0 ** (np.arange(0, HD, 2, dtype=np.float32) / HD)).astype(np.float32)
    angle = np.arange(S, dtype=np.float32)[:, None] * inv_freq[None, :]
    cos, sin = np.cos(angle).astype(np.float32), np.sin(angle).astype(np.float32)

    def position_tiles(a):
        return np.ascontiguousarray(a.reshape(TPB, P, HD).transpose(1, 0, 2))

    arrays = {
        "x": np.ascontiguousarray(x),
        "ctx": np.ascontiguousarray(ctx_2048),
        "wqkv": contraction_tiles(np.concatenate([halves(L0_attn_wq), halves(L0_attn_wk), np.asarray(L0_attn_wv)], 1)),
        "wo": contraction_tiles(L0_attn_wo),
        "theta_w": contraction_tiles(np.asarray(L0_xattn_theta_w).T),
        "phi_w": contraction_tiles(np.asarray(L0_xattn_phi_w).T),
        "g_w": contraction_tiles(np.asarray(L0_xattn_g_w).T),
        "out_w": np.ascontiguousarray(np.asarray(L0_xattn_out_w).T),
        "router_w": contraction_tiles(L0_ffn_Wg),
        "theta_b": np.ascontiguousarray(L0_xattn_theta_b),
        "phi_b": np.ascontiguousarray(L0_xattn_phi_b),
        "g_b": np.ascontiguousarray(L0_xattn_g_b),
        "out_b": np.ascontiguousarray(np.asarray(L0_xattn_out_b).reshape(TPB, P).T),
        "gamma": np.ascontiguousarray(L0_xattn_ln_gamma),
        "beta": np.ascontiguousarray(L0_xattn_ln_beta),
        "cos": position_tiles(np.concatenate([cos, cos], 1)),
        "sin": position_tiles(np.concatenate([-sin, sin], 1)),
        "w1_tiles": np.ascontiguousarray(np.asarray(L0_ffn_w1).reshape(E, KD, P, NF, P).transpose(0, 3, 2, 1, 4)
                                         .reshape(E * NF, P, D)),
        "w2_tiles": np.ascontiguousarray(np.asarray(L0_ffn_w2).reshape(E * NF, P, D)),
    }
    nc = bacc.Bacc("TRN2", target_bir_lowering=False, num_devices=1)
    out = nc.dram_tensor("out_dram", [B, S, D], F32, kind="ExternalOutput").ap()
    build(nc, {n: (a.shape, mybir.dt.from_np(a.dtype)) for n, a in arrays.items()}, out)
    r = run_bass_kernel_spmd(nc, [{f"in_{n}_dram": a for n, a in arrays.items()}], core_ids=[0])
    return r.results[0]["out_dram"]
```
